# Optimizing a Trainium2 kernel written in Bass

```python
import numpy as np
import jax
import jax.numpy as jnp

def _softmax(x, axis=-1):
    return jax.nn.softmax(x, axis=axis)

def _gelu(x):
    return jax.nn.gelu(x, approximate=True)

def _silu(x):
    return jax.nn.silu(x)

def _sigmoid(x):
    return jax.nn.sigmoid(x)

def _layernorm(x, axis=-1, eps=1e-05):
    m = jnp.mean(x, axis=axis, keepdims=True)
    v = jnp.var(x, axis=axis, keepdims=True)
    return (x - m) / jnp.sqrt(v + eps)

def _scatter_add(tgt, idx, src, axis=0):
    return tgt.at[idx].add(src)

def _segment_sum(src, seg, n):
    return jax.ops.segment_sum(src, seg, n)
kernel_name = 'mk_decoder_postln_d2_seqx_r4_e75783'

def setup_inputs(seed: int=0):
    np.random.seed(seed)
    _w = jnp.asarray

    def _rec_inputs():
        import jax
        import jax.numpy as jnp
        _rk = jax.random.key(seed)
        x = -0.0002928 + 1 * jax.random.normal(jax.random.fold_in(_rk, 1), (1, 2048, 256), jnp.float32)
        _lenS = 2048 - jax.random.randint(jax.random.fold_in(_rk, 7), (1,), 0, max(1, 2048 // 4) + 1, jnp.int32)
        _lenS2 = 1601 - jax.random.randint(jax.random.fold_in(_rk, 8), (1,), 0, max(1, 1601 // 4) + 1, jnp.int32)
        _ctx_1024P = jax.random.normal(jax.random.fold_in(_rk, 11), (1, 16, 256), jnp.float32)
        _ctx_1024c = jax.random.dirichlet(jax.random.fold_in(_rk, 511), 0.3 * jnp.ones((16,), jnp.float32), (1, 1601))
        _ctx_1024t = jnp.einsum('bsk,bkd->bsd', _ctx_1024c, _ctx_1024P)
        _ctx_1024t = _ctx_1024t * jax.lax.rsqrt(jnp.mean(jnp.square(_ctx_1024t)) + 1e-12) * 0.953939
        ctx_1024 = -1.39393e-06 + 0.999914 * (_ctx_1024t + 0.3 * jax.random.normal(jax.random.fold_in(_rk, 611), (1, 1601, 256), jnp.float32))
        _validS = jnp.arange(2048)[None, :] < _lenS[:, None]
        _validS2 = jnp.arange(1601)[None, :] < _lenS2[:, None]
        _causal = jnp.tril(jnp.ones((2048, 2048), dtype=bool))
        mask_Bx1xS2_bf1 = jnp.ones((1, 1, 1601), dtype=bool)
        return (x, ctx_1024, mask_Bx1xS2_bf1)
    x, ctx_1024, mask_Bx1xS2_bf1 = _rec_inputs()

    def _L0_attn_setup():
        import jax, jax.numpy as jnp
        import numpy as np
        H_HEADS = 8
        WIN = 64

        def _layernorm(x, gamma, beta, eps=1e-05):
            mu = jnp.mean(x, axis=-1, keepdims=True)
            var = jnp.var(x, axis=-1, keepdims=True)
            return (x - mu) * jax.lax.rsqrt(var + eps) * gamma + beta
        key = jax.random.key(seed)
        ks = jax.random.split(key, 8)
        B, S, D = (4, 1024, 256)
        F = 4 * D
        s = 0.02
        return {'x': jax.random.normal(ks[0], (B, S, D), dtype=jnp.float32), 'Wq': jax.random.normal(ks[1], (D, D), dtype=jnp.float32) * s, 'bq': jnp.zeros((D,), jnp.float32), 'Wk': jax.random.normal(ks[2], (D, D), dtype=jnp.float32) * s, 'bk': jnp.zeros((D,), jnp.float32), 'Wv': jax.random.normal(ks[3], (D, D), dtype=jnp.float32) * s, 'bv': jnp.zeros((D,), jnp.float32), 'Wo': jax.random.normal(ks[4], (D, D), dtype=jnp.float32) * s, 'bo': jnp.zeros((D,), jnp.float32), 'gamma': jnp.ones((D,), jnp.float32), 'beta': jnp.zeros((D,), jnp.float32), 'W1': jax.random.normal(ks[5], (D, F), dtype=jnp.float32) * s, 'b1': jnp.zeros((F,), jnp.float32), 'W2': jax.random.normal(ks[6], (F, D), dtype=jnp.float32) * s, 'b2': jnp.zeros((D,), jnp.float32)}
    _L0_attn_all = _L0_attn_setup()
    _L0_attn_in = {k: v for k, v in _L0_attn_all.items() if k in ('Wq', 'bq', 'Wk', 'bk', 'Wv', 'bv', 'Wo', 'bo', 'gamma', 'beta', 'W1', 'b1', 'W2', 'b2')}
    del _L0_attn_all

    def _L0_xattn_setup():
        import jax, jax.numpy as jnp
        import numpy as np
        D_MODEL = 256
        NUM_HEADS = 16
        HEAD_DIM = D_MODEL // NUM_HEADS
        key = jax.random.key(seed)
        ks = jax.random.split(key, 10)
        B, SQ, SKV = (2, 512, 512)
        s = 1.0 / np.sqrt(D_MODEL)
        inp = {'query': jax.random.normal(ks[0], (B, SQ, D_MODEL), jnp.float32), 'key_value': jax.random.normal(ks[1], (B, SKV, D_MODEL), jnp.float32), 'Wq': jax.random.normal(ks[2], (D_MODEL, D_MODEL), jnp.float32) * s, 'bq': jnp.zeros((D_MODEL,), jnp.float32), 'Wk': jax.random.normal(ks[3], (D_MODEL, D_MODEL), jnp.float32) * s, 'bk': jnp.zeros((D_MODEL,), jnp.float32), 'Wv': jax.random.normal(ks[4], (D_MODEL, D_MODEL), jnp.float32) * s, 'bv': jnp.zeros((D_MODEL,), jnp.float32), 'Wo': jax.random.normal(ks[5], (D_MODEL, D_MODEL), jnp.float32) * s, 'bo': jnp.zeros((D_MODEL,), jnp.float32)}
        return inp
    _L0_xattn_all = _L0_xattn_setup()
    _L0_xattn_in = {k: v for k, v in _L0_xattn_all.items() if k in ('Wq', 'bq', 'Wk', 'bk', 'Wv', 'bv', 'Wo', 'bo')}
    del _L0_xattn_all

    def _L0_ffn_setup():
        import jax, jax.numpy as jnp
        import numpy as np
        B, S, D_MODEL, D_FF, E, R, TOP_K = (4, 512, 256, 1024, 8, 16, 2)
        key = jax.random.key(seed)
        ks = jax.random.split(key, 9)
        sd = 1.0 / np.sqrt(D_MODEL)
        return {'hidden_states': jax.random.normal(ks[0], (B, S, D_MODEL), jnp.float32), 'wi': jax.random.normal(ks[1], (D_FF, D_MODEL), jnp.float32) * sd, 'bi': jax.random.normal(ks[2], (D_FF,), jnp.float32) * 0.01, 'wo': jax.random.normal(ks[3], (D_MODEL, D_FF), jnp.float32) * (1.0 / np.sqrt(D_FF)), 'bo': jax.random.normal(ks[4], (D_MODEL,), jnp.float32) * 0.01, 'lora_A': jax.random.normal(ks[5], (E, R, D_MODEL), jnp.float32) * sd, 'lora_B': jax.random.normal(ks[6], (E, D_FF, R), jnp.float32) * 0.02, 'gate_w': jax.random.normal(ks[7], (E, D_MODEL), jnp.float32) * sd, 'gate_b': jax.random.normal(ks[8], (E,), jnp.float32) * 0.01}
    _L0_ffn_all = _L0_ffn_setup()
    _L0_ffn_in = {k: v for k, v in _L0_ffn_all.items() if k in ('wi', 'bi', 'wo', 'bo', 'lora_A', 'lora_B', 'gate_w', 'gate_b')}
    del _L0_ffn_all

    def _L1_attn_setup():
        import jax, jax.numpy as jnp
        import numpy as np
        B, N, D, H = (8, 256, 256, 16)
        HD = D // H
        SCALE = HD ** (-0.5)
        key = jax.random.key(seed)
        k1, k2, k3, k4, k5 = jax.random.split(key, 5)
        return {'x': jax.random.normal(k1, (B, N, D), dtype=jnp.float32), 'qkv_w': jax.random.normal(k2, (3 * D, D), dtype=jnp.float32) * 0.02, 'qkv_b': jax.random.normal(k3, (3 * D,), dtype=jnp.float32) * 0.02, 'fc_w': jax.random.normal(k4, (D, D), dtype=jnp.float32) * 0.02, 'fc_b': jax.random.normal(k5, (D,), dtype=jnp.float32) * 0.02}
    _L1_attn_all = _L1_attn_setup()
    _L1_attn_in = {k: v for k, v in _L1_attn_all.items() if k in ('qkv_w', 'qkv_b', 'fc_w', 'fc_b')}
    del _L1_attn_all

    def _L1_xattn_setup():
        import jax, jax.numpy as jnp
        import numpy as np
        B, S, D, H = (4, 512, 256, 16)
        HD = D // H
        key = jax.random.key(seed)
        ks = jax.random.split(key, 12)
        inp = {'k': jax.random.normal(ks[0], (B, S, D), jnp.float32), 'v': jax.random.normal(ks[1], (B, S, D), jnp.float32), 'q': jax.random.normal(ks[2], (B, S, D), jnp.float32), 'mask': jnp.ones((B, 1, S), dtype=bool), 'Wq': jax.random.normal(ks[3], (D, D), jnp.float32) / np.sqrt(D), 'bq': jax.random.normal(ks[4], (D,), jnp.float32) * 0.01, 'Wk': jax.random.normal(ks[5], (D, D), jnp.float32) / np.sqrt(D), 'bk': jax.random.normal(ks[6], (D,), jnp.float32) * 0.01, 'Wv': jax.random.normal(ks[7], (D, D), jnp.float32) / np.sqrt(D), 'bv': jax.random.normal(ks[8], (D,), jnp.float32) * 0.01, 'Wo': jax.random.normal(ks[9], (D, D), jnp.float32) / np.sqrt(D), 'bo': jax.random.normal(ks[10], (D,), jnp.float32) * 0.01}
        return inp
    _L1_xattn_all = _L1_xattn_setup()
    _L1_xattn_in = {k: v for k, v in _L1_xattn_all.items() if k in ('Wq', 'bq', 'Wk', 'bk', 'Wv', 'bv', 'Wo', 'bo')}
    del _L1_xattn_all

    def _L1_ffn_setup():
        import jax, jax.numpy as jnp
        import numpy as np
        D_MODEL = 256
        D_FF = 1024
        N_EXPERTS = 8
        TOP_K = 2
        S, B = (512, 4)
        key = jax.random.key(seed)
        ks = jax.random.split(key, 7)
        sc_in = 1.0 / np.sqrt(D_MODEL)
        sc_ff = 1.0 / np.sqrt(D_FF)
        return {'x': jax.random.normal(ks[0], (S, B, D_MODEL), dtype=jnp.float32), 'gate_w': jax.random.uniform(ks[1], (D_MODEL, N_EXPERTS), jnp.float32, -sc_in, sc_in), 'gate_b': jnp.zeros((N_EXPERTS,), jnp.float32), 'w1': jax.random.uniform(ks[2], (N_EXPERTS, D_MODEL, D_FF), jnp.float32, -sc_in, sc_in), 'b1': jax.random.uniform(ks[3], (N_EXPERTS, D_FF), jnp.float32, -sc_in, sc_in), 'w2': jax.random.uniform(ks[4], (N_EXPERTS, D_FF, D_MODEL), jnp.float32, -sc_ff, sc_ff), 'b2': jax.random.uniform(ks[5], (N_EXPERTS, D_MODEL), jnp.float32, -sc_ff, sc_ff)}
    _L1_ffn_all = _L1_ffn_setup()
    _L1_ffn_in = {k: v for k, v in _L1_ffn_all.items() if k in ('gate_w', 'gate_b', 'w1', 'b1', 'w2', 'b2')}
    del _L1_ffn_all
    return {'x': x, 'ctx_1024': ctx_1024, 'mask_Bx1xS2_bf1': mask_Bx1xS2_bf1, 'L0_attn_Wq': _L0_attn_in['Wq'], 'L0_attn_bq': _L0_attn_in['bq'], 'L0_attn_Wk': _L0_attn_in['Wk'], 'L0_attn_bk': _L0_attn_in['bk'], 'L0_attn_Wv': _L0_attn_in['Wv'], 'L0_attn_bv': _L0_attn_in['bv'], 'L0_attn_Wo': _L0_attn_in['Wo'], 'L0_attn_bo': _L0_attn_in['bo'], 'L0_attn_gamma': _L0_attn_in['gamma'], 'L0_attn_beta': _L0_attn_in['beta'], 'L0_attn_W1': _L0_attn_in['W1'], 'L0_attn_b1': _L0_attn_in['b1'], 'L0_attn_W2': _L0_attn_in['W2'], 'L0_attn_b2': _L0_attn_in['b2'], 'L0_xattn_Wq': _L0_xattn_in['Wq'], 'L0_xattn_bq': _L0_xattn_in['bq'], 'L0_xattn_Wk': _L0_xattn_in['Wk'], 'L0_xattn_bk': _L0_xattn_in['bk'], 'L0_xattn_Wv': _L0_xattn_in['Wv'], 'L0_xattn_bv': _L0_xattn_in['bv'], 'L0_xattn_Wo': _L0_xattn_in['Wo'], 'L0_xattn_bo': _L0_xattn_in['bo'], 'L0_ffn_wi': _L0_ffn_in['wi'], 'L0_ffn_bi': _L0_ffn_in['bi'], 'L0_ffn_wo': _L0_ffn_in['wo'], 'L0_ffn_bo': _L0_ffn_in['bo'], 'L0_ffn_lora_A': _L0_ffn_in['lora_A'], 'L0_ffn_lora_B': _L0_ffn_in['lora_B'], 'L0_ffn_gate_w': _L0_ffn_in['gate_w'], 'L0_ffn_gate_b': _L0_ffn_in['gate_b'], 'L1_attn_qkv_w': _L1_attn_in['qkv_w'], 'L1_attn_qkv_b': _L1_attn_in['qkv_b'], 'L1_attn_fc_w': _L1_attn_in['fc_w'], 'L1_attn_fc_b': _L1_attn_in['fc_b'], 'L1_xattn_Wq': _L1_xattn_in['Wq'], 'L1_xattn_bq': _L1_xattn_in['bq'], 'L1_xattn_Wk': _L1_xattn_in['Wk'], 'L1_xattn_bk': _L1_xattn_in['bk'], 'L1_xattn_Wv': _L1_xattn_in['Wv'], 'L1_xattn_bv': _L1_xattn_in['bv'], 'L1_xattn_Wo': _L1_xattn_in['Wo'], 'L1_xattn_bo': _L1_xattn_in['bo'], 'L1_ffn_gate_w': _L1_ffn_in['gate_w'], 'L1_ffn_gate_b': _L1_ffn_in['gate_b'], 'L1_ffn_w1': _L1_ffn_in['w1'], 'L1_ffn_b1': _L1_ffn_in['b1'], 'L1_ffn_w2': _L1_ffn_in['w2'], 'L1_ffn_b2': _L1_ffn_in['b2']}

def reference(x, ctx_1024, mask_Bx1xS2_bf1, L0_attn_Wq, L0_attn_bq, L0_attn_Wk, L0_attn_bk, L0_attn_Wv, L0_attn_bv, L0_attn_Wo, L0_attn_bo, L0_attn_gamma, L0_attn_beta, L0_attn_W1, L0_attn_b1, L0_attn_W2, L0_attn_b2, L0_xattn_Wq, L0_xattn_bq, L0_xattn_Wk, L0_xattn_bk, L0_xattn_Wv, L0_xattn_bv, L0_xattn_Wo, L0_xattn_bo, L0_ffn_wi, L0_ffn_bi, L0_ffn_wo, L0_ffn_bo, L0_ffn_lora_A, L0_ffn_lora_B, L0_ffn_gate_w, L0_ffn_gate_b, L1_attn_qkv_w, L1_attn_qkv_b, L1_attn_fc_w, L1_attn_fc_b, L1_xattn_Wq, L1_xattn_bq, L1_xattn_Wk, L1_xattn_bk, L1_xattn_Wv, L1_xattn_bv, L1_xattn_Wo, L1_xattn_bo, L1_ffn_gate_w, L1_ffn_gate_b, L1_ffn_w1, L1_ffn_b1, L1_ffn_w2, L1_ffn_b2):
    import jax
    import jax.numpy as jnp

    def _L0_attn_ref(x, Wq, bq, Wk, bk, Wv, bv, Wo, bo, gamma, beta, W1, b1, W2, b2):
        import jax, jax.numpy as jnp
        import numpy as np
        H_HEADS = 8
        WIN = 64

        def _layernorm(x, gamma, beta, eps=1e-05):
            mu = jnp.mean(x, axis=-1, keepdims=True)
            var = jnp.var(x, axis=-1, keepdims=True)
            return (x - mu) * jax.lax.rsqrt(var + eps) * gamma + beta
        B, S, D = x.shape
        w, H = (WIN, H_HEADS)
        dh = D // H
        pad = -S % w
        if pad:
            x = jnp.pad(x, ((0, 0), (0, pad), (0, 0)))
        mask = jnp.concatenate([jnp.ones((B, S), jnp.float32), jnp.zeros((B, pad), jnp.float32)], axis=1)
        Sp = S + pad
        nc = Sp // w

        def proj(W, b):
            return (x @ W + b).reshape(B, Sp, H, dh).transpose(0, 2, 1, 3).reshape(B, H, nc, w, dh)
        q = proj(Wq, bq)
        k = proj(Wk, bk)
        v = proj(Wv, bv)

        def ext3(t):
            tp = jnp.pad(t, ((0, 0), (0, 0), (1, 1), (0, 0), (0, 0)))
            return jnp.concatenate([tp[:, :, :-2], tp[:, :, 1:-1], tp[:, :, 2:]], axis=3)
        k3 = ext3(k)
        v3 = ext3(v)
        mc = mask.reshape(B, nc, w)
        mp = jnp.pad(mc, ((0, 0), (1, 1), (0, 0)))
        m3 = jnp.concatenate([mp[:, :-2], mp[:, 1:-1], mp[:, 2:]], axis=2)
        qi = jnp.arange(w)
        kj = jnp.arange(3 * w)
        band = jnp.abs(qi[:, None] - (kj[None, :] - w)) <= w
        allow = band[None, None, None, :, :] & (m3[:, None, :, None, :] > 0)
        scale = float(dh) ** (-0.5)
        scores = jnp.einsum('bhcqd,bhckd->bhcqk', q, k3) * scale
        scores = jnp.where(allow, scores, jnp.float32(-1e+30))
        p = jax.nn.softmax(scores, axis=-1)
        o = jnp.einsum('bhcqk,bhckd->bhcqd', p, v3)
        o = o.reshape(B, H, Sp, dh).transpose(0, 2, 1, 3).reshape(B, Sp, D)
        attn = o @ Wo + bo
        x = x + attn
        x = _layernorm(x, gamma, beta)
        h = jax.nn.gelu(x @ W1 + b1, approximate=False)
        x = x + (h @ W2 + b2)
        return x

    def _L0_xattn_ref(query, key_value, Wq, bq, Wk, bk, Wv, bv, Wo, bo):
        import jax, jax.numpy as jnp
        import numpy as np
        D_MODEL = 256
        NUM_HEADS = 16
        HEAD_DIM = D_MODEL // NUM_HEADS
        B, SQ, _ = query.shape
        SKV = key_value.shape[1]
        Q = query @ Wq.T + bq
        K = key_value @ Wk.T + bk
        V = key_value @ Wv.T + bv
        Q = Q.reshape(B, SQ, NUM_HEADS, HEAD_DIM).transpose(0, 2, 1, 3)
        K = K.reshape(B, SKV, NUM_HEADS, HEAD_DIM).transpose(0, 2, 1, 3)
        V = V.reshape(B, SKV, NUM_HEADS, HEAD_DIM).transpose(0, 2, 1, 3)
        scores = jnp.einsum('bhqd,bhkd->bhqk', Q, K) / np.sqrt(HEAD_DIM)
        causal = jnp.tril(jnp.ones((SQ, SKV), bool))
        scores = jnp.where(causal[None, None], scores, -jnp.inf)
        attn = jax.nn.softmax(scores, axis=-1)
        out = jnp.einsum('bhqk,bhkd->bhqd', attn, V)
        out = out.transpose(0, 2, 1, 3).reshape(B, SQ, D_MODEL)
        return out @ Wo.T + bo

    def _L0_ffn_ref(hidden_states, wi, bi, wo, bo, lora_A, lora_B, gate_w, gate_b):
        import jax, jax.numpy as jnp
        import numpy as np
        B, S, D_MODEL, D_FF, E, R, TOP_K = (4, 512, 256, 1024, 8, 16, 2)
        logits = jnp.einsum('bsd,ed->bse', hidden_states, gate_w) + gate_b
        scores = jax.nn.softmax(logits, axis=-1)
        top_v, top_i = jax.lax.top_k(scores, TOP_K)
        val_sum = top_v.sum(axis=-1)
        out = jnp.zeros_like(hidden_states)
        for e in range(E):
            count = (top_i == e).sum(axis=-1).astype(hidden_states.dtype)
            gate = count * val_sum
            inter = jnp.einsum('bsd,fd->bsf', hidden_states, wi) + bi + jnp.einsum('bsr,fr->bsf', jnp.einsum('bsd,rd->bsr', hidden_states, lora_A[e]), lora_B[e])
            h = jax.nn.relu(inter)
            expert_out = jnp.einsum('bsf,df->bsd', h, wo) + bo
            out = out + gate[..., None] * expert_out
        return out

    def _L1_attn_ref(x, qkv_w, qkv_b, fc_w, fc_b):
        import jax, jax.numpy as jnp
        import numpy as np
        B, N, D, H = (8, 256, 256, 16)
        HD = D // H
        SCALE = HD ** (-0.5)
        b, n, d = x.shape
        qkv = (jnp.einsum('bnd,ed->bne', x, qkv_w) + qkv_b).reshape(b, n, H, 3 * HD)
        q, k, v = jnp.split(qkv, 3, axis=-1)
        q = q.transpose(0, 2, 1, 3)
        k = k.transpose(0, 2, 1, 3)
        v = v.transpose(0, 2, 1, 3)
        attn = jax.nn.softmax(jnp.einsum('bhqd,bhkd->bhqk', q, k) * SCALE, axis=-1)
        out = jnp.einsum('bhqk,bhkd->bhqd', attn, v)
        out = out.transpose(0, 2, 1, 3).reshape(b, n, d)
        return jnp.einsum('bnd,ed->bne', out, fc_w) + fc_b + x

    def _L1_xattn_ref(k, v, q, mask, Wq, bq, Wk, bk, Wv, bv, Wo, bo):
        import jax, jax.numpy as jnp
        import numpy as np
        B, S, D, H = (4, 512, 256, 16)
        HD = D // H
        b = q.shape[0]

        def split_heads(x):
            return x.reshape(b, -1, H, HD).transpose(0, 2, 1, 3)
        qh = split_heads(q @ Wq + bq) / jnp.sqrt(jnp.asarray(HD, q.dtype))
        kh = split_heads(k @ Wk + bk)
        vh = split_heads(v @ Wv + bv)
        scores = jnp.einsum('bhqd,bhkd->bhqk', qh, kh)
        if mask is not None:
            scores = jnp.where(mask[:, None, :, :], scores, jnp.asarray(-jnp.inf, scores.dtype))
        attn = jax.nn.softmax(scores, axis=-1)
        ctx = jnp.einsum('bhqk,bhkd->bhqd', attn, vh)
        ctx = ctx.transpose(0, 2, 1, 3).reshape(b, -1, H * HD)
        out = ctx @ Wo + bo
        return out

    def _L1_ffn_ref(x, gate_w, gate_b, w1, b1, w2, b2):
        import jax, jax.numpy as jnp
        import numpy as np
        D_MODEL = 256
        D_FF = 1024
        N_EXPERTS = 8
        TOP_K = 2
        S, B = (512, 4)
        s, b, d = x.shape
        T = s * b
        x_flat = x.reshape(T, d)
        scores = x_flat @ gate_w + gate_b
        topk_vals, topk_idx = jax.lax.top_k(scores, TOP_K)
        topk_probs = jax.nn.softmax(topk_vals, axis=-1)
        tok = jnp.arange(T)[:, None]
        combine_w = jnp.zeros((T, N_EXPERTS), x.dtype).at[tok, topk_idx].add(topk_probs)
        h = jax.nn.relu(jnp.einsum('td,edf->etf', x_flat, w1) + b1[:, None, :])
        y = jnp.einsum('etf,efd->etd', h, w2) + b2[:, None, :]
        out = jnp.einsum('te,etd->td', combine_w, y)
        return out.reshape(s, b, d)
    x = _layernorm(x + _L0_attn_ref(x, L0_attn_Wq, L0_attn_bq, L0_attn_Wk, L0_attn_bk, L0_attn_Wv, L0_attn_bv, L0_attn_Wo, L0_attn_bo, L0_attn_gamma, L0_attn_beta, L0_attn_W1, L0_attn_b1, L0_attn_W2, L0_attn_b2), axis=-1)
    x = _layernorm(x + _L0_xattn_ref(x, ctx_1024, L0_xattn_Wq, L0_xattn_bq, L0_xattn_Wk, L0_xattn_bk, L0_xattn_Wv, L0_xattn_bv, L0_xattn_Wo, L0_xattn_bo), axis=-1)
    x = _layernorm(x + _L0_ffn_ref(x, L0_ffn_wi, L0_ffn_bi, L0_ffn_wo, L0_ffn_bo, L0_ffn_lora_A, L0_ffn_lora_B, L0_ffn_gate_w, L0_ffn_gate_b), axis=-1)
    x = _layernorm(x + _L1_attn_ref(x, L1_attn_qkv_w, L1_attn_qkv_b, L1_attn_fc_w, L1_attn_fc_b), axis=-1)
    x = _layernorm(x + _L1_xattn_ref(ctx_1024, ctx_1024, x, mask_Bx1xS2_bf1, L1_xattn_Wq, L1_xattn_bq, L1_xattn_Wk, L1_xattn_bk, L1_xattn_Wv, L1_xattn_bv, L1_xattn_Wo, L1_xattn_bo), axis=-1)
    x = _layernorm(x + _L1_ffn_ref(x, L1_ffn_gate_w, L1_ffn_gate_b, L1_ffn_w1, L1_ffn_b1, L1_ffn_w2, L1_ffn_b2), axis=-1)
    return x

_drawn_inputs = setup_inputs


def setup_inputs(seed=0):
    import zlib

    import numpy as np

    out = dict(_drawn_inputs(seed))
    spreads = {'L0_attn_bq': (0.0, 0.8),
     'L0_attn_bk': (0.0, 0.8),
     'L0_attn_bv': (0.0, 0.364),
     'L0_attn_bo': (0.0, 0.1),
     'L0_attn_gamma': (1.0, 0.2),
     'L0_attn_beta': (0.0, 0.1),
     'L0_attn_b1': (0.0, 0.341),
     'L0_attn_b2': (0.0, 0.1),
     'L0_xattn_bq': (0.0, 0.28),
     'L0_xattn_bk': (0.0, 0.8),
     'L0_xattn_bv': (0.0, 0.1),
     'L0_xattn_bo': (0.0, 0.1),
     'L1_ffn_gate_b': (0.0, 0.1)}
    factors = {'L0_attn_Wq': 8.0,
     'L0_attn_Wk': 8.0,
     'L0_attn_Wv': 6.021,
     'L0_attn_Wo': 2.735,
     'L0_ffn_bi': 5.111,
     'L0_ffn_bo': 4.341,
     'L0_ffn_gate_b': 6.601,
     'L1_attn_qkv_b': 6.443,
     'L1_attn_fc_b': 3.83,
     'L1_xattn_bq': 8.0,
     'L1_xattn_bk': 8.0,
     'L1_xattn_bv': 3.605,
     'L1_xattn_bo': 3.737,
     'L1_ffn_b1': 5.31,
     'L1_ffn_b2': 4.383}
    for name, (base, spread) in spreads.items():
        noise = np.random.default_rng([zlib.crc32(name.encode()), seed]).standard_normal(out[name].shape)
        drawn = base * np.exp(spread * noise) if base else spread * noise
        out[name] = jnp.asarray(drawn.astype(out[name].dtype))
    for name, factor in factors.items():
        out[name] = (out[name] * factor).astype(out[name].dtype)
    return out
```

```python
import concourse.bass as bass
from concourse import mybir
from contextlib import ExitStack

F32 = mybir.dt.float32
BF16 = mybir.dt.bfloat16
U8 = mybir.dt.uint8
U32 = mybir.dt.uint32
ALU = mybir.AluOpType
ACT = mybir.ActivationFunctionType
AX = mybir.AxisListType

P = 128
S = 2048
D = 256
DT = D // P
NT = S // P
CTX = 1601
CT = -(-CTX // P)
CTXP = CT * P
SH = 16
NSH = D // SH
GH = 4
NG = NSH // GH
QC = 512
NQ = S // QC
QT = QC // P
DFF = 1024
FT = DFF // P
E = 8
R = 16
NEG = -1.0e30
EPS = 1e-5
Q_PARTS = (0, 0, 1, 0, 2, 1)
K_PARTS = (0, 1, 0, 2, 0, 1)
ROWS_SPLIT = SH * len(Q_PARTS)
ROW_MASK, ROW_MAX = ROWS_SPLIT, ROWS_SPLIT + 1
BAND = 64


class Attention:

    def __init__(self, kind, keys, head_dim):
        self.kind, self.keys, self.head_dim = kind, keys, head_dim
        self.tiles = keys // P
        self.halves = head_dim // SH
        self.heads = GH // self.halves
        self.units = self.heads // 2
        self.pairs = [len(self.key_tiles(c)) for c in range(NQ)]
        self.pairs_group = sum(self.pairs)
        self.jobs = [self.heads * QT * len(self.max_chunks(QT * c)) for c in range(NQ)]
        self.jobs_group = sum(self.jobs)

    def key_tiles(self, c):
        if self.kind == "band":
            return [-1, 0, 1]
        if self.kind == "causal":
            return list(range(min(self.tiles, QT * (c + 1))))
        return list(range(self.tiles))

    def max_chunks(self, t):
        if self.kind == "band":
            lo, hi = max(t - 1, 0), min(t + 2, NT)
            return [(lo * P, (hi - lo) * P)]
        end = min(self.keys, (t + 1) * P) if self.kind == "causal" else self.keys
        return [(k, min(QC, end - k)) for k in range(0, end, QC)]


def clear_semaphores(nc, held):
    nc.clear_and_free_semaphores(held)
    held.clear()
    nc.all_engine_barrier()


def make_constants(nc, sb, sem):
    c = {"semaphores": []}
    c["ident"] = sb("ident", [P, P], F32)
    c["ident_bf"] = sb("ident_bf", [P, P], BF16)
    c["eps"] = sb("eps", [P, 1], F32)
    c["causal_k"] = sb("causal_k", [P, 2 * QC], BF16)
    c["causal_q"] = sb("causal_q", [P, QC], BF16)
    c["band_k"] = sb("band_k", [P, 5, P], BF16)
    c["band_q"] = sb("band_q", [P, 3 * P], BF16)
    with ExitStack() as ctx:
        done = ctx.enter_context(nc.semaphore("const_done"))
        block = ctx.enter_context(nc.Block())

        @block.gpsimd
        def _(pool):
            n = 0

            def fill(t, value):
                nonlocal n
                pool.memset(t, value).then_inc(done, 1)
                n += 1
                pool.wait_ge(done, n)

            def select(t, op, fill_value, base, pattern, mult):
                nonlocal n
                pool.affine_select(out=t, in_=t, compare_op=op, fill=fill_value, base=base, pattern=pattern,
                                   channel_multiplier=mult).then_inc(done, 1)
                n += 1
                pool.wait_ge(done, n)

            for t in (c["ident"], c["ident_bf"]):
                fill(t[:, :], 0.0)
                select(t[:, :], ALU.not_equal, 1.0, 0, [[-1, P]], 1)
            fill(c["eps"][:, :], EPS)
            off = QC - P
            fill(c["causal_k"][:, :], 0.0)
            select(c["causal_k"][:, :], ALU.is_ge, NEG, -off, [[1, 2 * QC]], -1)
            fill(c["causal_q"][:, :], 0.0)
            select(c["causal_q"][:, :], ALU.is_ge, NEG, off, [[-1, QC]], 1)
            fill(c["band_k"][:, :, :], 0.0)
            fill(c["band_k"][:, 3, :], NEG)
            for i, r in enumerate((-1, 0, 1)):
                select(c["band_k"][:, i, :], ALU.is_ge, NEG, BAND - P * r, [[1, P]], -1)
                select(c["band_k"][:, i, :], ALU.is_ge, NEG, BAND + P * r, [[-1, P]], 1)
            fill(c["band_q"][:, :], 0.0)
            select(c["band_q"][:, :], ALU.is_ge, NEG, BAND - P, [[1, 3 * P]], -1)
            select(c["band_q"][:, :], ALU.is_ge, NEG, BAND + P, [[-1, 3 * P]], 1)
    return c


class RowNorm:

    def __init__(self, nc, name, sb, pb, sem, x_tok, x_fm, cst, gain=None):
        self.x_tok, self.x_fm, self.cst, self.gain = x_tok, x_fm, cst, gain
        self.stat = sb("rn_stat", [P, NT, 6], F32)
        self.mean_var = sb("rn_mean_var", [P, NT, 2], F32)
        self.std = sb("rn_std", [P, NT], F32)
        self.inv = sb("rn_inv", [P, NT], F32)
        self.ps = [pb(f"rn_ps{i}", [P, QC], F32) for i in range(2)] if x_fm is not None else None
        self.s_stat, self.s_mv, self.s_std, self.s_inv, self.s_x, self.s_turn, self.s_fm = map(
            sem, ("rn_stat", "rn_mv", "rn_std", "rn_inv", "rn_x", "rn_turn", "rn_fm"))
        self.per_tile = 3 if gain is not None else 1

    def statistics(self, dve, t):
        dve.bn_stats(self.stat[:, t, :], self.x_tok[:, t, :]).then_inc(self.s_stat, 1)
        dve.wait_ge(self.s_stat, t + 1)
        dve.bn_aggr(self.mean_var[:, t, :], self.stat[:, t, :]).then_inc(self.s_mv, 1)

    def root(self, act, quad):
        q = slice(quad * 4, quad * 4 + 4)
        act.wait_ge(self.s_mv, 4 * (quad + 1))
        act.activation(self.std[:, q], self.mean_var[:, q, 1], ACT.Sqrt,
                       bias=self.cst["eps"][:, 0:1]).then_inc(self.s_std, 1)

    def scale(self, dve, quad):
        q = slice(quad * 4, quad * 4 + 4)
        dve.wait_ge(self.s_std, quad + 1)
        dve.reciprocal(self.inv[:, q], self.std[:, q]).then_inc(self.s_inv, 1)
        dve.wait_ge(self.s_inv, quad + 1)
        for t in range(quad * 4, quad * 4 + 4):
            x = self.x_tok[:, t, :]
            dve.tensor_scalar(x, x, self.mean_var[:, t, 0:1], self.inv[:, t:t + 1], ALU.subtract,
                              ALU.mult).then_inc(self.s_x, 1)
            if self.gain is not None:
                dve.wait_ge(self.s_x, 3 * t + 1)
                dve.tensor_tensor(x, x, self.gain[:, 0, :], ALU.mult).then_inc(self.s_x, 1)
                dve.wait_ge(self.s_x, 3 * t + 2)
                dve.tensor_tensor(x, x, self.gain[:, 1, :], ALU.add).then_inc(self.s_x, 1)

    def turn(self, pe, t):
        pe.wait_ge(self.s_x, self.per_tile * (t + 1))
        if t >= 2:
            pe.wait_ge(self.s_fm, t - 1)
        for m in range(DT):
            mm = pe.transpose(self.ps[t % 2][:, m * P:(m + 1) * P], self.x_tok[:, t, m * P:(m + 1) * P],
                              self.cst["ident"][:, :])
        mm.then_inc(self.s_turn, 1)

    def copy_out(self, act, t):
        act.wait_ge(self.s_turn, t + 1)
        act.activation(self.x_fm[:, :, t * P:(t + 1) * P],
                       self.ps[t % 2][:, 0:DT * P].rearrange("p (a b) -> p a b", a=DT),
                       ACT.Copy).then_inc(self.s_fm, 1)


def load_stacks(sp, at, g, slot, q_st, k_st, parts_q, parts_k, s_load):
    for n, (qp, kp) in enumerate(zip(Q_PARTS, K_PARTS)):
        rows = slice(n * SH, (n + 1) * SH)
        for st, parts, part, length in ((q_st, parts_q, qp, S), (k_st, parts_k, kp, at.keys)):
            src = parts[part, bass.ds(g * GH * SH, GH * SH), 0:length]
            sp.dma_start(st[rows, bass.ds(slot, 1), :, 0:length],
                         src.rearrange("(o j d) n -> d o j n", d=SH, o=1)).then_inc(s_load, 16)


LOADS = 2 * len(Q_PARTS)


def project(nc, at, name, x_fm, kv_fm, w, bias, v_bias, v_tok, parts_q, parts_k, stacks, s_load, mask, cst):
    q_st, k_st = stacks
    units = [(side, m, k, min(QC, n - k)) for m in range(DT) for side, n in ((0, S), (1, at.keys))
             for k in range(0, n, QC)]
    first = len(units) // DT
    NB, NS = 4, 6
    with ExitStack() as ctx:
        def sb(n, shape, dt):
            return ctx.enter_context(nc.sbuf_tensor(f"{name}_{n}", shape, dt))

        def sem(n):
            cst["semaphores"].append(nc.alloc_semaphore(f"{name}_{n}"))
            return cst["semaphores"][-1]

        w_sb = sb("w", [P, 3, DT, D], F32)
        bias_sb = sb("bias", [P, 2, DT], F32)
        vb_sb = sb("vb", [P, D], F32)
        exact = sb("exact", [P, 2, QC], F32)
        rest = sb("rest", [P, 2, QC], F32)
        parts = sb("parts", [P, NS, 3, QC], BF16)
        ps = [ctx.enter_context(nc.psum_tensor(f"{name}_ps{i}", [P, QC], F32)) for i in range(NB)]
        ps_v = [ctx.enter_context(nc.psum_tensor(f"{name}_psv{i}", [P, QC], F32)) for i in range(2)]
        s_w, s_mm, s_exact, s_high, s_rest, s_mid, s_low = map(
            sem, ("w", "mm", "exact", "high", "rest", "mid", "low"))
        s_vmm, s_vout, s_mask = sem("vmm"), sem("vout"), sem("mask")
        s_store = [sem(f"store{i}") for i in range(NS)]
        block = ctx.enter_context(nc.Block())

        @block.sync
        def _(sp):
            sp.dma_start(w_sb[:, 0, :, :], w[0].rearrange("(t p) n -> p t n", p=P)).then_inc(s_w, 16)
            sp.dma_start(bias_sb[:, :, :], bias.rearrange("s p t -> p s t")).then_inc(s_w, 16)
            for side in (1, 2):
                sp.dma_start(w_sb[:, side, :, :], w[side].rearrange("(t p) n -> p t n", p=P)).then_inc(s_w, 16)
            sp.dma_start(vb_sb[:, :], v_bias.to_broadcast((P, D))).then_inc(s_w, 16)
            for slot in range(2):
                for j in range(GH):
                    sp.dma_start(k_st[ROW_MASK:ROW_MASK + 1, slot, j, 0:at.keys],
                                 mask[:, 0:at.keys]).then_inc(s_mask, 16)
            for u, (side, m, k, n) in enumerate(units):
                sp.wait_ge(s_low, u + 1)
                sp.wait_ge(s_mid, u + 1)
                sp.wait_ge(s_high, u + 1)
                dst = (parts_q, parts_k)[side]
                sp.dma_start(dst[:, m * P:(m + 1) * P, k:k + n].rearrange("s p n -> p s n"),
                             parts[:, u % NS, :, 0:n]).then_inc(s_store[u % NS], 16)
                if u == first - 1:
                    for i in range(NS):
                        sp.wait_ge(s_store[i], 16 * len(range(i, u + 1, NS)))
                    load_stacks(sp, at, 0, 0, q_st, k_st, parts_q, parts_k, s_load)
            for i in range(NS):
                sp.wait_ge(s_store[i], 16 * len(range(i, len(units), NS)))
            sp.wait_ge(s_mask, 16 * 2 * GH)

        @block.tensor
        def _(pe):
            def v_tiles():
                for i in range(at.tiles):
                    if i >= 2:
                        pe.wait_ge(s_vout, i - 1)
                    for t in range(DT):
                        mm = pe.matmul(ps_v[i % 2][:, 0:D], kv_fm[:, t, i * P:(i + 1) * P], w_sb[:, 2, t, :],
                                       start=(t == 0), stop=(t == DT - 1))
                    mm.then_inc(s_vmm, 1)

            pe.wait_ge(s_w, 80)
            for u, (side, m, k, n) in enumerate(units):
                if u == first:
                    v_tiles()
                src = (x_fm, kv_fm)[side]
                if u >= NB:
                    pe.wait_ge(s_high, u - NB + 1)
                for t in range(DT):
                    mm = pe.matmul(ps[u % NB][:, 0:n], w_sb[:, side, t, m * P:(m + 1) * P], src[:, t, k:k + n],
                                   start=(t == 0), stop=(t == DT - 1))
                mm.then_inc(s_mm, 1)

        @block.scalar
        def _(act):
            act.wait_ge(s_w, 80)
            for u, (side, m, k, n) in enumerate(units):
                act.wait_ge(s_mm, u + 1)
                if u >= 2:
                    act.wait_ge(s_rest, u - 1)
                act.activation(exact[:, u % 2, 0:n], ps[u % NB][:, 0:n], ACT.Identity,
                               bias=bias_sb[:, side, m:m + 1]).then_inc(s_exact, 1)
                if u >= NS:
                    act.wait_ge(s_store[u % NS], 16 * (u // NS))
                act.activation(parts[:, u % NS, 0, 0:n], ps[u % NB][:, 0:n], ACT.Identity,
                               bias=bias_sb[:, side, m:m + 1]).then_inc(s_high, 1)

        @block.gpsimd
        def _(pool):
            for u, (side, m, k, n) in enumerate(units):
                pool.wait_ge(s_rest, u + 1)
                if u >= NS:
                    pool.wait_ge(s_store[u % NS], 16 * (u // NS))
                pool.tensor_copy(parts[:, u % NS, 1, 0:n], rest[:, u % 2, 0:n]).then_inc(s_mid, 1)

        @block.vector
        def _(dve):
            def low(u):
                n = units[u][3]
                dve.wait_ge(s_mid, u + 1)
                if u >= NS:
                    dve.wait_ge(s_store[u % NS], 16 * (u // NS))
                dve.tensor_tensor(parts[:, u % NS, 2, 0:n], rest[:, u % 2, 0:n], parts[:, u % NS, 1, 0:n],
                                  ALU.subtract).then_inc(s_low, 1)

            def v_tiles():
                for i in range(at.tiles):
                    dve.wait_ge(s_vmm, i + 1)
                    dve.tensor_tensor(v_tok[:, i, :], ps_v[i % 2][:, 0:D], vb_sb[:, :],
                                      ALU.add).then_inc(s_vout, 1)

            dve.wait_ge(s_w, 80)
            for u, (side, m, k, n) in enumerate(units):
                if u == first:
                    low(u - 1)
                    v_tiles()
                dve.wait_ge(s_exact, u + 1)
                dve.wait_ge(s_high, u + 1)
                if u >= 2:
                    dve.wait_ge(s_low, u - 1)
                dve.tensor_tensor(rest[:, u % 2, 0:n], exact[:, u % 2, 0:n], parts[:, u % NS, 0, 0:n],
                                  ALU.subtract).then_inc(s_rest, 1)
                if u >= 1 and u != first:
                    low(u - 1)
            low(len(units) - 1)


class MaxStream:
    PLACES = 4

    @staticmethod
    def sequence(at, groups):
        out, waiting = [], []
        for dg in range(groups):
            for c in range(NQ):
                jobs = [(h, a, i, k, n) for h in range(at.heads) for a in range(QT)
                        for i, (k, n) in enumerate(at.max_chunks(QT * c + a))]
                for job in jobs:
                    out.append(("max", dg, c) + job + (job is jobs[-1],))
                    waiting = [(w, due - 1) for w, due in waiting]
                    if waiting and waiting[0][1] <= 0:
                        out.append(waiting.pop(0)[0])
                waiting.append((("turn", dg, c), 4))
        return out + [w for w, _ in waiting]

    @classmethod
    def windows(cls, at):
        one, two = cls.sequence(at, 1), cls.sequence(at, 2)
        ahead = cls.AHEAD[at.kind] // 2 * 2
        return cls(one[:ahead]), cls(two[ahead:ahead + len(one)]), cls(one[ahead:])

    AHEAD = {"full": 84, "causal": 44, "band": 16}

    def __init__(self, entries):
        self.entries = entries
        self.turn_at = {e[1:3]: x for x, e in enumerate(entries) if e[0] == "turn"}

    def spread(self, at):
        starts = {(0, c): sum(at.pairs[:c]) for c in range(NQ)}
        starts[(1, 0)] = at.pairs_group
        due = [(max(starts[step] - 2, 1), x + 1) for step, x in self.turn_at.items() if step in starts]
        due.append((at.pairs_group, len(self.entries)))
        knots = [(0, 0)]
        while knots[-1][0] < at.pairs_group:
            k0, n0 = knots[-1]
            left = [(k, n) for k, n in due if k > k0]
            knots.append(max(left, key=lambda d: ((d[1] - n0) / (d[0] - k0), d[0])))

        def issued(k):
            for (k0, n0), (k1, n1) in zip(knots, knots[1:]):
                if k <= k1:
                    return min(len(self.entries), round(n0 + (n1 - n0) * (k - k0) / (k1 - k0)))

        marks = (0.25, 0.5, 0.75, 1.0) if at.units == 2 else (0.5, 0.5, 1.0, 1.0)
        self.places, done = [], 0
        for k in range(at.pairs_group):
            row = []
            for m in marks:
                upto = max(done, issued(k + m))
                row.append(range(done, upto))
                done = upto
            self.places.append(row)


def attend(nc, at, name, v_tok, parts_q, parts_k, o_tok, stacks, s_load, cst):
    scale = float(at.head_dim) ** -0.5
    HEADS, UNITS, HALVES = at.heads, at.units, at.halves
    NEGC = HEADS * QT
    q_st, k_st, v_grp = stacks
    pro, body, end = MaxStream.windows(at)
    total = len(body.entries)
    body.spread(at)
    end.spread(at)
    with ExitStack() as ctx:
        def sb(n, shape, dt):
            return ctx.enter_context(nc.sbuf_tensor(f"{name}_{n}", shape, dt))

        def pb(n, shape, dt):
            return ctx.enter_context(nc.psum_tensor(f"{name}_{n}", shape, dt))

        def sem(n):
            cst["semaphores"].append(nc.alloc_semaphore(f"{name}_{n}"))
            return cst["semaphores"][-1]

        prob = sb("prob", [P, 2, HEADS, QC], F32)
        part_max = sb("part_max", [P, NEGC, 4], F32)
        neg_max = sb("neg_max", [P, NEGC], BF16)
        neg_row = sb("neg_row", [NEGC, P], BF16)
        o_raw = sb("o_raw", [P, QC], F32)
        inv_den = sb("inv_den", [P, QT, GH, 1], F32)
        ps_s = [pb(f"ps_s{i}", [P, 2, QC], F32) for i in range(2)]
        ps_m = [pb(f"ps_m{i}", [P, QC], F32) for i in range(2)]
        ps_o = pb("ps_o", [P, QC], F32)
        ps_x = pb("ps_x", [P, QC], F32)
        s_scores = sem("scores")
        s_prob = sem("prob")
        s_pv = sem("pv")
        s_vgrp = sem("vgrp")
        s_msc = sem("msc")
        s_mred = sem("mred")
        s_neg = sem("neg")
        s_negd = sem("negd")
        s_ocopy = sem("ocopy")
        s_turn = sem("turn")
        s_inv = sem("inv")
        s_norm = sem("norm")
        block = ctx.enter_context(nc.Block())

        def pairs_before(g, c):
            return g * at.pairs_group + sum(at.pairs[:c])

        def entries_before(g):
            return len(pro.entries) + g * total

        def slot(g):
            return g % 2

        @block.sync
        def _(sp):
            def store_max(g, c, n, entry):
                sp.wait_ge(s_mred, 2 + entry + 1)
                for h in range(HEADS):
                    sp.dma_start(q_st[ROW_MAX:ROW_MAX + 1, bass.ds(slot(g), 1), HALVES * h, c * QC:(c + 1) * QC],
                                 neg_row[h * QT:(h + 1) * QT, :]).then_inc(s_negd, 16)

            def group(g, stream, last):
                if not last:
                    sp.wait_ge(s_load, 16 * LOADS * (g + 1))
                    sp.wait_ge(s_pv, 2 + pairs_before(g, 0))
                    load_stacks(sp, at, g + 1, slot(g + 1), q_st, k_st, parts_q, parts_k, s_load)
                for (dg, c), x in stream.turn_at.items():
                    store_max(g + dg, c, (g + dg) * NQ + c, entries_before(g) + x)

            for (_, c), x in pro.turn_at.items():
                store_max(0, c, c, x)
            with sp.Fori(0, NG - 1) as g:
                group(g, body, False)
            group(NG - 1, end, True)

        @block.gpsimd
        def _(pool):
            pool.sem_inc(s_prob, 2)
            pool.sem_inc(s_pv, 2)
            pool.sem_inc(s_mred, 2)
            pool.sem_inc(s_ocopy, 1)
            pool.sem_inc(s_norm, 1)
            pool.sem_inc(s_turn, 1)

            def group(g):
                pool.wait_ge(s_pv, 2 + pairs_before(g, 0))
                pool.tensor_copy(v_grp[:, 0:at.tiles, :, 0:SH],
                                 v_tok[:, 0:at.tiles, bass.ds(g * GH * SH, GH * SH)]
                                 .rearrange("p t (j d) -> p t j d", d=SH)).then_inc(s_vgrp, 1)

            with pool.Fori(0, NG - 1) as g:
                group(g)
            group(NG - 1)

        @block.tensor
        def _(pe):
            def scores(g, c, k, kt, u, un):
                bank = ps_s[k % 2 if UNITS == 1 else u]
                pe.wait_ge(s_prob, un + 1)
                for hh in range(2):
                    h = 2 * u + hh
                    if at.kind == "band":
                        for a in range(QT):
                            t = QT * c + a
                            inside = 0 <= t + kt < NT
                            key = (t + kt if inside else t) * P
                            qs = slice(c * QC + a * P, c * QC + (a + 1) * P)
                            out = bank[:, hh, a * P:(a + 1) * P]
                            for half in range(HALVES):
                                rows = ROW_MAX + 1 if half == 0 else ROWS_SPLIT
                                j = HALVES * h + half
                                pe.matmul(out, k_st[0:rows, bass.ds(slot(g), 1), j, key:key + P],
                                          q_st[0:rows, bass.ds(slot(g), 1), j, qs],
                                          start=(half == 0), stop=False)
                            mm = pe.matmul(out, cst["ident_bf"][:, :],
                                           cst["band_k"][:, kt + 1 if inside else 3, :],
                                           start=False, stop=True)
                    else:
                        diag = at.kind == "causal" and kt >= QT * c
                        mm = pe.matmul(bank[:, hh, :],
                                       k_st[0:ROW_MAX + 1, bass.ds(slot(g), 1), h, kt * P:(kt + 1) * P],
                                       q_st[0:ROW_MAX + 1, bass.ds(slot(g), 1), h, c * QC:(c + 1) * QC],
                                       start=True, stop=not diag)
                        if diag:
                            off = QC - P - P * (kt - QT * c)
                            mm = pe.matmul(bank[:, hh, :], cst["ident_bf"][:, :],
                                           cst["causal_k"][:, off:off + QC], start=False, stop=True)
                mm.then_inc(s_scores, 1)

            def max_entry(g, stream, x, count):
                entry = stream.entries[x]
                pe.wait_ge(s_mred, count + x + 1)
                dg, c = entry[1:3]
                if entry[0] == "turn":
                    pe.wait_ge(s_neg, (g + dg) * NQ + c + 1)
                    pe.transpose(ps_m[x % 2][:, :].bitcast(BF16)[0:NEGC, 0:P], neg_max[:, :],
                                 cst["ident_bf"][:, :]).then_inc(s_msc, 1)
                    return
                h, a, i, k, w, last = entry[3:]
                t = QT * c + a
                out = ps_m[x % 2][:, 0:w]
                masked = at.kind == "band" or (at.kind == "causal" and k + w == (t + 1) * P)
                for half in range(HALVES):
                    rows = ROW_MASK + 1 if half == 0 else ROWS_SPLIT
                    j = HALVES * h + half
                    mm = pe.matmul(out, q_st[0:rows, bass.ds(slot(g + dg), 1), j, t * P:(t + 1) * P],
                                   k_st[0:rows, bass.ds(slot(g + dg), 1), j, k:k + w],
                                   start=(half == 0), stop=(half == HALVES - 1 and not masked))
                if masked:
                    if at.kind == "band":
                        m = cst["band_q"][:, k - (t - 1) * P:k - (t - 1) * P + w]
                    else:
                        m = cst["causal_q"][:, QC - w:QC]
                    mm = pe.matmul(out, cst["ident_bf"][:, :], m, start=False, stop=True)
                mm.then_inc(s_msc, 1)

            def times_v(g, c, i, k, kt, between=lambda: None):
                if i == 0:
                    pe.wait_ge(s_ocopy, g * NQ + c + 1)
                    if c == 0:
                        pe.wait_ge(s_vgrp, g + 1)
                pe.wait_ge(s_prob, 2 + UNITS * (pairs_before(g, 0) + k + 1))
                n = at.pairs[c]
                if at.kind == "band":
                    for a in range(QT):
                        t = QT * c + a
                        key = t + kt if 0 <= t + kt < NT else t
                        for j in range(GH):
                            mm = pe.matmul(ps_o[32 * j:32 * j + 32, a * P:(a + 1) * P], v_grp[:, key, j, :],
                                           prob[:, k % 2, j // HALVES, a * P:(a + 1) * P],
                                           start=(i == 0 and a == 0), stop=(i == n - 1),
                                           skip_group_check=True)
                else:
                    for j in range(GH):
                        mm = pe.matmul(ps_o[32 * j:32 * j + 32, :], v_grp[:, kt, j, :],
                                       prob[:, k % 2, j, :], start=(i == 0), stop=(i == n - 1))
                        if j == 1:
                            between()
                mm.then_inc(s_pv, 1)

            def turn_out(n):
                pe.wait_ge(s_ocopy, n + 2)
                pe.wait_ge(s_norm, n + 1)
                for a in range(QT):
                    mm = pe.transpose(ps_x[:, a * P:(a + 1) * P], o_raw[:, a * P:(a + 1) * P],
                                      cst["ident"][:, :])
                mm.then_inc(s_turn, 1)

            def group(g, stream):
                before = None
                k = 0
                for c in range(NQ):
                    n = g * NQ + c
                    pe.wait_ge(s_negd, 16 * HEADS * (n + 1))
                    for i, kt in enumerate(at.key_tiles(c)):
                        places = stream.places[k]
                        for u in range(UNITS):
                            scores(g, c, k, kt, u, UNITS * (pairs_before(g, 0) + k) + u)
                            for x in places[u]:
                                stream_entry(g, stream, x)
                        def entries(x):
                            for e in x:
                                stream_entry(g, stream, e)

                        if before is not None:
                            times_v(*before, between=(lambda: entries(places[2])) if UNITS == 2 else (lambda: None))
                        for x in ([] if UNITS == 2 and before is not None else list(places[2])) + list(places[3]):
                            stream_entry(g, stream, x)
                        if i == 2 and c > 0:
                            turn_out(n - 1)
                        before = (g, c, i, k, kt)
                        k += 1
                times_v(*before)
                turn_out(g * NQ + NQ - 1)

            def stream_entry(g, stream, x):
                ahead = [i for i, e in enumerate(stream.entries) if e[1] == 1]
                if ahead and x == ahead[0]:
                    pe.wait_ge(s_load, 16 * LOADS * (g + 2))
                max_entry(g, stream, x, entries_before(g))

            pe.wait_ge(s_load, 16 * LOADS)
            for x in range(len(pro.entries)):
                max_entry(0, pro, x, 0)
            for g in range(NG - 1):
                group(g, body)
            group(NG - 1, end)

        @block.scalar
        def _(act):
            def copy_o(g, c):
                n = g * NQ + c
                act.wait_ge(s_pv, 2 + pairs_before(g, c) + at.pairs[c])
                act.wait_ge(s_turn, n + 1)
                act.activation(o_raw[:, :], ps_o[:, :], ACT.Copy).then_inc(s_ocopy, 1)

            def group(g):
                k = 0
                for c in range(NQ):
                    for i in range(at.pairs[c]):
                        pair = pairs_before(g, 0) + k
                        act.wait_ge(s_pv, pair + (2 if k == 0 and at.pairs_group % 2 else 1))
                        for u in range(UNITS):
                            un = UNITS * pair + u
                            act.wait_ge(s_scores, un + 1)
                            bank = ps_s[k % 2 if UNITS == 1 else u]
                            act.activation(prob[:, k % 2, 2 * u:2 * u + 2, :], bank[:, :, :], ACT.Exp,
                                           scale=scale).then_inc(s_prob, 1)
                        if i == 0 and c > 0:
                            copy_o(g, c - 1)
                        k += 1
                copy_o(g, NQ - 1)

            act.wait_ge(s_prob, 2)
            act.wait_ge(s_ocopy, 1)
            act.wait_ge(s_turn, 1)
            with act.Fori(0, NG - 1) as g:
                group(g)
            group(NG - 1)

        @block.vector
        def _(dve):
            def max_entry(g, stream, x, count):
                entry = stream.entries[x]
                dg, c = entry[1:3]
                n = (g + dg) * NQ + c
                dve.wait_ge(s_msc, count + x + 1)
                if entry[0] == "turn":
                    if not (type(n) is int and n == 0):
                        dve.wait_ge(s_negd, 16 * HEADS * n)
                    dve.tensor_copy(neg_row[:, :],
                                    ps_m[x % 2][:, :].bitcast(BF16)[0:NEGC, 0:P]).then_inc(s_mred, 1)
                    return
                h, a, i, k, w, last = entry[3:]
                dve.tensor_reduce(part_max[:, h * QT + a, i:i + 1], ps_m[x % 2][:, 0:w], AX.X,
                                  ALU.max).then_inc(s_mred, 1)
                if last:
                    dve.wait_ge(s_mred, 2 + count + x + 1)
                    dve.tensor_reduce(neg_max[:, :], part_max[:, :, 0:len(at.max_chunks(QT * c))], AX.X,
                                      ALU.max, negate=True).then_inc(s_neg, 1)
                    dve.wait_ge(s_neg, n + 1)

            def normalise(g, c):
                n = g * NQ + c
                heads = ps_x[:, :].rearrange("p (a j d) -> p a j d", a=QT, j=GH)
                dve.wait_ge(s_turn, n + 2)
                dve.reciprocal(inv_den[:, :, :, :], heads[:, :, :, SH:SH + 1]).then_inc(s_inv, 1)
                dve.wait_ge(s_inv, n + 1)
                dve.tensor_tensor(o_tok[:, c * QT:(c + 1) * QT, bass.ds(g * GH * SH, GH * SH)]
                                  .rearrange("p a (j d) -> p a j d", d=SH), heads[:, :, :, 0:SH],
                                  inv_den[:, :, :, :].to_broadcast((P, QT, GH, SH)), ALU.mult).then_inc(s_norm, 1)

            def group(g, stream):
                k = 0
                for c in range(NQ):
                    for i in range(at.pairs[c]):
                        for place in stream.places[k]:
                            for x in place:
                                max_entry(g, stream, x, entries_before(g))
                        if i == 2 and c > 0:
                            normalise(g, c - 1)
                        k += 1
                normalise(g, NQ - 1)

            dve.wait_ge(s_mred, 2)
            dve.wait_ge(s_norm, 1)
            for x in range(len(pro.entries)):
                max_entry(0, pro, x, 0)
            with dve.Fori(0, NG - 1) as g:
                group(g, body)
            group(NG - 1, end)


def close_attention(nc, name, x_tok, dst, x_fm, o_tok, wo, bo, keep, gamma, beta, cst):
    with ExitStack() as ctx:
        def sb(n, shape, dt):
            return ctx.enter_context(nc.sbuf_tensor(f"{name}_{n}", shape, dt))

        def pb(n, shape, dt):
            return ctx.enter_context(nc.psum_tensor(f"{name}_{n}", shape, dt))

        def sem(n):
            cst["semaphores"].append(nc.alloc_semaphore(f"{name}_{n}"))
            return cst["semaphores"][-1]

        wo_sb = sb("wo", [P, DT, D], F32)
        bo_sb = sb("bo", [P, D], F32)
        gain = sb("gain", [P, 2, D], F32) if gamma is not None else None
        o_fm = sb("o_fm", [P, 2, DT, P], F32)
        ps_o = [pb(f"pso{i}", [P, QC], F32) for i in range(2)]
        ps_y = [pb(f"psy{i}", [P, QC], F32) for i in range(2)]
        s_w, s_turn, s_fm, s_mm, s_base, s_y = map(sem, ("w", "turn", "fm", "mm", "base", "y"))
        norm = RowNorm(nc, name, sb, pb, sem, dst, x_fm, cst, gain)
        LAG = 7
        block = ctx.enter_context(nc.Block())
        loads = 16 * (2 + (2 if gamma is not None else 0))

        @block.sync
        def _(sp):
            sp.dma_start(wo_sb[:, :, :], wo.rearrange("(t p) n -> p t n", p=P)).then_inc(s_w, 16)
            sp.dma_start(bo_sb[:, :], bo.to_broadcast((P, D))).then_inc(s_w, 16)
            if gamma is not None:
                sp.dma_start(gain[:, 0, :], gamma.to_broadcast((P, D))).then_inc(s_w, 16)
                sp.dma_start(gain[:, 1, :], beta.to_broadcast((P, D))).then_inc(s_w, 16)

        @block.gpsimd
        def _(pool):
            pool.wait_ge(s_w, loads)
            for t in range(NT):
                src = x_tok
                if keep == 2:
                    pool.tensor_tensor(dst[:, t, :], x_tok[:, t, :], x_tok[:, t, :], ALU.add).then_inc(s_base, 1)
                    pool.wait_ge(s_base, 2 * t + 1)
                    src = dst
                pool.tensor_tensor(dst[:, t, :], src[:, t, :], bo_sb[:, :], ALU.add).then_inc(s_base, 1)

        @block.tensor
        def _(pe):
            def turn(t):
                if t >= 2:
                    pe.wait_ge(s_fm, t - 1)
                for m in range(DT):
                    mm = pe.transpose(ps_o[t % 2][:, m * P:(m + 1) * P], o_tok[:, t, m * P:(m + 1) * P],
                                      cst["ident"][:, :])
                mm.then_inc(s_turn, 1)

            def product(t):
                pe.wait_ge(s_fm, t + 1)
                if t >= 2:
                    pe.wait_ge(s_y, t - 1)
                for m in range(DT):
                    mm = pe.matmul(ps_y[t % 2][:, 0:D], o_fm[:, t % 2, m, :], wo_sb[:, m, :],
                                   start=(m == 0), stop=(m == DT - 1))
                mm.then_inc(s_mm, 1)

            pe.wait_ge(s_w, loads)
            turn(0)
            for t in range(NT):
                if t + 1 < NT:
                    turn(t + 1)
                product(t)
                if t >= LAG:
                    norm.turn(pe, t - LAG)
            for t in range(NT - LAG, NT):
                norm.turn(pe, t)

        @block.scalar
        def _(act):
            def copy(t):
                act.wait_ge(s_turn, t + 1)
                if t >= 2:
                    act.wait_ge(s_mm, t - 1)
                act.activation(o_fm[:, t % 2, :, :], ps_o[t % 2][:, 0:D].rearrange("p (a b) -> p a b", a=DT),
                               ACT.Copy).then_inc(s_fm, 1)

            copy(0)
            for t in range(NT):
                if t + 1 < NT:
                    copy(t + 1)
                if t % 4 == 1 and t > 4:
                    norm.root(act, t // 4 - 1)
                if t >= LAG:
                    norm.copy_out(act, t - LAG)
            norm.root(act, NT // 4 - 1)
            for t in range(NT - LAG, NT):
                norm.copy_out(act, t)

        @block.vector
        def _(dve):
            for t in range(NT):
                dve.wait_ge(s_mm, t + 1)
                dve.wait_ge(s_base, (t + 1) * (2 if keep == 2 else 1))
                dve.tensor_tensor(dst[:, t, :], dst[:, t, :], ps_y[t % 2][:, 0:D], ALU.add).then_inc(s_y, 1)
                dve.wait_ge(s_y, t + 1)
                norm.statistics(dve, t)
                if t % 4 == 1 and t > 4:
                    norm.scale(dve, t // 4 - 1)
            norm.scale(dve, NT // 4 - 1)


def gelu_ffn(nc, name, x_tok, z_tok, x_fm, w1, b1, w2, b2, cst):
    with ExitStack() as ctx:
        def sb(n, shape, dt):
            return ctx.enter_context(nc.sbuf_tensor(f"{name}_{n}", shape, dt))

        def pb(n, shape, dt):
            return ctx.enter_context(nc.psum_tensor(f"{name}_{n}", shape, dt))

        def sem(n):
            cst["semaphores"].append(nc.alloc_semaphore(f"{name}_{n}"))
            return cst["semaphores"][-1]

        w1_sb = sb("w1", [P, DT, DFF], F32)
        w2_sb = sb("w2", [P, FT, D], F32)
        b1_sb = sb("b1", [P, FT], F32)
        b2_sb = sb("b2", [P, D], F32)
        h_fm = sb("h", [P, 2, FT, QC], F32)
        ps_h = [pb(f"psh{i}", [P, QC], F32) for i in range(4)]
        ps_y = [pb(f"psy{i}", [P, QC], F32) for i in range(2)]
        s_w, s_w2, s_up, s_h, s_dn, s_y, s_base = map(sem, ("w", "w2", "up", "h", "dn", "y", "base"))
        norm = RowNorm(nc, name, sb, pb, sem, x_tok, x_fm, cst)
        block = ctx.enter_context(nc.Block())

        @block.sync
        def _(sp):
            sp.dma_start(w1_sb[:, :, :], w1.rearrange("(t p) n -> p t n", p=P)).then_inc(s_w, 16)
            sp.dma_start(b1_sb[:, :], b1).then_inc(s_w, 16)
            sp.dma_start(b2_sb[:, :], b2.to_broadcast((P, D))).then_inc(s_w, 16)
            sp.dma_start(w2_sb[:, :, :], w2.rearrange("(t p) n -> p t n", p=P)).then_inc(s_w2, 16)

        @block.gpsimd
        def _(pool):
            pool.wait_ge(s_w, 48)
            for n in range(NT):
                pool.tensor_tensor(x_tok[:, n, :], x_tok[:, n, :], z_tok[:, n, :], ALU.add).then_inc(s_base, 1)
                pool.wait_ge(s_base, 2 * n + 1)
                pool.tensor_tensor(x_tok[:, n, :], x_tok[:, n, :], b2_sb[:, :], ALU.add).then_inc(s_base, 1)

        @block.tensor
        def _(pe):
            def up(c):
                for f in range(FT):
                    u = c * FT + f
                    if u >= 4:
                        pe.wait_ge(s_h, u - 3)
                    for t in range(DT):
                        mm = pe.matmul(ps_h[u % 4][:, :], w1_sb[:, t, f * P:(f + 1) * P],
                                       x_fm[:, t, c * QC:(c + 1) * QC], start=(t == 0), stop=(t == DT - 1))
                    mm.then_inc(s_up, 1)

            def down(c):
                pe.wait_ge(s_h, (c + 1) * FT)
                for a in range(QT):
                    n = c * QT + a
                    if n >= 2:
                        pe.wait_ge(s_y, n - 1)
                    for f in range(FT):
                        mm = pe.matmul(ps_y[n % 2][:, 0:D], h_fm[:, c % 2, f, a * P:(a + 1) * P],
                                       w2_sb[:, f, :], start=(f == 0), stop=(f == FT - 1))
                    mm.then_inc(s_dn, 1)

            pe.wait_ge(s_w, 48)
            up(0)
            pe.wait_ge(s_w2, 16)
            for c in range(NQ):
                if c + 1 < NQ:
                    up(c + 1)
                if c >= 2:
                    for t in range((c - 2) * QT, (c - 1) * QT):
                        norm.turn(pe, t)
                down(c)
            for t in range((NQ - 2) * QT, NT):
                norm.turn(pe, t)

        @block.scalar
        def _(act):
            act.wait_ge(s_w, 48)
            for c in range(NQ):
                if c >= 2:
                    act.wait_ge(s_dn, (c - 1) * QT)
                for f in range(FT):
                    u = c * FT + f
                    act.wait_ge(s_up, u + 1)
                    act.activation(h_fm[:, c % 2, f, :], ps_h[u % 4][:, :], ACT.Gelu,
                                   bias=b1_sb[:, f:f + 1]).then_inc(s_h, 1)
                if c >= 2:
                    norm.root(act, c - 2)
            for c in range(NQ):
                if c >= NQ - 2:
                    norm.root(act, c)
                for t in range(c * QT, (c + 1) * QT):
                    norm.copy_out(act, t)

        @block.vector
        def _(dve):
            for n in range(NT):
                dve.wait_ge(s_base, 2 * n + 2)
                dve.wait_ge(s_dn, n + 1)
                dve.tensor_tensor(x_tok[:, n, :], x_tok[:, n, :], ps_y[n % 2][:, 0:D], ALU.add).then_inc(s_y, 1)
                dve.wait_ge(s_y, n + 1)
                norm.statistics(dve, n)
                if n % 4 == 3 and n > 4:
                    norm.scale(dve, n // 4 - 1)
            norm.scale(dve, NT // 4 - 1)


def layer_norm(nc, name, x_tok, gamma, beta, x_fm, cst):
    with ExitStack() as ctx:
        def sb(n, shape, dt):
            return ctx.enter_context(nc.sbuf_tensor(f"{name}_{n}", shape, dt))

        def sem(n):
            cst["semaphores"].append(nc.alloc_semaphore(f"{name}_{n}"))
            return cst["semaphores"][-1]


        rows = sb("rows", [P, 2, D], F32)
        stats = sb("stats", [P, NT, 6], F32)
        mv = sb("mv", [P, NT, 2], F32)
        eps = sb("eps", [P, 1], F32)
        std = sb("std", [P, NT], F32)
        inv = sb("inv", [P, NT], F32)
        ps_t = [ctx.enter_context(nc.psum_tensor(f"{name}_pst{i}", [P, QC], F32)) for i in range(2)]
        s_w, s_st, s_mv, s_eps, s_std, s_inv, s_x, s_g, s_t, s_c = map(
            sem, ("w", "st", "mv", "eps", "std", "inv", "x", "g", "t", "c"))
        block = ctx.enter_context(nc.Block())

        @block.sync
        def _(sp):
            if gamma is not None:
                sp.dma_start(rows[:, 0, :], gamma.to_broadcast((P, D))).then_inc(s_w, 16)
                sp.dma_start(rows[:, 1, :], beta.to_broadcast((P, D))).then_inc(s_w, 16)

        @block.vector
        def _(dve):
            dve.memset(eps[:, :], EPS).then_inc(s_eps, 1)
            for t in range(NT):
                dve.bn_stats(stats[:, t, :], x_tok[:, t, :]).then_inc(s_st, 1)
            for t in range(NT):
                dve.wait_ge(s_st, t + 1)
                dve.bn_aggr(mv[:, t, :], stats[:, t, :]).then_inc(s_mv, 1)
            dve.wait_ge(s_std, 1)
            dve.reciprocal(inv[:, :], std[:, :]).then_inc(s_inv, 1)
            dve.wait_ge(s_inv, 1)
            if gamma is not None:
                dve.wait_ge(s_w, 32)
            for t in range(NT):
                dve.tensor_scalar(x_tok[:, t, :], x_tok[:, t, :], mv[:, t, 0:1], inv[:, t:t + 1], ALU.subtract,
                                  ALU.mult).then_inc(s_x, 1)
                if gamma is not None:
                    dve.wait_ge(s_x, 3 * t + 1)
                    dve.tensor_tensor(x_tok[:, t, :], x_tok[:, t, :], rows[:, 0, :], ALU.mult).then_inc(s_x, 1)
                    dve.wait_ge(s_x, 3 * t + 2)
                    dve.tensor_tensor(x_tok[:, t, :], x_tok[:, t, :], rows[:, 1, :], ALU.add).then_inc(s_x, 1)

        per = 3 if gamma is not None else 1

        @block.scalar
        def _(act):
            act.wait_ge(s_eps, 1)
            act.wait_ge(s_mv, NT)
            act.activation(std[:, :], mv[:, :, 1], ACT.Sqrt, bias=eps[:, 0:1]).then_inc(s_std, 1)
            if x_fm is not None:
                for t in range(NT):
                    act.wait_ge(s_t, t + 1)
                    act.activation(x_fm[:, :, t * P:(t + 1) * P],
                                   ps_t[t % 2][:, 0:DT * P].rearrange("p (a b) -> p a b", a=DT),
                                   ACT.Copy).then_inc(s_c, 1)

        if x_fm is not None:
            @block.tensor
            def _(pe):
                for t in range(NT):
                    pe.wait_ge(s_x, per * (t + 1))
                    if t >= 2:
                        pe.wait_ge(s_c, t - 1)
                    for m in range(DT):
                        mm = pe.transpose(ps_t[t % 2][:, m * P:(m + 1) * P], x_tok[:, t, m * P:(m + 1) * P],
                                          cst["ident"][:, :])
                    mm.then_inc(s_t, 1)


def route(nc, name, x_fm, gate_w, gate_b, cols, gates, top, sums, spread, cst):
    lora = cols > E
    with ExitStack() as ctx:
        def sb(n, shape, dt):
            return ctx.enter_context(nc.sbuf_tensor(f"{name}_{n}", shape, dt))

        def sem(n):
            cst["semaphores"].append(nc.alloc_semaphore(f"{name}_{n}"))
            return cst["semaphores"][-1]


        w_sb = sb("w", [P, DT, cols], F32)
        b_sb = sb("b", [P, E], F32)
        logit = sb("logit", [P, NT, E], F32)
        best = sb("best", [P, NT, 8], F32)
        index = sb("index", [P, NT, 8], U32)
        index_f = sb("index_f", [P, NT, 2], F32)
        order = sb("order", [P, E], F32)
        delta = sb("delta", [P, NT, E + 1], F32)
        a_tok = sb("a", [P, NT, E * R], F32) if lora else None
        picked = sb("picked", [P, 2, NT, E * R], F32) if lora else None
        swap = sb("swap", [P, NT, E], F32)
        ps = [ctx.enter_context(nc.psum_tensor(f"{name}_ps{i}", [P, QC], F32)) for i in range(2)]
        ps_t = [ctx.enter_context(nc.psum_tensor(f"{name}_pst{i}", [P, QC], F32)) for i in range(2)]
        s_w, s_mm, s_logit, s_a, s_exp, s_turn, s_out = map(sem, ("w", "mm", "logit", "a", "exp", "turn", "out"))
        s_best, s_index, s_chain, s_delta, s_picked = map(sem, ("best", "index", "chain", "delta", "picked"))
        block = ctx.enter_context(nc.Block())

        @block.sync
        def _(sp):
            sp.dma_start(w_sb[:, :, :], gate_w.rearrange("(t p) n -> p t n", p=P)).then_inc(s_w, 16)
            sp.dma_start(b_sb[:, :], gate_b.to_broadcast((P, E))).then_inc(s_w, 16)

        @block.tensor
        def _(pe):
            pe.wait_ge(s_w, 32)
            for t in range(NT):
                if t >= 2:
                    pe.wait_ge(s_logit, t - 1)
                for k in range(DT):
                    mm = pe.matmul(ps[t % 2][:, 0:cols], x_fm[:, k, t * P:(t + 1) * P], w_sb[:, k, :],
                                   start=(k == 0), stop=(k == DT - 1))
                mm.then_inc(s_mm, 1)
            if lora:
                for n in range(2 * NQ):
                    which, c = divmod(n, NQ)
                    pe.wait_ge(s_picked, which + 1)
                    if n >= 2:
                        pe.wait_ge(s_out, n - 1)
                    for a in range(QT):
                        mm = pe.transpose(ps_t[n % 2][:, a * P:(a + 1) * P], picked[:, which, c * QT + a, :],
                                          cst["ident"][:, :])
                    mm.then_inc(s_turn, 1)

        @block.vector
        def _(dve):
            links = 0

            def link(instruction):
                nonlocal links
                instruction.then_inc(s_chain, 1)
                links += 1
                dve.wait_ge(s_chain, links)

            for e in range(E):
                link(dve.memset(order[:, e:e + 1], float(e)))
            dve.wait_ge(s_w, 32)
            for t in range(NT):
                dve.wait_ge(s_mm, t + 1)
                if lora:
                    link(dve.tensor_copy(a_tok[:, t, :], ps[t % 2][:, 0:E * R]))
                dve.tensor_tensor(logit[:, t, :], ps[t % 2][:, cols - E:cols], b_sb[:, :],
                                  ALU.add).then_inc(s_logit, 1)
                dve.wait_ge(s_logit, t + 1)
                dve.max(best[:, t, :], logit[:, t, :]).then_inc(s_best, 1)
                dve.wait_ge(s_best, t + 1)
                dve.max_index(index[:, t, :], best[:, t, :], logit[:, t, :]).then_inc(s_index, 1)
            dve.tensor_tensor(delta[:, :, 0:E], logit[:, :, :], best[:, :, 0:1].to_broadcast((P, NT, E)),
                              ALU.subtract).then_inc(s_delta, 1)
            dve.tensor_tensor(delta[:, :, E:E + 1], best[:, :, 1:2], best[:, :, 0:1],
                              ALU.subtract).then_inc(s_delta, 1)
            dve.wait_ge(s_index, NT)
            link(dve.tensor_copy(index_f[:, :, :], index[:, :, 0:2]))
            for s in range(2):
                for t in range(NT):
                    ins = dve.tensor_scalar(gates[:, t, s, :], order[:, :], index_f[:, t, s:s + 1], None,
                                            ALU.is_equal)
                    if t == NT - 1:
                        link(ins)
            dve.wait_ge(s_exp, 1)
            link(dve.tensor_reduce(sums[:, :], delta[:, :, 0:E], AX.X, ALU.add))
            link(dve.tensor_copy(top[:, :], delta[:, :, E]))
            if lora:
                def wide(g):
                    return g.rearrange("p t (e o) -> p t e o", o=1).to_broadcast((P, NT, E, R))

                a4 = a_tok[:, :, :].rearrange("p t (e r) -> p t e r", r=R)
                link(dve.tensor_tensor(swap[:, :, :], gates[:, :, 1, :], gates[:, :, 0, :], ALU.subtract))
                for s, g in ((0, gates[:, :, 0, :]), (1, swap[:, :, :])):
                    dve.tensor_tensor(picked[:, s, :, :].rearrange("p t (e r) -> p t e r", r=R), a4, wide(g),
                                      ALU.mult).then_inc(s_picked, 1)

        @block.scalar
        def _(act):
            act.wait_ge(s_delta, 2)
            act.activation(delta[:, :, :], delta[:, :, :], ACT.Exp).then_inc(s_exp, 1)
            if lora:
                for n in range(2 * NQ):
                    which, c = divmod(n, NQ)
                    act.wait_ge(s_turn, n + 1)
                    act.activation(spread[:, which, c * QC:(c + 1) * QC], ps_t[n % 2][:, :],
                                   ACT.Copy).then_inc(s_out, 1)


def lora_ffn(nc, name, x_tok, x_fm, gates, top, sums, spread, wi, bi, wo, bo, lora_b, cst):
    with ExitStack() as ctx:
        def sb(n, shape, dt):
            return ctx.enter_context(nc.sbuf_tensor(f"{name}_{n}", shape, dt))

        def sem(n):
            cst["semaphores"].append(nc.alloc_semaphore(f"{name}_{n}"))
            return cst["semaphores"][-1]


        w1_sb = sb("w1", [P, DT, DFF], F32)
        lb_sb = sb("lb", [P, DFF], F32)
        w2_sb = sb("w2", [P, FT, D], F32)
        b1_sb = sb("b1", [P, FT], F32)
        b2_sb = sb("b2", [P, 2, D], F32)
        val = sb("val", [P, 2, NT], F32)
        h_fm = sb("h", [P, 2, FT, QC], F32)
        h_two = sb("h_two", [P, 2, 2, QC], F32)
        y_sb = sb("y", [P, 2, D], F32)
        ps_h = [ctx.enter_context(nc.psum_tensor(f"{name}_psh{i}", [P, QC], F32)) for i in range(4)]
        ps_y = [ctx.enter_context(nc.psum_tensor(f"{name}_psy{i}", [P, QC], F32)) for i in range(2)]
        s_w, s_w2, s_one, s_two, s_h1, s_h2, s_h, s_dn, s_a, s_b, s_v = map(
            sem, ("w", "w2", "one", "two", "h1", "h2", "h", "dn", "a", "b", "v"))
        norm = RowNorm(nc, name, sb, lambda n, shape, dt: ctx.enter_context(nc.psum_tensor(f"{name}_{n}", shape, dt)),
                       sem, x_tok, x_fm, cst)
        block = ctx.enter_context(nc.Block())
        UNITS = NQ * FT

        @block.sync
        def _(sp):
            sp.dma_start(w1_sb[:, :, :], wi.rearrange("(t p) n -> p t n", p=P)).then_inc(s_w, 16)
            sp.dma_start(lb_sb[:, :], lora_b).then_inc(s_w, 16)
            sp.dma_start(b1_sb[:, :], bi).then_inc(s_w, 16)
            sp.dma_start(w2_sb[:, :, :], wo.rearrange("(t p) n -> p t n", p=P)).then_inc(s_w2, 16)
            sp.dma_start(b2_sb[:, 0, :], bo.to_broadcast((P, D))).then_inc(s_w2, 16)

        @block.tensor
        def _(pe):
            def first(u):
                c, f = divmod(u, FT)
                if u >= 4:
                    pe.wait_ge(s_h2, u - 3)
                for t in range(DT):
                    pe.matmul(ps_h[u % 4][:, :], w1_sb[:, t, f * P:(f + 1) * P], x_fm[:, t, c * QC:(c + 1) * QC],
                              start=(t == 0), stop=False)
                pe.matmul(ps_h[u % 4][:, :], lb_sb[:, f * P:(f + 1) * P], spread[:, 0, c * QC:(c + 1) * QC],
                          start=False, stop=True).then_inc(s_one, 1)

            def second(u):
                c, f = divmod(u, FT)
                pe.wait_ge(s_h1, u + 1)
                pe.matmul(ps_h[u % 4][:, :], lb_sb[:, f * P:(f + 1) * P], spread[:, 1, c * QC:(c + 1) * QC],
                          start=False, stop=True, skip_group_check=True).then_inc(s_two, 1)

            def down(n):
                c, a = divmod(n, QT)
                pe.wait_ge(s_h, (c + 1) * FT)
                if n >= 2:
                    pe.wait_ge(s_a, n - 1)
                for f in range(FT):
                    mm = pe.matmul(ps_y[n % 2][:, 0:D], h_fm[:, c % 2, f, a * P:(a + 1) * P],
                                   w2_sb[:, f, :], start=(f == 0), stop=(f == FT - 1))
                mm.then_inc(s_dn, 1)

            pe.wait_ge(s_w, 48)
            for u in range(UNITS):
                first(u)
                if u >= 1:
                    second(u - 1)
                if u == 4:
                    pe.wait_ge(s_w2, 32)
                c, f = divmod(u, FT)
                if c >= 1 and f >= FT - QT:
                    down((c - 1) * QT + f - (FT - QT))
                if c >= 2 and f >= FT - QT:
                    norm.turn(pe, (c - 2) * QT + f - (FT - QT))
            second(UNITS - 1)
            for a in range(QT):
                norm.turn(pe, (NQ - 2) * QT + a)
                down((NQ - 1) * QT + a)
            for a in range(QT):
                norm.turn(pe, (NQ - 1) * QT + a)

        @block.scalar
        def _(act):
            act.wait_ge(s_w, 48)
            for u in range(UNITS):
                c, f = divmod(u, FT)
                if u >= 2:
                    act.wait_ge(s_h, u - 1)
                act.wait_ge(s_one, u + 1)
                act.activation(h_two[:, u % 2, 0, :], ps_h[u % 4][:, :], ACT.Relu,
                               bias=b1_sb[:, f:f + 1]).then_inc(s_h1, 1)
                act.wait_ge(s_two, u + 1)
                act.activation(h_two[:, u % 2, 1, :], ps_h[u % 4][:, :], ACT.Relu,
                               bias=b1_sb[:, f:f + 1]).then_inc(s_h2, 1)
                if c >= 2 and f == 1:
                    norm.root(act, c - 2)
                if c >= 2 and f >= FT - QT:
                    norm.copy_out(act, (c - 2) * QT + f - (FT - QT))
            for c in (NQ - 2, NQ - 1):
                norm.root(act, c)
                for a in range(QT):
                    norm.copy_out(act, c * QT + a)

        @block.vector
        def _(dve):
            dve.reciprocal(val[:, 0, :], sums[:, :]).then_inc(s_v, 1)
            dve.wait_ge(s_v, 1)
            dve.scalar_tensor_tensor(out=val[:, 1, :], in0=top[:, :], scalar=1.0, in1=val[:, 0, :], op0=ALU.add,
                                     op1=ALU.mult).then_inc(s_v, 1)
            dve.wait_ge(s_w2, 32)
            dve.tensor_scalar(b2_sb[:, 1, :], b2_sb[:, 0, :], 2.0, None, ALU.mult).then_inc(s_v, 1)
            dve.wait_ge(s_v, 3)

            def out(n):
                dve.wait_ge(s_dn, n + 1)
                if n >= 2:
                    dve.wait_ge(s_b, n - 1)
                dve.tensor_tensor(y_sb[:, n % 2, :], ps_y[n % 2][:, 0:D], b2_sb[:, 1, :], ALU.add).then_inc(s_a, 1)
                dve.wait_ge(s_a, n + 1)
                dve.scalar_tensor_tensor(out=x_tok[:, n, :], in0=y_sb[:, n % 2, :], scalar=val[:, 1, n:n + 1],
                                         in1=x_tok[:, n, :], op0=ALU.mult, op1=ALU.add).then_inc(s_b, 1)
                dve.wait_ge(s_b, n + 1)
                norm.statistics(dve, n)

            for u in range(UNITS):
                c, f = divmod(u, FT)
                dve.wait_ge(s_h2, u + 1)
                if f == 0 and c >= 2:
                    dve.wait_ge(s_dn, (c - 1) * QT)
                dve.tensor_tensor(h_fm[:, c % 2, f, :], h_two[:, u % 2, 0, :], h_two[:, u % 2, 1, :],
                                  ALU.add).then_inc(s_h, 1)
                if c >= 1 and f >= FT - QT:
                    out((c - 1) * QT + f - (FT - QT))
                if c >= 2 and f == 2:
                    norm.scale(dve, c - 2)
            norm.scale(dve, NQ - 2)
            for a in range(QT):
                out((NQ - 1) * QT + a)
            norm.scale(dve, NQ - 1)


def expert_ffn(nc, name, x_tok, x_fm, gates, top, w1, b1, w2, b2, cst):
    with ExitStack() as ctx:
        def sb(n, shape, dt):
            return ctx.enter_context(nc.sbuf_tensor(f"{name}_{n}", shape, dt))

        def sem(n):
            cst["semaphores"].append(nc.alloc_semaphore(f"{name}_{n}"))
            return cst["semaphores"][-1]


        w1_sb = sb("w1", [P, 2, DT, DFF], F32)
        w2_sb = sb("w2", [P, 2, FT, D], F32)
        b1_sb = sb("b1", [P, E, FT], F32)
        b2_sb = sb("b2", [E, D], F32)
        part = sb("part", [P, 2, NT], F32)
        weight = sb("weight", [P, NT, E], F32)
        second = sb("second", [P, NT, E], F32)
        weight_fm = sb("weight_fm", [E, S], F32)
        h_fm = sb("h", [P, 2, FT, QC], F32)
        ps_h = [ctx.enter_context(nc.psum_tensor(f"{name}_psh{i}", [P, QC], F32)) for i in range(4)]
        ps_y = [ctx.enter_context(nc.psum_tensor(f"{name}_psy{i}", [P, QC], F32)) for i in range(2)]
        s_b, s_chain, s_second, s_wt, s_wc, s_up, s_h, s_dn, s_a = map(
            sem, ("b", "chain", "second", "wt", "wc", "up", "h", "dn", "a"))
        s_w = [sem(f"w_{i}") for i in range(2)]
        block = ctx.enter_context(nc.Block())
        PAIRS = E // 2

        @block.sync
        def _(sp):
            sp.dma_start(b1_sb[:, :, :], b1).then_inc(s_b, 16)
            sp.dma_start(b2_sb[:, :], b2).then_inc(s_b, 16)

            def load(e, s):
                sp.dma_start(w1_sb[:, s, :, :], w1[bass.ds(e, 1), :, :].rearrange("o (t p) n -> p (o t) n", p=P))\
                    .then_inc(s_w[s], 16)
                sp.dma_start(w2_sb[:, s, :, :], w2[bass.ds(e, 1), :, :].rearrange("o (t p) n -> p (o t) n", p=P))\
                    .then_inc(s_w[s], 16)

            load(0, 0)
            load(1, 1)
            with sp.Fori(0, PAIRS - 1) as g:
                for s in range(2):
                    sp.wait_ge(s_dn, NT * (2 * g + s + 2))
                    load(2 * g + 2 + s, s)

        @block.tensor
        def _(pe):
            pe.wait_ge(s_chain, 4)
            for c in range(NQ):
                if c >= 2:
                    pe.wait_ge(s_wc, c - 1)
                for a in range(QT):
                    mm = pe.transpose(ps_y[c % 2][0:E, a * P:(a + 1) * P], weight[:, c * QT + a, :],
                                      cst["ident"][:, :])
                mm.then_inc(s_wt, 1)
            pe.wait_ge(s_wc, NQ)
            pe.wait_ge(s_b, 32)
            for n in range(NT):
                if n >= 2:
                    pe.wait_ge(s_a, n - 1)
                pe.matmul(ps_y[n % 2][:, 0:D], weight_fm[:, n * P:(n + 1) * P], b2_sb[:, :], start=True,
                          stop=True).then_inc(s_dn, 1)

            def expert(e, s, g):
                pe.wait_ge(s_w[s], 32 * (g + 1))

                def up(c):
                    for f in range(FT):
                        u = c * FT + f
                        pe.wait_ge(s_h, e * NQ * FT + u + 1)
                        for t in range(DT):
                            mm = pe.matmul(ps_h[u % 4][:, :], w1_sb[:, s, t, f * P:(f + 1) * P],
                                           x_fm[:, t, c * QC:(c + 1) * QC], start=(t == 0), stop=(t == DT - 1))
                        mm.then_inc(s_up, 1)

                def down(c):
                    pe.wait_ge(s_h, 4 + e * NQ * FT + (c + 1) * FT)
                    for a in range(QT):
                        n = c * QT + a
                        pe.wait_ge(s_a, (e + 1) * NT + n - 1)
                        for f in range(FT):
                            mm = pe.matmul(ps_y[n % 2][:, 0:D], h_fm[:, c % 2, f, a * P:(a + 1) * P],
                                           w2_sb[:, s, f, :], start=(f == 0), stop=(f == FT - 1))
                        mm.then_inc(s_dn, 1)

                up(0)
                for c in range(NQ):
                    if c + 1 < NQ:
                        up(c + 1)
                    down(c)

            with pe.Fori(0, PAIRS) as g:
                for s in range(2):
                    expert(2 * g + s, s, g)

        @block.scalar
        def _(act):
            for c in range(NQ):
                act.wait_ge(s_wt, c + 1)
                act.activation(weight_fm[:, c * QC:(c + 1) * QC], ps_y[c % 2][0:E, :], ACT.Copy).then_inc(s_wc, 1)
            act.wait_ge(s_b, 32)

            with act.Fori(0, E) as e:
                for c in range(NQ):
                    act.wait_ge(s_dn, NT * (e + 1) + (c - 1) * QT)
                    for f in range(FT):
                        u = c * FT + f
                        act.wait_ge(s_up, e * NQ * FT + u + 1)
                        act.activation(h_fm[:, c % 2, f, :], ps_h[u % 4][:, :], ACT.Relu,
                                       bias=b1_sb[:, bass.ds(e, 1), f]).then_inc(s_h, 1)

        @block.vector
        def _(dve):
            dve.memset(part[:, 0, 0:1], 0.0).then_inc(s_h, 4)
            dve.tensor_scalar(part[:, 1, :], top[:, :], 1.0, None, ALU.add).then_inc(s_chain, 1)
            dve.wait_ge(s_chain, 1)
            dve.wait_ge(s_h, 4)
            dve.reciprocal(part[:, 0, :], part[:, 1, :]).then_inc(s_chain, 1)
            dve.wait_ge(s_chain, 2)
            dve.tensor_tensor(part[:, 1, :], part[:, 0, :], top[:, :], ALU.mult).then_inc(s_chain, 1)
            dve.wait_ge(s_chain, 3)
            for t in range(NT):
                dve.tensor_scalar(second[:, t, :], gates[:, t, 1, :], part[:, 1, t:t + 1], None,
                                  ALU.mult).then_inc(s_second, 1)
            dve.wait_ge(s_second, NT)
            for t in range(NT):
                ins = dve.scalar_tensor_tensor(out=weight[:, t, :], in0=gates[:, t, 0, :],
                                               scalar=part[:, 0, t:t + 1], in1=second[:, t, :], op0=ALU.mult,
                                               op1=ALU.add)
            ins.then_inc(s_chain, 1)
            for n in range(NT):
                dve.wait_ge(s_dn, n + 1)
                dve.tensor_tensor(x_tok[:, n, :], x_tok[:, n, :], ps_y[n % 2][:, 0:D], ALU.add).then_inc(s_a, 1)

            with dve.Fori(0, E) as e:
                for n in range(NT):
                    dve.wait_ge(s_dn, NT * (e + 1) + n + 1)
                    dve.wait_ge(s_a, NT * e + n + 1)
                    dve.scalar_tensor_tensor(out=x_tok[:, n, :], in0=ps_y[n % 2][:, 0:D],
                                             scalar=weight[:, n, bass.ds(e, 1)], in1=x_tok[:, n, :],
                                             op0=ALU.mult, op1=ALU.add).then_inc(s_a, 1)


def decoder_kernel(nc, t, out, stages=range(6)):
    nc.disable_value_cache = True
    with ExitStack() as ctx:
        def sb(name, shape, dt, c=ctx):
            return c.enter_context(nc.sbuf_tensor(name, shape, dt))

        parts_q = nc.dram_tensor("parts_q", (3, D, S), BF16).ap()
        parts_k = nc.dram_tensor("parts_k", (3, D, S), BF16).ap()
        masks = nc.dram_tensor("key_masks", (3, S), BF16).ap()
        x_tok = sb("x_tok", [P, NT, D], F32)
        x_fm = sb("x_fm", [P, DT, S], F32)
        cst = make_constants(nc, sb, None)
        shared = ctx.enter_context(ExitStack())
        q_st = sb("q_st", [P, 2, GH, S], BF16, shared)
        k_st = sb("k_st", [P, 2, GH, S], BF16, shared)
        v_grp = sb("v_grp", [P, NT, GH, 2 * SH], F32, shared)

        with ExitStack() as c:
            user = sb("user_mask", [1, CTX], U8, c)
            rows = sb("mask_rows", [1, 3, S], BF16, c)
            s_x, s_user, s_rows, s_store, s_query_ones, s_key_ones, s_v_ones = (
                c.enter_context(nc.semaphore(n)) for n in (
                    "load_x", "load_mask", "mask_rows", "store_masks", "query_ones", "key_ones", "v_ones"))
            block = c.enter_context(nc.Block())

            @block.sync
            def _(sp):
                sp.dma_start(user[:, :], t["mask"]).then_inc(s_user, 16)
                sp.dma_start(x_fm[:, :, :], t["x_fm"].rearrange("(t p) n -> p t n", p=P)).then_inc(s_x, 16)
                sp.dma_start(x_tok[:, :, :], t["x"].rearrange("(t p) n -> p t n", p=P)).then_inc(s_x, 16)
                sp.wait_ge(s_rows, 5)
                sp.dma_start(masks.rearrange("(o r) n -> o r n", o=1), rows[:, :, :]).then_inc(s_store, 16)
                sp.wait_ge(s_store, 16)
                sp.wait_ge(s_x, 32)

            @block.vector
            def _(dve):
                dve.memset(rows[:, 0, :], 0.0).then_inc(s_rows, 1)
                dve.memset(rows[:, 1, 0:CTX], 0.0).then_inc(s_rows, 1)
                dve.memset(rows[:, 1, CTX:S], NEG).then_inc(s_rows, 1)
                dve.memset(rows[:, 2, CTX:S], NEG).then_inc(s_rows, 1)
                dve.wait_ge(s_user, 16)
                dve.tensor_scalar(rows[:, 2, 0:CTX], user[:, :], 1.0, -NEG, ALU.subtract,
                                  ALU.mult).then_inc(s_rows, 1)
                dve.memset(q_st[ROW_MASK:ROW_MAX + 1, :, :, :], 1.0).then_inc(s_query_ones, 1)

            @block.gpsimd
            def _(pool):
                pool.memset(k_st[ROW_MASK:ROW_MAX + 1, :, :, :], 1.0).then_inc(s_key_ones, 1)
                pool.wait_ge(s_key_ones, 1)
                pool.memset(v_grp[:, :, :, :], 1.0).then_inc(s_v_ones, 1)

        def attention(at, name, kv_source, mask, keep, dst, gamma=None, beta=None):
            with ExitStack() as c:
                s_load = nc.alloc_semaphore(f"{name}_load_stacks")
                cst["semaphores"].append(s_load)
                o_tok = sb(f"{name}_o_tok", [P, NT, D], F32, c)
                with ExitStack() as cc:
                    v_tok = sb(f"{name}_v", [P, at.tiles, D], F32, cc)
                    with ExitStack() as ccc:
                        kv = x_fm
                        if kv_source is not None:
                            kv = sb(f"{name}_ctx", [P, DT, at.keys], F32, ccc)
                            with ExitStack() as c4:
                                s_c = c4.enter_context(nc.semaphore(f"{name}_load_ctx"))
                                s_p = c4.enter_context(nc.semaphore(f"{name}_pad_ctx"))
                                block = c4.enter_context(nc.Block())

                                @block.sync
                                def _(sp):
                                    sp.dma_start(kv[:, :, 0:CTX], kv_source.rearrange("(t p) n -> p t n", p=P))\
                                        .then_inc(s_c, 16)
                                    sp.wait_ge(s_c, 16)

                                @block.vector
                                def _(dve):
                                    dve.memset(kv[:, :, CTX:CTXP], 0.0).then_inc(s_p, 1)

                        project(nc, at, f"{name}_proj", x_fm, kv, t[f"{name}_w"], t[f"{name}_bqk"],
                                t[f"{name}_bv"], v_tok, parts_q, parts_k, (q_st, k_st), s_load,
                                masks[mask:mask + 1, :], cst)
                    attend(nc, at, f"{name}_att", v_tok, parts_q, parts_k, o_tok, (q_st, k_st, v_grp), s_load, cst)
                close_attention(nc, f"{name}_close", x_tok, dst, x_fm, o_tok, t[f"{name}_wo"], t[f"{name}_bo"],
                                keep, gamma, beta, cst)

        if 0 in stages:
            clear_semaphores(nc, cst["semaphores"])
            with ExitStack() as c:
                z_tok = sb("z_tok", [P, NT, D], F32, c)
                attention(Attention("band", S, 32), "a0", None, 0, 1, z_tok, t["gamma"], t["beta"])
                gelu_ffn(nc, "f0", x_tok, z_tok, x_fm, t["f0_w1"], t["f0_b1"], t["f0_w2"], t["f0_b2"], cst)
        if 1 in stages:
            clear_semaphores(nc, cst["semaphores"])
            attention(Attention("causal", CTXP, 16), "x0", t["ctx_fm"], 1, 1, x_tok)
        if 2 in stages:
            clear_semaphores(nc, cst["semaphores"])
            with ExitStack() as c:
                gates = sb("l0_gates", [P, NT, 2, E], F32, c)
                top = sb("l0_top", [P, NT], F32, c)
                sums = sb("l0_sums", [P, NT], F32, c)
                spread = sb("l0_spread", [P, 2, S], F32, c)
                route(nc, "l0r", x_fm, t["l0_gate_w"], t["l0_gate_b"], E * R + E, gates, top, sums, spread, cst)
                lora_ffn(nc, "l0f", x_tok, x_fm, gates, top, sums, spread, t["l0_wi"], t["l0_bi"], t["l0_wo"],
                         t["l0_bo"], t["l0_lora_b"], cst)
        if 3 in stages:
            clear_semaphores(nc, cst["semaphores"])
            attention(Attention("full", S, 16), "a1", None, 0, 2, x_tok)
        if 4 in stages:
            clear_semaphores(nc, cst["semaphores"])
            attention(Attention("full", CTXP, 16), "x1", t["ctx_fm"], 2, 1, x_tok)
        shared.close()
        if 5 in stages:
            clear_semaphores(nc, cst["semaphores"])
            with ExitStack() as c:
                gates = sb("l1_gates", [P, NT, 2, E], F32, c)
                top = sb("l1_top", [P, NT], F32, c)
                sums = sb("l1_sums", [P, NT], F32, c)
                route(nc, "l1r", x_fm, t["l1_gate_w"], t["l1_gate_b"], E, gates, top, sums, None, cst)
                expert_ffn(nc, "l1f", x_tok, x_fm, gates, top, t["l1_w1"], t["l1_b1"], t["l1_w2"], t["l1_b2"], cst)
            layer_norm(nc, "n2", x_tok, None, None, None, cst)

        with ExitStack() as c:
            s_out = c.enter_context(nc.semaphore("store_out"))
            block = c.enter_context(nc.Block())

            @block.sync
            def _(sp):
                sp.dma_start(out.rearrange("(t p) n -> p t n", p=P), x_tok[:, :, :]).then_inc(s_out, 16)
                sp.wait_ge(s_out, 16)


def _layout(inputs):
    import numpy as np
    a = {k: np.asarray(v) for k, v in inputs.items()}
    x, ctx = a["x"][0], a["ctx_1024"][0]
    o = {"x": x, "x_fm": x.T, "ctx_fm": ctx.T, "mask": a["mask_Bx1xS2_bf1"].reshape(1, CTX).view(np.uint8)}

    def columns(b):
        return b.reshape(-1, P).T

    def row(b):
        return b.reshape(1, -1)

    def block(name, q, k, v, out, bq, bk, bv, bo):
        o[f"{name}_w"] = np.stack([q, k, v])
        o[f"{name}_bqk"] = np.stack([columns(bq), columns(bk)])
        o[f"{name}_bv"], o[f"{name}_wo"], o[f"{name}_bo"] = row(bv), out, row(bo)

    p = "L0_attn_"
    block("a0", *(a[p + n] for n in ("Wq", "Wk", "Wv", "Wo", "bq", "bk", "bv", "bo")))
    o["gamma"], o["beta"] = row(a[p + "gamma"]), row(a[p + "beta"])
    o["f0_w1"], o["f0_b1"], o["f0_w2"], o["f0_b2"] = a[p + "W1"], columns(a[p + "b1"]), a[p + "W2"], row(a[p + "b2"])
    p = "L0_xattn_"
    block("x0", *(a[p + n].T for n in ("Wq", "Wk", "Wv", "Wo")), *(a[p + n] for n in ("bq", "bk", "bv", "bo")))
    p = "L0_ffn_"
    o["l0_wi"], o["l0_bi"], o["l0_wo"], o["l0_bo"] = a[p + "wi"].T, columns(a[p + "bi"]), a[p + "wo"].T, row(a[p + "bo"])
    o["l0_gate_w"] = np.concatenate([a[p + "lora_A"].reshape(E * R, D).T, a[p + "gate_w"].T], axis=1)
    o["l0_gate_b"] = row(a[p + "gate_b"])
    o["l0_lora_b"] = a[p + "lora_B"].transpose(0, 2, 1).reshape(E * R, DFF)
    p = "L1_attn_"
    w = a[p + "qkv_w"].reshape(NSH, 3, SH, D).transpose(1, 3, 0, 2).reshape(3, D, D)
    b = a[p + "qkv_b"].reshape(NSH, 3, SH).transpose(1, 0, 2).reshape(3, D)
    block("a1", w[0], w[1], w[2], a[p + "fc_w"].T, b[0], b[1], b[2], a[p + "fc_b"])
    p = "L1_xattn_"
    block("x1", *(a[p + n] for n in ("Wq", "Wk", "Wv", "Wo", "bq", "bk", "bv", "bo")))
    p = "L1_ffn_"
    o["l1_gate_w"], o["l1_gate_b"], o["l1_w1"], o["l1_w2"] = a[p + "gate_w"], row(a[p + "gate_b"]), a[p + "w1"], a[p + "w2"]
    o["l1_b1"], o["l1_b2"] = a[p + "b1"].reshape(E, FT, P).transpose(2, 0, 1), a[p + "b2"]
    return o


def kernel(**inputs):
    import numpy as np
    import concourse.bacc as bacc
    from concourse.bass_utils import run_bass_kernel_spmd

    nc = bacc.Bacc("TRN2", target_bir_lowering=False, num_devices=1)
    arrays, t = {}, {}
    for name, a in _layout(inputs).items():
        a = np.ascontiguousarray(a)
        arrays[f"in_{name}"] = a
        t[name] = nc.dram_tensor(f"in_{name}", a.shape, mybir.dt.from_np(a.dtype), kind="ExternalInput").ap()
    out = nc.dram_tensor("out", (S, D), F32, kind="ExternalOutput").ap()
    decoder_kernel(nc, t, out)
    r = run_bass_kernel_spmd(nc, [arrays], core_ids=[0])
    return r.results[0]["out"].reshape(1, S, D)
```

```python
import concourse.bass as bass
from concourse import mybir
from contextlib import ExitStack

F32 = mybir.dt.float32
BF16 = mybir.dt.bfloat16
U8 = mybir.dt.uint8
U32 = mybir.dt.uint32
I32 = mybir.dt.int32
ALU = mybir.AluOpType
ACT = mybir.ActivationFunctionType
AX = mybir.AxisListType

P = 128
S = 2048
D = 256
DT = D // P
NT = S // P
CTX = 1601
CT = -(-CTX // P)
CTXP = CT * P
SH = 16
NSH = D // SH
GH = 4
NG = NSH // GH
QC = 512
NQ = S // QC
QT = QC // P
DFF = 1024
FT = DFF // P
E = 8
R = 16
EXPERT_TILES = 2 * NT + E - 1
NEG = -1.0e30
EPS = 1e-5
Q_PARTS = (0, 0, 1, 0, 2, 1)
K_PARTS = (0, 1, 0, 2, 0, 1)
ROWS_SPLIT = SH * len(Q_PARTS)
ROW_MASK, ROW_MAX = ROWS_SPLIT, ROWS_SPLIT + 1
BAND = 64


class Attention:

    def __init__(self, kind, keys, head_dim):
        self.kind, self.keys, self.head_dim = kind, keys, head_dim
        self.tiles = keys // P
        self.halves = head_dim // SH
        self.heads = GH // self.halves
        self.units = self.heads // 2
        self.pairs = [len(self.key_tiles(c)) for c in range(NQ)]
        self.pairs_group = sum(self.pairs)
        self.jobs = [self.heads * QT * len(self.max_chunks(QT * c)) for c in range(NQ)]
        self.jobs_group = sum(self.jobs)

    def key_tiles(self, c):
        if self.kind == "band":
            return [-1, 0, 1]
        if self.kind == "causal":
            return list(range(min(self.tiles, QT * (c + 1))))
        return list(range(self.tiles))

    def max_chunks(self, t):
        if self.kind == "band":
            lo, hi = max(t - 1, 0), min(t + 2, NT)
            return [(lo * P, (hi - lo) * P)]
        end = min(self.keys, (t + 1) * P) if self.kind == "causal" else self.keys
        return [(k, min(QC, end - k)) for k in range(0, end, QC)]


def clear_semaphores(nc, held):
    nc.clear_and_free_semaphores(held)
    held.clear()
    nc.all_engine_barrier()


def make_constants(nc, sb, sem):
    c = {"semaphores": []}
    c["ident"] = sb("ident", [P, P], F32)
    c["ident_bf"] = sb("ident_bf", [P, P], BF16)
    c["eps"] = sb("eps", [P, 1], F32)
    c["causal_k"] = sb("causal_k", [P, 2 * QC], BF16)
    c["causal_q"] = sb("causal_q", [P, QC], BF16)
    c["band_k"] = sb("band_k", [P, 5, P], BF16)
    c["band_q"] = sb("band_q", [P, 3 * P], BF16)
    with ExitStack() as ctx:
        done = ctx.enter_context(nc.semaphore("const_done"))
        block = ctx.enter_context(nc.Block())

        @block.gpsimd
        def _(pool):
            n = 0

            def fill(t, value):
                nonlocal n
                pool.memset(t, value).then_inc(done, 1)
                n += 1
                pool.wait_ge(done, n)

            def select(t, op, fill_value, base, pattern, mult):
                nonlocal n
                pool.affine_select(out=t, in_=t, compare_op=op, fill=fill_value, base=base, pattern=pattern,
                                   channel_multiplier=mult).then_inc(done, 1)
                n += 1
                pool.wait_ge(done, n)

            for t in (c["ident"], c["ident_bf"]):
                fill(t[:, :], 0.0)
                select(t[:, :], ALU.not_equal, 1.0, 0, [[-1, P]], 1)
            fill(c["eps"][:, :], EPS)
            off = QC - P
            fill(c["causal_k"][:, :], 0.0)
            select(c["causal_k"][:, :], ALU.is_ge, NEG, -off, [[1, 2 * QC]], -1)
            fill(c["causal_q"][:, :], 0.0)
            select(c["causal_q"][:, :], ALU.is_ge, NEG, off, [[-1, QC]], 1)
            fill(c["band_k"][:, :, :], 0.0)
            fill(c["band_k"][:, 3, :], NEG)
            for i, r in enumerate((-1, 0, 1)):
                select(c["band_k"][:, i, :], ALU.is_ge, NEG, BAND - P * r, [[1, P]], -1)
                select(c["band_k"][:, i, :], ALU.is_ge, NEG, BAND + P * r, [[-1, P]], 1)
            fill(c["band_q"][:, :], 0.0)
            select(c["band_q"][:, :], ALU.is_ge, NEG, BAND - P, [[1, 3 * P]], -1)
            select(c["band_q"][:, :], ALU.is_ge, NEG, BAND + P, [[-1, 3 * P]], 1)
    return c


class RowNorm:

    def __init__(self, nc, name, sb, pb, sem, x_tok, x_fm, cst, gain=None):
        self.x_tok, self.x_fm, self.cst, self.gain = x_tok, x_fm, cst, gain
        self.stat = sb("rn_stat", [P, NT, 6], F32)
        self.mean_var = sb("rn_mean_var", [P, NT, 2], F32)
        self.std = sb("rn_std", [P, NT], F32)
        self.inv = sb("rn_inv", [P, NT], F32)
        self.ps = [pb(f"rn_ps{i}", [P, QC], F32) for i in range(2)] if x_fm is not None else None
        self.s_stat, self.s_mv, self.s_std, self.s_inv, self.s_x, self.s_turn, self.s_fm = map(
            sem, ("rn_stat", "rn_mv", "rn_std", "rn_inv", "rn_x", "rn_turn", "rn_fm"))
        self.per_tile = 3 if gain is not None else 1

    def statistics(self, dve, t):
        dve.bn_stats(self.stat[:, t, :], self.x_tok[:, t, :]).then_inc(self.s_stat, 1)
        dve.wait_ge(self.s_stat, t + 1)
        dve.bn_aggr(self.mean_var[:, t, :], self.stat[:, t, :]).then_inc(self.s_mv, 1)

    def root(self, act, quad):
        q = slice(quad * 4, quad * 4 + 4)
        act.wait_ge(self.s_mv, 4 * (quad + 1))
        act.activation(self.std[:, q], self.mean_var[:, q, 1], ACT.Sqrt,
                       bias=self.cst["eps"][:, 0:1]).then_inc(self.s_std, 1)

    def scale(self, dve, quad):
        q = slice(quad * 4, quad * 4 + 4)
        dve.wait_ge(self.s_std, quad + 1)
        dve.reciprocal(self.inv[:, q], self.std[:, q]).then_inc(self.s_inv, 1)
        dve.wait_ge(self.s_inv, quad + 1)
        for t in range(quad * 4, quad * 4 + 4):
            x = self.x_tok[:, t, :]
            dve.tensor_scalar(x, x, self.mean_var[:, t, 0:1], self.inv[:, t:t + 1], ALU.subtract,
                              ALU.mult).then_inc(self.s_x, 1)
            if self.gain is not None:
                dve.wait_ge(self.s_x, 3 * t + 1)
                dve.tensor_tensor(x, x, self.gain[:, 0, :], ALU.mult).then_inc(self.s_x, 1)
                dve.wait_ge(self.s_x, 3 * t + 2)
                dve.tensor_tensor(x, x, self.gain[:, 1, :], ALU.add).then_inc(self.s_x, 1)

    def turn(self, pe, t):
        pe.wait_ge(self.s_x, self.per_tile * (t + 1))
        if t >= 2:
            pe.wait_ge(self.s_fm, t - 1)
        for m in range(DT):
            mm = pe.transpose(self.ps[t % 2][:, m * P:(m + 1) * P], self.x_tok[:, t, m * P:(m + 1) * P],
                              self.cst["ident"][:, :])
        mm.then_inc(self.s_turn, 1)

    def copy_out(self, act, t):
        act.wait_ge(self.s_turn, t + 1)
        act.activation(self.x_fm[:, :, t * P:(t + 1) * P],
                       self.ps[t % 2][:, 0:DT * P].rearrange("p (a b) -> p a b", a=DT),
                       ACT.Copy).then_inc(self.s_fm, 1)


def load_stacks(sp, at, g, slot, q_st, k_st, parts_q, parts_k, s_load):
    for n, (qp, kp) in enumerate(zip(Q_PARTS, K_PARTS)):
        rows = slice(n * SH, (n + 1) * SH)
        for st, parts, part, length in ((q_st, parts_q, qp, S), (k_st, parts_k, kp, at.keys)):
            src = parts[part, bass.ds(g * GH * SH, GH * SH), 0:length]
            sp.dma_start(st[rows, bass.ds(slot, 1), :, 0:length],
                         src.rearrange("(o j d) n -> d o j n", d=SH, o=1)).then_inc(s_load, 16)


LOADS = 2 * len(Q_PARTS)


def project(nc, at, name, x_fm, kv_fm, w, bias, v_bias, v_tok, parts_q, parts_k, stacks, s_load, mask, cst):
    q_st, k_st = stacks
    units = [(side, m, k, min(QC, n - k)) for m in range(DT) for side, n in ((0, S), (1, at.keys))
             for k in range(0, n, QC)]
    first = len(units) // DT
    NB, NS = 4, 6
    with ExitStack() as ctx:
        def sb(n, shape, dt):
            return ctx.enter_context(nc.sbuf_tensor(f"{name}_{n}", shape, dt))

        def sem(n):
            cst["semaphores"].append(nc.alloc_semaphore(f"{name}_{n}"))
            return cst["semaphores"][-1]

        w_sb = sb("w", [P, 3, DT, D], F32)
        bias_sb = sb("bias", [P, 2, DT], F32)
        vb_sb = sb("vb", [P, D], F32)
        exact = sb("exact", [P, 2, QC], F32)
        rest = sb("rest", [P, 2, QC], F32)
        parts = sb("parts", [P, NS, 3, QC], BF16)
        ps = [ctx.enter_context(nc.psum_tensor(f"{name}_ps{i}", [P, QC], F32)) for i in range(NB)]
        ps_v = [ctx.enter_context(nc.psum_tensor(f"{name}_psv{i}", [P, QC], F32)) for i in range(2)]
        s_w, s_mm, s_exact, s_high, s_rest, s_mid, s_low = map(
            sem, ("w", "mm", "exact", "high", "rest", "mid", "low"))
        s_vmm, s_vout, s_mask = sem("vmm"), sem("vout"), sem("mask")
        s_store = [sem(f"store{i}") for i in range(NS)]
        block = ctx.enter_context(nc.Block())

        @block.sync
        def _(sp):
            sp.dma_start(w_sb[:, 0, :, :], w[0].rearrange("(t p) n -> p t n", p=P)).then_inc(s_w, 16)
            sp.dma_start(bias_sb[:, :, :], bias.rearrange("s p t -> p s t")).then_inc(s_w, 16)
            for side in (1, 2):
                sp.dma_start(w_sb[:, side, :, :], w[side].rearrange("(t p) n -> p t n", p=P)).then_inc(s_w, 16)
            sp.dma_start(vb_sb[:, :], v_bias.to_broadcast((P, D))).then_inc(s_w, 16)
            for slot in range(2):
                for j in range(GH):
                    sp.dma_start(k_st[ROW_MASK:ROW_MASK + 1, slot, j, 0:at.keys],
                                 mask[:, 0:at.keys]).then_inc(s_mask, 16)
            for u, (side, m, k, n) in enumerate(units):
                sp.wait_ge(s_low, u + 1)
                sp.wait_ge(s_mid, u + 1)
                sp.wait_ge(s_high, u + 1)
                dst = (parts_q, parts_k)[side]
                sp.dma_start(dst[:, m * P:(m + 1) * P, k:k + n].rearrange("s p n -> p s n"),
                             parts[:, u % NS, :, 0:n]).then_inc(s_store[u % NS], 16)
                if u == first - 1:
                    for i in range(NS):
                        sp.wait_ge(s_store[i], 16 * len(range(i, u + 1, NS)))
                    load_stacks(sp, at, 0, 0, q_st, k_st, parts_q, parts_k, s_load)
            for i in range(NS):
                sp.wait_ge(s_store[i], 16 * len(range(i, len(units), NS)))
            sp.wait_ge(s_mask, 16 * 2 * GH)

        @block.tensor
        def _(pe):
            def v_tiles():
                for i in range(at.tiles):
                    if i >= 2:
                        pe.wait_ge(s_vout, i - 1)
                    for t in range(DT):
                        mm = pe.matmul(ps_v[i % 2][:, 0:D], kv_fm[:, t, i * P:(i + 1) * P], w_sb[:, 2, t, :],
                                       start=(t == 0), stop=(t == DT - 1))
                    mm.then_inc(s_vmm, 1)

            pe.wait_ge(s_w, 80)
            for u, (side, m, k, n) in enumerate(units):
                if u == first:
                    v_tiles()
                src = (x_fm, kv_fm)[side]
                if u >= NB:
                    pe.wait_ge(s_high, u - NB + 1)
                for t in range(DT):
                    mm = pe.matmul(ps[u % NB][:, 0:n], w_sb[:, side, t, m * P:(m + 1) * P], src[:, t, k:k + n],
                                   start=(t == 0), stop=(t == DT - 1))
                mm.then_inc(s_mm, 1)

        @block.scalar
        def _(act):
            act.wait_ge(s_w, 80)
            for u, (side, m, k, n) in enumerate(units):
                act.wait_ge(s_mm, u + 1)
                if u >= 2:
                    act.wait_ge(s_rest, u - 1)
                act.activation(exact[:, u % 2, 0:n], ps[u % NB][:, 0:n], ACT.Identity,
                               bias=bias_sb[:, side, m:m + 1]).then_inc(s_exact, 1)
                if u >= NS:
                    act.wait_ge(s_store[u % NS], 16 * (u // NS))
                act.activation(parts[:, u % NS, 0, 0:n], ps[u % NB][:, 0:n], ACT.Identity,
                               bias=bias_sb[:, side, m:m + 1]).then_inc(s_high, 1)

        @block.gpsimd
        def _(pool):
            for u, (side, m, k, n) in enumerate(units):
                pool.wait_ge(s_rest, u + 1)
                if u >= NS:
                    pool.wait_ge(s_store[u % NS], 16 * (u // NS))
                pool.tensor_copy(parts[:, u % NS, 1, 0:n], rest[:, u % 2, 0:n]).then_inc(s_mid, 1)

        @block.vector
        def _(dve):
            def low(u):
                n = units[u][3]
                dve.wait_ge(s_mid, u + 1)
                if u >= NS:
                    dve.wait_ge(s_store[u % NS], 16 * (u // NS))
                dve.tensor_tensor(parts[:, u % NS, 2, 0:n], rest[:, u % 2, 0:n], parts[:, u % NS, 1, 0:n],
                                  ALU.subtract).then_inc(s_low, 1)

            def v_tiles():
                for i in range(at.tiles):
                    dve.wait_ge(s_vmm, i + 1)
                    dve.tensor_tensor(v_tok[:, i, :], ps_v[i % 2][:, 0:D], vb_sb[:, :],
                                      ALU.add).then_inc(s_vout, 1)

            dve.wait_ge(s_w, 80)
            for u, (side, m, k, n) in enumerate(units):
                if u == first:
                    low(u - 1)
                    v_tiles()
                dve.wait_ge(s_exact, u + 1)
                dve.wait_ge(s_high, u + 1)
                if u >= 2:
                    dve.wait_ge(s_low, u - 1)
                dve.tensor_tensor(rest[:, u % 2, 0:n], exact[:, u % 2, 0:n], parts[:, u % NS, 0, 0:n],
                                  ALU.subtract).then_inc(s_rest, 1)
                if u >= 1 and u != first:
                    low(u - 1)
            low(len(units) - 1)


class MaxStream:
    PLACES = 4

    @staticmethod
    def sequence(at, groups):
        out, waiting = [], []
        for dg in range(groups):
            for c in range(NQ):
                jobs = [(h, a, i, k, n) for h in range(at.heads) for a in range(QT)
                        for i, (k, n) in enumerate(at.max_chunks(QT * c + a))]
                for job in jobs:
                    out.append(("max", dg, c) + job + (job is jobs[-1],))
                    waiting = [(w, due - 1) for w, due in waiting]
                    if waiting and waiting[0][1] <= 0:
                        out.append(waiting.pop(0)[0])
                waiting.append((("turn", dg, c), 4))
        return out + [w for w, _ in waiting]

    @classmethod
    def windows(cls, at):
        one, two = cls.sequence(at, 1), cls.sequence(at, 2)
        ahead = cls.AHEAD[at.kind] // 2 * 2
        return cls(one[:ahead]), cls(two[ahead:ahead + len(one)]), cls(one[ahead:])

    AHEAD = {"full": 84, "causal": 44, "band": 16}

    def __init__(self, entries):
        self.entries = entries
        self.turn_at = {e[1:3]: x for x, e in enumerate(entries) if e[0] == "turn"}

    def spread(self, at):
        starts = {(0, c): sum(at.pairs[:c]) for c in range(NQ)}
        starts[(1, 0)] = at.pairs_group
        due = [(max(starts[step] - 2, 1), x + 1) for step, x in self.turn_at.items() if step in starts]
        due.append((at.pairs_group, len(self.entries)))
        knots = [(0, 0)]
        while knots[-1][0] < at.pairs_group:
            k0, n0 = knots[-1]
            left = [(k, n) for k, n in due if k > k0]
            knots.append(max(left, key=lambda d: ((d[1] - n0) / (d[0] - k0), d[0])))

        def issued(k):
            for (k0, n0), (k1, n1) in zip(knots, knots[1:]):
                if k <= k1:
                    return min(len(self.entries), round(n0 + (n1 - n0) * (k - k0) / (k1 - k0)))

        marks = (0.25, 0.5, 0.75, 1.0) if at.units == 2 else (0.5, 0.5, 1.0, 1.0)
        self.places, done = [], 0
        for k in range(at.pairs_group):
            row = []
            for m in marks:
                upto = max(done, issued(k + m))
                row.append(range(done, upto))
                done = upto
            self.places.append(row)


def attend(nc, at, name, v_tok, parts_q, parts_k, o_tok, stacks, s_load, cst):
    scale = float(at.head_dim) ** -0.5
    HEADS, UNITS, HALVES = at.heads, at.units, at.halves
    NEGC = HEADS * QT
    q_st, k_st, v_grp = stacks
    pro, body, end = MaxStream.windows(at)
    total = len(body.entries)
    body.spread(at)
    end.spread(at)
    with ExitStack() as ctx:
        def sb(n, shape, dt):
            return ctx.enter_context(nc.sbuf_tensor(f"{name}_{n}", shape, dt))

        def pb(n, shape, dt):
            return ctx.enter_context(nc.psum_tensor(f"{name}_{n}", shape, dt))

        def sem(n):
            cst["semaphores"].append(nc.alloc_semaphore(f"{name}_{n}"))
            return cst["semaphores"][-1]

        prob = sb("prob", [P, 2, HEADS, QC], F32)
        part_max = sb("part_max", [P, NEGC, 4], F32)
        neg_max = sb("neg_max", [P, NEGC], BF16)
        neg_row = sb("neg_row", [NEGC, P], BF16)
        o_raw = sb("o_raw", [P, QC], F32)
        inv_den = sb("inv_den", [P, QT, GH, 1], F32)
        ps_s = [pb(f"ps_s{i}", [P, 2, QC], F32) for i in range(2)]
        ps_m = [pb(f"ps_m{i}", [P, QC], F32) for i in range(2)]
        ps_o = pb("ps_o", [P, QC], F32)
        ps_x = pb("ps_x", [P, QC], F32)
        s_scores = sem("scores")
        s_prob = sem("prob")
        s_pv = sem("pv")
        s_vgrp = sem("vgrp")
        s_msc = sem("msc")
        s_mred = sem("mred")
        s_neg = sem("neg")
        s_negd = sem("negd")
        s_ocopy = sem("ocopy")
        s_turn = sem("turn")
        s_inv = sem("inv")
        s_norm = sem("norm")
        block = ctx.enter_context(nc.Block())

        def pairs_before(g, c):
            return g * at.pairs_group + sum(at.pairs[:c])

        def entries_before(g):
            return len(pro.entries) + g * total

        def slot(g):
            return g % 2

        @block.sync
        def _(sp):
            def store_max(g, c, n, entry):
                sp.wait_ge(s_mred, 2 + entry + 1)
                for h in range(HEADS):
                    sp.dma_start(q_st[ROW_MAX:ROW_MAX + 1, bass.ds(slot(g), 1), HALVES * h, c * QC:(c + 1) * QC],
                                 neg_row[h * QT:(h + 1) * QT, :]).then_inc(s_negd, 16)

            def group(g, stream, last):
                if not last:
                    sp.wait_ge(s_load, 16 * LOADS * (g + 1))
                    sp.wait_ge(s_pv, 2 + pairs_before(g, 0))
                    load_stacks(sp, at, g + 1, slot(g + 1), q_st, k_st, parts_q, parts_k, s_load)
                for (dg, c), x in stream.turn_at.items():
                    store_max(g + dg, c, (g + dg) * NQ + c, entries_before(g) + x)

            for (_, c), x in pro.turn_at.items():
                store_max(0, c, c, x)
            with sp.Fori(0, NG - 1) as g:
                group(g, body, False)
            group(NG - 1, end, True)

        @block.gpsimd
        def _(pool):
            pool.sem_inc(s_prob, 2)
            pool.sem_inc(s_pv, 2)
            pool.sem_inc(s_mred, 2)
            pool.sem_inc(s_ocopy, 1)
            pool.sem_inc(s_norm, 1)
            pool.sem_inc(s_turn, 1)

            def group(g):
                pool.wait_ge(s_pv, 2 + pairs_before(g, 0))
                pool.tensor_copy(v_grp[:, 0:at.tiles, :, 0:SH],
                                 v_tok[:, 0:at.tiles, bass.ds(g * GH * SH, GH * SH)]
                                 .rearrange("p t (j d) -> p t j d", d=SH)).then_inc(s_vgrp, 1)

            with pool.Fori(0, NG - 1) as g:
                group(g)
            group(NG - 1)

        @block.tensor
        def _(pe):
            def scores(g, c, k, kt, u, un):
                bank = ps_s[k % 2 if UNITS == 1 else u]
                pe.wait_ge(s_prob, un + 1)
                for hh in range(2):
                    h = 2 * u + hh
                    if at.kind == "band":
                        for a in range(QT):
                            t = QT * c + a
                            inside = 0 <= t + kt < NT
                            key = (t + kt if inside else t) * P
                            qs = slice(c * QC + a * P, c * QC + (a + 1) * P)
                            out = bank[:, hh, a * P:(a + 1) * P]
                            for half in range(HALVES):
                                rows = ROW_MAX + 1 if half == 0 else ROWS_SPLIT
                                j = HALVES * h + half
                                pe.matmul(out, k_st[0:rows, bass.ds(slot(g), 1), j, key:key + P],
                                          q_st[0:rows, bass.ds(slot(g), 1), j, qs],
                                          start=(half == 0), stop=False)
                            mm = pe.matmul(out, cst["ident_bf"][:, :],
                                           cst["band_k"][:, kt + 1 if inside else 3, :],
                                           start=False, stop=True)
                    else:
                        diag = at.kind == "causal" and kt >= QT * c
                        mm = pe.matmul(bank[:, hh, :],
                                       k_st[0:ROW_MAX + 1, bass.ds(slot(g), 1), h, kt * P:(kt + 1) * P],
                                       q_st[0:ROW_MAX + 1, bass.ds(slot(g), 1), h, c * QC:(c + 1) * QC],
                                       start=True, stop=not diag)
                        if diag:
                            off = QC - P - P * (kt - QT * c)
                            mm = pe.matmul(bank[:, hh, :], cst["ident_bf"][:, :],
                                           cst["causal_k"][:, off:off + QC], start=False, stop=True)
                mm.then_inc(s_scores, 1)

            def max_entry(g, stream, x, count):
                entry = stream.entries[x]
                pe.wait_ge(s_mred, count + x + 1)
                dg, c = entry[1:3]
                if entry[0] == "turn":
                    pe.wait_ge(s_neg, (g + dg) * NQ + c + 1)
                    pe.transpose(ps_m[x % 2][:, :].bitcast(BF16)[0:NEGC, 0:P], neg_max[:, :],
                                 cst["ident_bf"][:, :]).then_inc(s_msc, 1)
                    return
                h, a, i, k, w, last = entry[3:]
                t = QT * c + a
                out = ps_m[x % 2][:, 0:w]
                masked = at.kind == "band" or (at.kind == "causal" and k + w == (t + 1) * P)
                for half in range(HALVES):
                    rows = ROW_MASK + 1 if half == 0 else ROWS_SPLIT
                    j = HALVES * h + half
                    mm = pe.matmul(out, q_st[0:rows, bass.ds(slot(g + dg), 1), j, t * P:(t + 1) * P],
                                   k_st[0:rows, bass.ds(slot(g + dg), 1), j, k:k + w],
                                   start=(half == 0), stop=(half == HALVES - 1 and not masked))
                if masked:
                    if at.kind == "band":
                        m = cst["band_q"][:, k - (t - 1) * P:k - (t - 1) * P + w]
                    else:
                        m = cst["causal_q"][:, QC - w:QC]
                    mm = pe.matmul(out, cst["ident_bf"][:, :], m, start=False, stop=True)
                mm.then_inc(s_msc, 1)

            def times_v(g, c, i, k, kt, between=lambda: None):
                if i == 0:
                    pe.wait_ge(s_ocopy, g * NQ + c + 1)
                    if c == 0:
                        pe.wait_ge(s_vgrp, g + 1)
                pe.wait_ge(s_prob, 2 + UNITS * (pairs_before(g, 0) + k + 1))
                n = at.pairs[c]
                if at.kind == "band":
                    for a in range(QT):
                        t = QT * c + a
                        key = t + kt if 0 <= t + kt < NT else t
                        for j in range(GH):
                            mm = pe.matmul(ps_o[32 * j:32 * j + 32, a * P:(a + 1) * P], v_grp[:, key, j, :],
                                           prob[:, k % 2, j // HALVES, a * P:(a + 1) * P],
                                           start=(i == 0 and a == 0), stop=(i == n - 1),
                                           skip_group_check=True)
                else:
                    for j in range(GH):
                        mm = pe.matmul(ps_o[32 * j:32 * j + 32, :], v_grp[:, kt, j, :],
                                       prob[:, k % 2, j, :], start=(i == 0), stop=(i == n - 1))
                        if j == 0:
                            between()
                mm.then_inc(s_pv, 1)

            def turn_out(n):
                pe.wait_ge(s_ocopy, n + 2)
                pe.wait_ge(s_norm, n + 1)
                for a in range(QT):
                    mm = pe.transpose(ps_x[:, a * P:(a + 1) * P], o_raw[:, a * P:(a + 1) * P],
                                      cst["ident"][:, :])
                mm.then_inc(s_turn, 1)

            def group(g, stream):
                before = None
                k = 0
                for c in range(NQ):
                    n = g * NQ + c
                    pe.wait_ge(s_negd, 16 * HEADS * (n + 1))
                    for i, kt in enumerate(at.key_tiles(c)):
                        places = stream.places[k]
                        for u in range(UNITS):
                            scores(g, c, k, kt, u, UNITS * (pairs_before(g, 0) + k) + u)
                            for x in places[u]:
                                stream_entry(g, stream, x)
                        def entries(x):
                            for e in x:
                                stream_entry(g, stream, e)

                        if before is not None:
                            times_v(*before, between=(lambda: entries(places[2])) if UNITS == 2 else (lambda: None))
                        for x in ([] if UNITS == 2 and before is not None else list(places[2])) + list(places[3]):
                            stream_entry(g, stream, x)
                        if i == 2 and c > 0:
                            turn_out(n - 1)
                        before = (g, c, i, k, kt)
                        k += 1
                times_v(*before)
                turn_out(g * NQ + NQ - 1)

            def stream_entry(g, stream, x):
                ahead = [i for i, e in enumerate(stream.entries) if e[1] == 1]
                if ahead and x == ahead[0]:
                    pe.wait_ge(s_load, 16 * LOADS * (g + 2))
                max_entry(g, stream, x, entries_before(g))

            pe.wait_ge(s_load, 16 * LOADS)
            for x in range(len(pro.entries)):
                max_entry(0, pro, x, 0)
            for g in range(NG - 1):
                group(g, body)
            group(NG - 1, end)

        @block.scalar
        def _(act):
            def copy_o(g, c):
                n = g * NQ + c
                act.wait_ge(s_pv, 2 + pairs_before(g, c) + at.pairs[c])
                act.wait_ge(s_turn, n + 1)
                act.activation(o_raw[:, :], ps_o[:, :], ACT.Copy).then_inc(s_ocopy, 1)

            def group(g):
                k = 0
                for c in range(NQ):
                    for i in range(at.pairs[c]):
                        pair = pairs_before(g, 0) + k
                        act.wait_ge(s_pv, pair + (2 if k == 0 and at.pairs_group % 2 else 1))
                        for u in range(UNITS):
                            un = UNITS * pair + u
                            act.wait_ge(s_scores, un + 1)
                            bank = ps_s[k % 2 if UNITS == 1 else u]
                            act.activation(prob[:, k % 2, 2 * u:2 * u + 2, :], bank[:, :, :], ACT.Exp,
                                           scale=scale).then_inc(s_prob, 1)
                        if i == 0 and c > 0:
                            copy_o(g, c - 1)
                        k += 1
                copy_o(g, NQ - 1)

            act.wait_ge(s_prob, 2)
            act.wait_ge(s_ocopy, 1)
            act.wait_ge(s_turn, 1)
            with act.Fori(0, NG - 1) as g:
                group(g)
            group(NG - 1)

        @block.vector
        def _(dve):
            def max_entry(g, stream, x, count):
                entry = stream.entries[x]
                dg, c = entry[1:3]
                n = (g + dg) * NQ + c
                dve.wait_ge(s_msc, count + x + 1)
                if entry[0] == "turn":
                    if not (type(n) is int and n == 0):
                        dve.wait_ge(s_negd, 16 * HEADS * n)
                    dve.tensor_copy(neg_row[:, :],
                                    ps_m[x % 2][:, :].bitcast(BF16)[0:NEGC, 0:P]).then_inc(s_mred, 1)
                    return
                h, a, i, k, w, last = entry[3:]
                dve.tensor_reduce(part_max[:, h * QT + a, i:i + 1], ps_m[x % 2][:, 0:w], AX.X,
                                  ALU.max).then_inc(s_mred, 1)
                if last:
                    dve.wait_ge(s_mred, 2 + count + x + 1)
                    dve.tensor_reduce(neg_max[:, :], part_max[:, :, 0:len(at.max_chunks(QT * c))], AX.X,
                                      ALU.max, negate=True).then_inc(s_neg, 1)
                    dve.wait_ge(s_neg, n + 1)

            def normalise(g, c):
                n = g * NQ + c
                heads = ps_x[:, :].rearrange("p (a j d) -> p a j d", a=QT, j=GH)
                dve.wait_ge(s_turn, n + 2)
                dve.reciprocal(inv_den[:, :, :, :], heads[:, :, :, SH:SH + 1]).then_inc(s_inv, 1)
                dve.wait_ge(s_inv, n + 1)
                dve.tensor_tensor(o_tok[:, c * QT:(c + 1) * QT, bass.ds(g * GH * SH, GH * SH)]
                                  .rearrange("p a (j d) -> p a j d", d=SH), heads[:, :, :, 0:SH],
                                  inv_den[:, :, :, :].to_broadcast((P, QT, GH, SH)), ALU.mult).then_inc(s_norm, 1)

            def group(g, stream):
                k = 0
                for c in range(NQ):
                    for i in range(at.pairs[c]):
                        for place in stream.places[k]:
                            for x in place:
                                max_entry(g, stream, x, entries_before(g))
                        if i == 2 and c > 0:
                            normalise(g, c - 1)
                        k += 1
                normalise(g, NQ - 1)

            dve.wait_ge(s_mred, 2)
            dve.wait_ge(s_norm, 1)
            for x in range(len(pro.entries)):
                max_entry(0, pro, x, 0)
            with dve.Fori(0, NG - 1) as g:
                group(g, body)
            group(NG - 1, end)


def close_attention(nc, name, x_tok, dst, x_fm, o_tok, wo, bo, keep, gamma, beta, cst):
    with ExitStack() as ctx:
        def sb(n, shape, dt):
            return ctx.enter_context(nc.sbuf_tensor(f"{name}_{n}", shape, dt))

        def pb(n, shape, dt):
            return ctx.enter_context(nc.psum_tensor(f"{name}_{n}", shape, dt))

        def sem(n):
            cst["semaphores"].append(nc.alloc_semaphore(f"{name}_{n}"))
            return cst["semaphores"][-1]

        wo_sb = sb("wo", [P, DT, D], F32)
        bo_sb = sb("bo", [P, D], F32)
        gain = sb("gain", [P, 2, D], F32) if gamma is not None else None
        o_fm = sb("o_fm", [P, 2, DT, P], F32)
        ps_o = [pb(f"pso{i}", [P, QC], F32) for i in range(2)]
        ps_y = [pb(f"psy{i}", [P, QC], F32) for i in range(2)]
        s_w, s_turn, s_fm, s_mm, s_base, s_y = map(sem, ("w", "turn", "fm", "mm", "base", "y"))
        norm = RowNorm(nc, name, sb, pb, sem, dst, x_fm, cst, gain)
        LAG = 7
        block = ctx.enter_context(nc.Block())
        loads = 16 * (2 + (2 if gamma is not None else 0))

        @block.sync
        def _(sp):
            sp.dma_start(wo_sb[:, :, :], wo.rearrange("(t p) n -> p t n", p=P)).then_inc(s_w, 16)
            sp.dma_start(bo_sb[:, :], bo.to_broadcast((P, D))).then_inc(s_w, 16)
            if gamma is not None:
                sp.dma_start(gain[:, 0, :], gamma.to_broadcast((P, D))).then_inc(s_w, 16)
                sp.dma_start(gain[:, 1, :], beta.to_broadcast((P, D))).then_inc(s_w, 16)

        @block.gpsimd
        def _(pool):
            pool.wait_ge(s_w, loads)
            for t in range(NT):
                src = x_tok
                if keep == 2:
                    pool.tensor_tensor(dst[:, t, :], x_tok[:, t, :], x_tok[:, t, :], ALU.add).then_inc(s_base, 1)
                    pool.wait_ge(s_base, 2 * t + 1)
                    src = dst
                pool.tensor_tensor(dst[:, t, :], src[:, t, :], bo_sb[:, :], ALU.add).then_inc(s_base, 1)

        @block.tensor
        def _(pe):
            def turn(t):
                if t >= 2:
                    pe.wait_ge(s_fm, t - 1)
                for m in range(DT):
                    mm = pe.transpose(ps_o[t % 2][:, m * P:(m + 1) * P], o_tok[:, t, m * P:(m + 1) * P],
                                      cst["ident"][:, :])
                mm.then_inc(s_turn, 1)

            def product(t):
                pe.wait_ge(s_fm, t + 1)
                if t >= 2:
                    pe.wait_ge(s_y, t - 1)
                for m in range(DT):
                    mm = pe.matmul(ps_y[t % 2][:, 0:D], o_fm[:, t % 2, m, :], wo_sb[:, m, :],
                                   start=(m == 0), stop=(m == DT - 1))
                mm.then_inc(s_mm, 1)

            pe.wait_ge(s_w, loads)
            turn(0)
            for t in range(NT):
                if t + 1 < NT:
                    turn(t + 1)
                product(t)
                if t >= LAG:
                    norm.turn(pe, t - LAG)
            for t in range(NT - LAG, NT):
                norm.turn(pe, t)

        @block.scalar
        def _(act):
            def copy(t):
                act.wait_ge(s_turn, t + 1)
                if t >= 2:
                    act.wait_ge(s_mm, t - 1)
                act.activation(o_fm[:, t % 2, :, :], ps_o[t % 2][:, 0:D].rearrange("p (a b) -> p a b", a=DT),
                               ACT.Copy).then_inc(s_fm, 1)

            copy(0)
            for t in range(NT):
                if t + 1 < NT:
                    copy(t + 1)
                if t % 4 == 1 and t > 4:
                    norm.root(act, t // 4 - 1)
                if t >= LAG:
                    norm.copy_out(act, t - LAG)
            norm.root(act, NT // 4 - 1)
            for t in range(NT - LAG, NT):
                norm.copy_out(act, t)

        @block.vector
        def _(dve):
            for t in range(NT):
                dve.wait_ge(s_mm, t + 1)
                dve.wait_ge(s_base, (t + 1) * (2 if keep == 2 else 1))
                dve.tensor_tensor(dst[:, t, :], dst[:, t, :], ps_y[t % 2][:, 0:D], ALU.add).then_inc(s_y, 1)
                dve.wait_ge(s_y, t + 1)
                norm.statistics(dve, t)
                if t % 4 == 1 and t > 4:
                    norm.scale(dve, t // 4 - 1)
            norm.scale(dve, NT // 4 - 1)


def gelu_ffn(nc, name, x_tok, z_tok, x_fm, w1, b1, w2, b2, cst):
    with ExitStack() as ctx:
        def sb(n, shape, dt):
            return ctx.enter_context(nc.sbuf_tensor(f"{name}_{n}", shape, dt))

        def pb(n, shape, dt):
            return ctx.enter_context(nc.psum_tensor(f"{name}_{n}", shape, dt))

        def sem(n):
            cst["semaphores"].append(nc.alloc_semaphore(f"{name}_{n}"))
            return cst["semaphores"][-1]

        w1_sb = sb("w1", [P, DT, DFF], F32)
        w2_sb = sb("w2", [P, FT, D], F32)
        b1_sb = sb("b1", [P, FT], F32)
        b2_sb = sb("b2", [P, D], F32)
        h_fm = sb("h", [P, 2, FT, QC], F32)
        ps_h = [pb(f"psh{i}", [P, QC], F32) for i in range(4)]
        ps_y = [pb(f"psy{i}", [P, QC], F32) for i in range(2)]
        s_w, s_w2, s_up, s_h, s_dn, s_y, s_base = map(sem, ("w", "w2", "up", "h", "dn", "y", "base"))
        norm = RowNorm(nc, name, sb, pb, sem, x_tok, x_fm, cst)
        block = ctx.enter_context(nc.Block())

        @block.sync
        def _(sp):
            sp.dma_start(w1_sb[:, :, :], w1.rearrange("(t p) n -> p t n", p=P)).then_inc(s_w, 16)
            sp.dma_start(b1_sb[:, :], b1).then_inc(s_w, 16)
            sp.dma_start(b2_sb[:, :], b2.to_broadcast((P, D))).then_inc(s_w, 16)
            sp.dma_start(w2_sb[:, :, :], w2.rearrange("(t p) n -> p t n", p=P)).then_inc(s_w2, 16)

        @block.gpsimd
        def _(pool):
            pool.wait_ge(s_w, 48)
            for n in range(NT):
                pool.tensor_tensor(x_tok[:, n, :], x_tok[:, n, :], z_tok[:, n, :], ALU.add).then_inc(s_base, 1)
                pool.wait_ge(s_base, 2 * n + 1)
                pool.tensor_tensor(x_tok[:, n, :], x_tok[:, n, :], b2_sb[:, :], ALU.add).then_inc(s_base, 1)

        @block.tensor
        def _(pe):
            def up(c):
                for f in range(FT):
                    u = c * FT + f
                    if u >= 4:
                        pe.wait_ge(s_h, u - 3)
                    for t in range(DT):
                        mm = pe.matmul(ps_h[u % 4][:, :], w1_sb[:, t, f * P:(f + 1) * P],
                                       x_fm[:, t, c * QC:(c + 1) * QC], start=(t == 0), stop=(t == DT - 1))
                    mm.then_inc(s_up, 1)

            def down(c):
                pe.wait_ge(s_h, (c + 1) * FT)
                for a in range(QT):
                    n = c * QT + a
                    if n >= 2:
                        pe.wait_ge(s_y, n - 1)
                    for f in range(FT):
                        mm = pe.matmul(ps_y[n % 2][:, 0:D], h_fm[:, c % 2, f, a * P:(a + 1) * P],
                                       w2_sb[:, f, :], start=(f == 0), stop=(f == FT - 1))
                    mm.then_inc(s_dn, 1)

            pe.wait_ge(s_w, 48)
            up(0)
            pe.wait_ge(s_w2, 16)
            for c in range(NQ):
                if c + 1 < NQ:
                    up(c + 1)
                if c >= 2:
                    for t in range((c - 2) * QT, (c - 1) * QT):
                        norm.turn(pe, t)
                down(c)
            for t in range((NQ - 2) * QT, NT):
                norm.turn(pe, t)

        @block.scalar
        def _(act):
            act.wait_ge(s_w, 48)
            for c in range(NQ):
                if c >= 2:
                    act.wait_ge(s_dn, (c - 1) * QT)
                for f in range(FT):
                    u = c * FT + f
                    act.wait_ge(s_up, u + 1)
                    act.activation(h_fm[:, c % 2, f, :], ps_h[u % 4][:, :], ACT.Gelu,
                                   bias=b1_sb[:, f:f + 1]).then_inc(s_h, 1)
                if c >= 2:
                    norm.root(act, c - 2)
            for c in range(NQ):
                if c >= NQ - 2:
                    norm.root(act, c)
                for t in range(c * QT, (c + 1) * QT):
                    norm.copy_out(act, t)

        @block.vector
        def _(dve):
            for n in range(NT):
                dve.wait_ge(s_base, 2 * n + 2)
                dve.wait_ge(s_dn, n + 1)
                dve.tensor_tensor(x_tok[:, n, :], x_tok[:, n, :], ps_y[n % 2][:, 0:D], ALU.add).then_inc(s_y, 1)
                dve.wait_ge(s_y, n + 1)
                norm.statistics(dve, n)
                if n % 4 == 3 and n > 4:
                    norm.scale(dve, n // 4 - 1)
            norm.scale(dve, NT // 4 - 1)


def route(nc, name, x_fm, gate_w, gate_b, cols, gates, top, sums, spread, cst, load_more=lambda sp: None):
    lora = cols > E
    with ExitStack() as ctx:
        def sb(n, shape, dt):
            return ctx.enter_context(nc.sbuf_tensor(f"{name}_{n}", shape, dt))

        def sem(n):
            cst["semaphores"].append(nc.alloc_semaphore(f"{name}_{n}"))
            return cst["semaphores"][-1]


        w_sb = sb("w", [P, DT, cols], F32)
        b_sb = sb("b", [P, E], F32)
        logit = sb("logit", [P, NT, E], F32)
        best = sb("best", [P, NT, 8], F32)
        index = sb("index", [P, NT, 8], U32)
        index_f = sb("index_f", [P, NT, 2], F32)
        order = sb("order", [P, E], F32)
        delta = sb("delta", [P, NT, E + 1], F32)
        a_tok = sb("a", [P, NT, E * R], F32) if lora else None
        picked = sb("picked", [P, 2, NT, E * R], F32) if lora else None
        swap = sb("swap", [P, NT, E], F32)
        ps = [ctx.enter_context(nc.psum_tensor(f"{name}_ps{i}", [P, QC], F32)) for i in range(2)]
        ps_t = [ctx.enter_context(nc.psum_tensor(f"{name}_pst{i}", [P, QC], F32)) for i in range(2)]
        s_w, s_mm, s_logit, s_a, s_exp, s_turn, s_out = map(sem, ("w", "mm", "logit", "a", "exp", "turn", "out"))
        s_best, s_index, s_chain, s_delta, s_picked = map(sem, ("best", "index", "chain", "delta", "picked"))
        block = ctx.enter_context(nc.Block())

        @block.sync
        def _(sp):
            sp.dma_start(w_sb[:, :, :], gate_w.rearrange("(t p) n -> p t n", p=P)).then_inc(s_w, 16)
            sp.dma_start(b_sb[:, :], gate_b.to_broadcast((P, E))).then_inc(s_w, 16)
            load_more(sp)

        @block.tensor
        def _(pe):
            pe.wait_ge(s_w, 32)
            for t in range(NT):
                if t >= 2:
                    pe.wait_ge(s_logit, t - 1)
                for k in range(DT):
                    mm = pe.matmul(ps[t % 2][:, 0:cols], x_fm[:, k, t * P:(t + 1) * P], w_sb[:, k, :],
                                   start=(k == 0), stop=(k == DT - 1))
                mm.then_inc(s_mm, 1)
            if lora:
                for n in range(2 * NQ):
                    which, c = divmod(n, NQ)
                    pe.wait_ge(s_picked, which + 1)
                    if n >= 2:
                        pe.wait_ge(s_out, n - 1)
                    for a in range(QT):
                        mm = pe.transpose(ps_t[n % 2][:, a * P:(a + 1) * P], picked[:, which, c * QT + a, :],
                                          cst["ident"][:, :])
                    mm.then_inc(s_turn, 1)

        @block.vector
        def _(dve):
            links = 0

            def link(instruction):
                nonlocal links
                instruction.then_inc(s_chain, 1)
                links += 1
                dve.wait_ge(s_chain, links)

            for e in range(E):
                link(dve.memset(order[:, e:e + 1], float(e)))
            dve.wait_ge(s_w, 32)
            for t in range(NT):
                dve.wait_ge(s_mm, t + 1)
                if lora:
                    link(dve.tensor_copy(a_tok[:, t, :], ps[t % 2][:, 0:E * R]))
                dve.tensor_tensor(logit[:, t, :], ps[t % 2][:, cols - E:cols], b_sb[:, :],
                                  ALU.add).then_inc(s_logit, 1)
                dve.wait_ge(s_logit, t + 1)
                dve.max(best[:, t, :], logit[:, t, :]).then_inc(s_best, 1)
                dve.wait_ge(s_best, t + 1)
                dve.max_index(index[:, t, :], best[:, t, :], logit[:, t, :]).then_inc(s_index, 1)
            dve.tensor_tensor(delta[:, :, 0:E], logit[:, :, :], best[:, :, 0:1].to_broadcast((P, NT, E)),
                              ALU.subtract).then_inc(s_delta, 1)
            dve.tensor_tensor(delta[:, :, E:E + 1], best[:, :, 1:2], best[:, :, 0:1],
                              ALU.subtract).then_inc(s_delta, 1)
            dve.wait_ge(s_index, NT)
            link(dve.tensor_copy(index_f[:, :, :], index[:, :, 0:2]))
            for s in range(2):
                for t in range(NT):
                    ins = dve.tensor_scalar(gates[:, t, s, :], order[:, :], index_f[:, t, s:s + 1], None,
                                            ALU.is_equal)
                    if t == NT - 1:
                        link(ins)
            dve.wait_ge(s_exp, 1)
            link(dve.tensor_reduce(sums[:, :], delta[:, :, 0:E], AX.X, ALU.add))
            link(dve.tensor_copy(top[:, :], delta[:, :, E]))
            if lora:
                def wide(g):
                    return g.rearrange("p t (e o) -> p t e o", o=1).to_broadcast((P, NT, E, R))

                a4 = a_tok[:, :, :].rearrange("p t (e r) -> p t e r", r=R)
                link(dve.tensor_tensor(swap[:, :, :], gates[:, :, 1, :], gates[:, :, 0, :], ALU.subtract))
                for s, g in ((0, gates[:, :, 0, :]), (1, swap[:, :, :])):
                    dve.tensor_tensor(picked[:, s, :, :].rearrange("p t (e r) -> p t e r", r=R), a4, wide(g),
                                      ALU.mult).then_inc(s_picked, 1)

        @block.scalar
        def _(act):
            act.wait_ge(s_delta, 2)
            act.activation(delta[:, :, :], delta[:, :, :], ACT.Exp).then_inc(s_exp, 1)
            if lora:
                for n in range(2 * NQ):
                    which, c = divmod(n, NQ)
                    act.wait_ge(s_turn, n + 1)
                    act.activation(spread[:, which, c * QC:(c + 1) * QC], ps_t[n % 2][:, :],
                                   ACT.Copy).then_inc(s_out, 1)


def lora_ffn(nc, name, x_tok, x_fm, gates, top, sums, spread, wi, bi, wo, bo, lora_b, cst):
    with ExitStack() as ctx:
        def sb(n, shape, dt):
            return ctx.enter_context(nc.sbuf_tensor(f"{name}_{n}", shape, dt))

        def sem(n):
            cst["semaphores"].append(nc.alloc_semaphore(f"{name}_{n}"))
            return cst["semaphores"][-1]


        w1_sb = sb("w1", [P, DT, DFF], F32)
        lb_sb = sb("lb", [P, DFF], F32)
        w2_sb = sb("w2", [P, FT, D], F32)
        b1_sb = sb("b1", [P, FT], F32)
        b2_sb = sb("b2", [P, 2, D], F32)
        val = sb("val", [P, 2, NT], F32)
        h_fm = sb("h", [P, 2, FT, QC], F32)
        h_two = sb("h_two", [P, 2, 2, QC], F32)
        y_sb = sb("y", [P, 2, D], F32)
        ps_h = [ctx.enter_context(nc.psum_tensor(f"{name}_psh{i}", [P, QC], F32)) for i in range(4)]
        ps_y = [ctx.enter_context(nc.psum_tensor(f"{name}_psy{i}", [P, QC], F32)) for i in range(2)]
        s_w, s_w2, s_one, s_two, s_h1, s_h2, s_h, s_dn, s_a, s_b, s_v = map(
            sem, ("w", "w2", "one", "two", "h1", "h2", "h", "dn", "a", "b", "v"))
        norm = RowNorm(nc, name, sb, lambda n, shape, dt: ctx.enter_context(nc.psum_tensor(f"{name}_{n}", shape, dt)),
                       sem, x_tok, x_fm, cst)
        block = ctx.enter_context(nc.Block())
        UNITS = NQ * FT

        @block.sync
        def _(sp):
            sp.dma_start(w1_sb[:, :, :], wi.rearrange("(t p) n -> p t n", p=P)).then_inc(s_w, 16)
            sp.dma_start(lb_sb[:, :], lora_b).then_inc(s_w, 16)
            sp.dma_start(b1_sb[:, :], bi).then_inc(s_w, 16)
            sp.dma_start(w2_sb[:, :, :], wo.rearrange("(t p) n -> p t n", p=P)).then_inc(s_w2, 16)
            sp.dma_start(b2_sb[:, 0, :], bo.to_broadcast((P, D))).then_inc(s_w2, 16)

        @block.tensor
        def _(pe):
            def first(u):
                c, f = divmod(u, FT)
                if u >= 4:
                    pe.wait_ge(s_h2, u - 3)
                for t in range(DT):
                    pe.matmul(ps_h[u % 4][:, :], w1_sb[:, t, f * P:(f + 1) * P], x_fm[:, t, c * QC:(c + 1) * QC],
                              start=(t == 0), stop=False)
                pe.matmul(ps_h[u % 4][:, :], lb_sb[:, f * P:(f + 1) * P], spread[:, 0, c * QC:(c + 1) * QC],
                          start=False, stop=True).then_inc(s_one, 1)

            def second(u):
                c, f = divmod(u, FT)
                pe.wait_ge(s_h1, u + 1)
                pe.matmul(ps_h[u % 4][:, :], lb_sb[:, f * P:(f + 1) * P], spread[:, 1, c * QC:(c + 1) * QC],
                          start=False, stop=True, skip_group_check=True).then_inc(s_two, 1)

            def down(n):
                c, a = divmod(n, QT)
                pe.wait_ge(s_h, (c + 1) * FT)
                if n >= 2:
                    pe.wait_ge(s_a, n - 1)
                for f in range(FT):
                    mm = pe.matmul(ps_y[n % 2][:, 0:D], h_fm[:, c % 2, f, a * P:(a + 1) * P],
                                   w2_sb[:, f, :], start=(f == 0), stop=(f == FT - 1))
                mm.then_inc(s_dn, 1)

            pe.wait_ge(s_w, 48)
            for u in range(UNITS):
                first(u)
                if u >= 1:
                    second(u - 1)
                if u == 4:
                    pe.wait_ge(s_w2, 32)
                c, f = divmod(u, FT)
                if c >= 1 and f >= FT - QT:
                    down((c - 1) * QT + f - (FT - QT))
                if c >= 2 and f >= FT - QT:
                    norm.turn(pe, (c - 2) * QT + f - (FT - QT))
            second(UNITS - 1)
            for a in range(QT):
                norm.turn(pe, (NQ - 2) * QT + a)
                down((NQ - 1) * QT + a)
            for a in range(QT):
                norm.turn(pe, (NQ - 1) * QT + a)

        @block.scalar
        def _(act):
            act.wait_ge(s_w, 48)
            for u in range(UNITS):
                c, f = divmod(u, FT)
                if u >= 2:
                    act.wait_ge(s_h, u - 1)
                act.wait_ge(s_one, u + 1)
                act.activation(h_two[:, u % 2, 0, :], ps_h[u % 4][:, :], ACT.Relu,
                               bias=b1_sb[:, f:f + 1]).then_inc(s_h1, 1)
                act.wait_ge(s_two, u + 1)
                act.activation(h_two[:, u % 2, 1, :], ps_h[u % 4][:, :], ACT.Relu,
                               bias=b1_sb[:, f:f + 1]).then_inc(s_h2, 1)
                if c >= 2 and f == 1:
                    norm.root(act, c - 2)
                if c >= 2 and f >= FT - QT:
                    norm.copy_out(act, (c - 2) * QT + f - (FT - QT))
            for c in (NQ - 2, NQ - 1):
                norm.root(act, c)
                for a in range(QT):
                    norm.copy_out(act, c * QT + a)

        @block.vector
        def _(dve):
            dve.reciprocal(val[:, 0, :], sums[:, :]).then_inc(s_v, 1)
            dve.wait_ge(s_v, 1)
            dve.scalar_tensor_tensor(out=val[:, 1, :], in0=top[:, :], scalar=1.0, in1=val[:, 0, :], op0=ALU.add,
                                     op1=ALU.mult).then_inc(s_v, 1)
            dve.wait_ge(s_w2, 32)
            dve.tensor_scalar(b2_sb[:, 1, :], b2_sb[:, 0, :], 2.0, None, ALU.mult).then_inc(s_v, 1)
            dve.wait_ge(s_v, 3)

            def out(n):
                dve.wait_ge(s_dn, n + 1)
                if n >= 2:
                    dve.wait_ge(s_b, n - 1)
                dve.tensor_tensor(y_sb[:, n % 2, :], ps_y[n % 2][:, 0:D], b2_sb[:, 1, :], ALU.add).then_inc(s_a, 1)
                dve.wait_ge(s_a, n + 1)
                dve.scalar_tensor_tensor(out=x_tok[:, n, :], in0=y_sb[:, n % 2, :], scalar=val[:, 1, n:n + 1],
                                         in1=x_tok[:, n, :], op0=ALU.mult, op1=ALU.add).then_inc(s_b, 1)
                dve.wait_ge(s_b, n + 1)
                norm.statistics(dve, n)

            for u in range(UNITS):
                c, f = divmod(u, FT)
                dve.wait_ge(s_h2, u + 1)
                if f == 0 and c >= 2:
                    dve.wait_ge(s_dn, (c - 1) * QT)
                dve.tensor_tensor(h_fm[:, c % 2, f, :], h_two[:, u % 2, 0, :], h_two[:, u % 2, 1, :],
                                  ALU.add).then_inc(s_h, 1)
                if c >= 1 and f >= FT - QT:
                    out((c - 1) * QT + f - (FT - QT))
                if c >= 2 and f == 2:
                    norm.scale(dve, c - 2)
            norm.scale(dve, NQ - 2)
            for a in range(QT):
                out((NQ - 1) * QT + a)
            norm.scale(dve, NQ - 1)


def place_tokens(nc, name, x_tok, gates, slots, tile_expert, x_slots, s_zero, s_scatter, cst):
    C = 2 * NT
    with ExitStack() as ctx:
        def sb(n, shape, dt):
            return ctx.enter_context(nc.sbuf_tensor(f"{name}_{n}", shape, dt))

        def sem(n):
            cst["semaphores"].append(nc.alloc_semaphore(f"{name}_{n}"))
            return cst["semaphores"][-1]

        before = sb("before", [P, P], F32)
        ones = sb("ones", [P, P], F32)
        ladder = sb("ladder", [P, 64], F32)
        total = sb("total", [P, C, E], F32)
        upto = sb("upto", [P, 2, C, E], F32)
        rank = sb("rank", [P, C, E], F32)
        over = sb("over", [P, E, NT], F32)
        tiles = sb("tiles", [P, E], F32)
        end = sb("end", [P, E], F32)
        base = sb("base", [P, E], F32)
        slot_f = sb("slot_f", [P, C], F32)
        past = sb("past", [1, EXPERT_TILES, E], F32)
        expert_f = sb("expert_f", [1, EXPERT_TILES], F32)
        ps_before = ctx.enter_context(nc.psum_tensor(f"{name}_ps_before", [P, QC], F32))
        ps_total = ctx.enter_context(nc.psum_tensor(f"{name}_ps_total", [P, QC], F32))
        s_const, s_count, s_chain, s_slots = map(sem, ("const", "count", "chain", "slots"))
        choice = gates[:, :, :, :].rearrange("p t s e -> p (t s) e")
        block = ctx.enter_context(nc.Block())

        @block.tensor
        def _(pe):
            pe.wait_ge(s_const, 3)
            flat = gates[:, :, :, :].rearrange("p t s e -> p (t s e)")
            pe.matmul(ps_total[:, 0:C * E], ones[:, :], flat, start=True, stop=True).then_inc(s_count, 1)
            pe.matmul(ps_before[:, 0:C * E], before[:, :], flat, start=True, stop=True).then_inc(s_count, 1)

        @block.vector
        def _(dve):
            links = 0

            def link(instruction):
                nonlocal links
                instruction.then_inc(s_chain, 1)
                links += 1
                dve.wait_ge(s_chain, links)

            link(dve.memset(ladder[:, 0:1], 0.0))
            for n in (1, 2, 4, 8, 16, 32):
                link(dve.tensor_scalar(ladder[:, n:2 * n], ladder[:, 0:n], float(n), None, ALU.add))
            dve.wait_ge(s_count, 1)
            link(dve.tensor_copy(total[:, :, :], ps_total[:, 0:C * E].rearrange("p (c e) -> p c e", e=E)))
            src, side, n = total[:, :, :], 0, 1
            while n < C:
                dst = upto[:, side, :, :]
                link(dve.tensor_copy(dst[:, 0:n, :], src[:, 0:n, :]))
                link(dve.tensor_tensor(dst[:, n:C, :], src[:, n:C, :], src[:, 0:C - n, :], ALU.add))
                src, side, n = dst, 1 - side, 2 * n
            count = src[:, C - 1, :].rearrange("p (e o) -> p e o", o=1)
            link(dve.tensor_scalar(base[:, :].rearrange("p (e o) -> p e o", o=1), count, 1.0 / P, None, ALU.mult))
            link(dve.tensor_tensor(over[:, :, :],
                                   base[:, :].rearrange("p (e o) -> p e o", o=1).to_broadcast((P, E, NT)),
                                   ladder[:, 0:NT].rearrange("p (o n) -> p o n", o=1).to_broadcast((P, E, NT)),
                                   ALU.is_gt))
            link(dve.tensor_reduce(tiles[:, :], over[:, :, :], AX.X, ALU.add))
            link(dve.tensor_copy(end[:, 0:1], tiles[:, 0:1]))
            for e in range(1, E):
                link(dve.tensor_tensor(end[:, e:e + 1], end[:, e - 1:e], tiles[:, e:e + 1], ALU.add))
            link(dve.tensor_tensor(base[:, :], end[:, :], tiles[:, :], ALU.subtract))
            link(dve.tensor_scalar(base[:, :], base[:, :], float(P), None, ALU.mult))
            link(dve.tensor_tensor(rank[:, :, :], src, total[:, :, :], ALU.subtract))
            link(dve.tensor_tensor(rank[:, :, :], rank[:, :, :],
                                   base[:, :].rearrange("p (o e) -> p o e", o=1).to_broadcast((P, C, E)), ALU.add))
            dve.wait_ge(s_count, 2)
            link(dve.tensor_tensor(rank[:, :, :], rank[:, :, :],
                                   ps_before[:, 0:C * E].rearrange("p (c e) -> p c e", e=E), ALU.add))
            link(dve.tensor_tensor(rank[:, :, :], rank[:, :, :], choice, ALU.mult))
            link(dve.tensor_reduce(slot_f[:, :], rank[:, :, :], AX.X, ALU.add))
            dve.tensor_copy(slots[:, :], slot_f[:, :]).then_inc(s_slots, 1)
            link(dve.tensor_tensor(
                past[:, :, :],
                ladder[0:1, 0:EXPERT_TILES].rearrange("p (n o) -> p n o", o=1).to_broadcast((1, EXPERT_TILES, E)),
                end[0:1, :].rearrange("p (o e) -> p o e", o=1).to_broadcast((1, EXPERT_TILES, E)), ALU.is_ge))
            link(dve.tensor_reduce(expert_f[:, :], past[:, :, :], AX.X, ALU.add))
            link(dve.tensor_scalar(expert_f[:, :], expert_f[:, :], float(E - 1), None, ALU.min))
            link(dve.tensor_copy(tile_expert[:, :], expert_f[:, :]))

        @block.gpsimd
        def _(pool):
            pool.memset(ones[:, :], 1.0).then_inc(s_const, 1)
            pool.wait_ge(s_const, 1)
            pool.memset(before[:, :], 1.0).then_inc(s_const, 1)
            pool.wait_ge(s_const, 2)
            pool.affine_select(out=before[:, :], in_=before[:, :], compare_op=ALU.is_ge, fill=0.0, base=-1,
                               pattern=[[1, P]], channel_multiplier=-1).then_inc(s_const, 1)
            pool.wait_ge(s_const, 3)
            pool.wait_ge(s_slots, 1)
            pool.wait_ge(s_zero, 16)
            for c in range(C):
                pool.indirect_dma_start(x_slots, bass.IndirectOffsetOnAxis(slots[:, c:c + 1], 0),
                                        x_tok[:, c // 2, :], None).then_inc(s_scatter, 16)


def load_experts(sp, w1, b1, w2, b2, w1_sb, b1_sb, w2_sb, b2_sb, s_weights):
    for e in range(E):
        sp.dma_start(w1_sb[:, e, :, :], w1[e].rearrange("(t p) n -> p t n", p=P)).then_inc(s_weights, 16)
        sp.dma_start(w2_sb[:, e, :, :], w2[e].rearrange("(t p) n -> p t n", p=P)).then_inc(s_weights, 16)
    sp.dma_start(b1_sb[:, :, :], b1).then_inc(s_weights, 16)
    sp.dma_start(b2_sb[:, :, :], b2.rearrange("(o e) n -> o e n", o=1).to_broadcast((P, E, D)))\
        .then_inc(s_weights, 16)


EXPERT_LOADS = 2 * E + 2


def expert_ffn(nc, name, x_tok, top, slots, tile_expert, x_slots, y_slots, weights, s_weights, s_scatter, out, cst):
    w1_sb, b1_sb, w2_sb, b2_sb = weights
    HALF = DFF // QC
    FH = FT // HALF
    DEPTH = 4
    with ExitStack() as ctx:
        def sb(n, shape, dt):
            return ctx.enter_context(nc.sbuf_tensor(f"{name}_{n}", shape, dt))

        def sem(n):
            cst["semaphores"].append(nc.alloc_semaphore(f"{name}_{n}"))
            return cst["semaphores"][-1]

        x_rows = sb("x_rows", [P, D], F32)
        x_cols = sb("x_cols", [P, DT, P], F32)
        h_rows = sb("h_rows", [P, HALF, QC], F32)
        h_cols = sb("h_cols", [P, FT, P], F32)
        y_rows = sb("y_rows", [P, D], F32)
        part = sb("part", [P, 2, NT], F32)
        y_two = sb("y_two", [P, DEPTH, 2, D], F32)
        ps_x = ctx.enter_context(nc.psum_tensor(f"{name}_ps_x", [P, QC], F32))
        ps_h = [ctx.enter_context(nc.psum_tensor(f"{name}_ps_h{i}", [P, QC], F32)) for i in range(HALF)]
        ps_t = [ctx.enter_context(nc.psum_tensor(f"{name}_ps_t{i}", [P, QC], F32)) for i in range(HALF)]
        ps_y = ctx.enter_context(nc.psum_tensor(f"{name}_ps_y", [P, QC], F32))
        s_row = sem("row")
        s_xturn = sem("xturn")
        s_xcol = sem("xcol")
        s_up = sem("up")
        s_hrow = sem("hrow")
        s_hturn = sem("hturn")
        s_hcol = sem("hcol")
        s_down = sem("down")
        s_y = sem("y")
        s_stored = sem("stored")
        s_part, s_first, s_sum, s_out = map(sem, ("part", "first", "sum", "out"))
        s_two = [sem(f"two{i}") for i in range(DEPTH)]
        norm = RowNorm(nc, name, sb, None, sem, x_tok, None, cst)
        block = ctx.enter_context(nc.Block())
        N = EXPERT_TILES

        def rows(dram, i):
            return dram[bass.ds(i * P, P), :]

        def expert_of(engine, i):
            return engine.value_load(tile_expert[0:1, bass.ds(i, 1)], min_val=0, max_val=E - 1)

        @block.sync
        def _(sp):
            def load(i):
                sp.dma_start(x_rows[:, :], rows(x_slots, i)).then_inc(s_row, 16)

            def store(i):
                sp.wait_ge(s_y, i + 2)
                sp.dma_start(rows(y_slots, i), y_rows[:, :]).then_inc(s_stored, 16)

            sp.wait_ge(s_scatter, 16 * 2 * NT)
            load(0)
            sp.wait_ge(s_xturn, 1)
            load(1)
            with sp.Fori(0, N - 2) as i:
                sp.wait_ge(s_xturn, i + 2)
                load(i + 2)
                store(i)
            store(N - 2)
            store(N - 1)
            for t in range(NT):
                sp.wait_ge(norm.s_x, t + 1)
                sp.dma_start(out[t * P:(t + 1) * P, :], x_tok[:, t, :]).then_inc(s_out, 16)
            sp.wait_ge(s_out, 16 * NT)

        @block.tensor
        def _(pe):
            def turn_x(i, first=False):
                pe.wait_ge(s_row, 16 * (i + 1))
                if not first:
                    pe.wait_ge(s_xcol, i)
                for m in range(DT):
                    mm = pe.transpose(ps_x[:, m * P:(m + 1) * P], x_rows[:, m * P:(m + 1) * P], cst["ident"][:, :])
                mm.then_inc(s_xturn, 1)

            def up(i, first=False):
                e = expert_of(pe, i)
                pe.wait_ge(s_xcol, i + 1)
                if not first:
                    pe.wait_ge(s_hrow, HALF * i)
                for hh in range(HALF):
                    for m in range(DT):
                        mm = pe.matmul(ps_h[hh][:, :], x_cols[:, m, :],
                                       w1_sb[:, bass.ds(e, 1), m, hh * QC:(hh + 1) * QC],
                                       start=(m == 0), stop=(m == DT - 1))
                    mm.then_inc(s_up, 1)

            def turn_h(i, first=False):
                for hh in range(HALF):
                    pe.wait_ge(s_hrow, HALF * i + hh + 1)
                    if not first:
                        pe.wait_ge(s_hcol, FT * i + FH * hh - FH)
                    for f in range(FH):
                        mm = pe.transpose(ps_t[hh][:, f * P:(f + 1) * P], h_rows[:, hh, f * P:(f + 1) * P],
                                          cst["ident"][:, :])
                    mm.then_inc(s_hturn, 1)

            def down(i):
                e = expert_of(pe, i)
                pe.wait_ge(s_y, i + 1)
                pe.wait_ge(s_hcol, FT * (i + 1))
                for f in range(FT):
                    mm = pe.matmul(ps_y[:, 0:D], h_cols[:, f, :], w2_sb[:, bass.ds(e, 1), f, :],
                                   start=(f == 0), stop=(f == FT - 1))
                mm.then_inc(s_down, 1)

            turn_x(0, first=True)
            pe.wait_ge(s_weights, 16 * EXPERT_LOADS)
            up(0, first=True)
            turn_x(1)
            turn_h(0, first=True)
            with pe.Fori(0, N - 2) as i:
                up(i + 1)
                turn_x(i + 2)
                down(i)
                turn_h(i + 1)
            up(N - 1)
            down(N - 2)
            turn_h(N - 1)
            down(N - 1)

        @block.scalar
        def _(act):
            def copy_x(i, first=False):
                act.wait_ge(s_xturn, i + 1)
                if not first:
                    act.wait_ge(s_up, HALF * i)
                act.activation(x_cols[:, :, :], ps_x[:, 0:D].rearrange("p (a b) -> p a b", a=DT),
                               ACT.Copy).then_inc(s_xcol, 1)

            def relu(i, first=False):
                e = expert_of(act, i)
                if not first:
                    act.wait_ge(s_down, i)
                for f in range(FT):
                    act.wait_ge(s_hturn, HALF * i + f // FH + 1)
                    act.activation(h_cols[:, f, :], ps_t[f // FH][:, f % FH * P:(f % FH + 1) * P], ACT.Relu,
                                   bias=b1_sb[:, bass.ds(e, 1), f]).then_inc(s_hcol, 1)

            copy_x(0, first=True)
            act.wait_ge(s_weights, 16 * EXPERT_LOADS)
            copy_x(1)
            relu(0, first=True)
            with act.Fori(0, N - 2) as i:
                copy_x(i + 2)
                relu(i + 1)
            relu(N - 1)
            for quad in range(NT // 4):
                norm.root(act, quad)

        @block.gpsimd
        def _(pool):
            pool.sem_inc(s_y, 1)
            pool.sem_inc(s_stored, 16)
            pool.wait_ge(s_stored, 16 * (N + 1))
            for t in range(NT):
                if t >= DEPTH:
                    pool.wait_ge(s_sum, t - DEPTH + 1)
                for s in range(2):
                    pool.indirect_dma_start(y_two[:, t % DEPTH, s, :], None, y_slots,
                                            bass.IndirectOffsetOnAxis(slots[:, 2 * t + s:2 * t + s + 1], 0))\
                        .then_inc(s_two[t % DEPTH], 16)

        @block.vector
        def _(dve):
            dve.tensor_scalar(part[:, 1, :], top[:, :], 1.0, None, ALU.add).then_inc(s_part, 1)
            dve.wait_ge(s_part, 1)
            dve.reciprocal(part[:, 0, :], part[:, 1, :]).then_inc(s_part, 1)
            dve.wait_ge(s_part, 2)
            dve.tensor_tensor(part[:, 1, :], part[:, 0, :], top[:, :], ALU.mult).then_inc(s_part, 1)
            dve.wait_ge(s_weights, 16 * EXPERT_LOADS)

            def copy_h(i, first=False):
                for hh in range(HALF):
                    dve.wait_ge(s_up, HALF * i + hh + 1)
                    if not first:
                        dve.wait_ge(s_hturn, HALF * i + hh - 1)
                    dve.tensor_copy(h_rows[:, hh, :], ps_h[hh][:, :]).then_inc(s_hrow, 1)

            def add_bias(i):
                e = expert_of(dve, i)
                dve.wait_ge(s_down, i + 1)
                dve.wait_ge(s_stored, 16 * (i + 1))
                dve.tensor_tensor(y_rows[:, :], ps_y[:, 0:D], b2_sb[:, bass.ds(e, 1), :]
                                  .rearrange("p o n -> p (o n)"), ALU.add).then_inc(s_y, 1)

            copy_h(0, first=True)
            with dve.Fori(0, N - 1) as i:
                copy_h(i + 1)
                add_bias(i)
            add_bias(N - 1)
            dve.wait_ge(s_part, 3)
            for t in range(NT):
                dve.wait_ge(s_two[t % DEPTH], 32 * (t // DEPTH + 1))
                dve.scalar_tensor_tensor(out=x_tok[:, t, :], in0=y_two[:, t % DEPTH, 0, :],
                                         scalar=part[:, 0, t:t + 1], in1=x_tok[:, t, :], op0=ALU.mult,
                                         op1=ALU.add).then_inc(s_first, 1)
                dve.wait_ge(s_first, t + 1)
                dve.scalar_tensor_tensor(out=x_tok[:, t, :], in0=y_two[:, t % DEPTH, 1, :],
                                         scalar=part[:, 1, t:t + 1], in1=x_tok[:, t, :], op0=ALU.mult,
                                         op1=ALU.add).then_inc(s_sum, 1)
                dve.wait_ge(s_sum, t + 1)
                norm.statistics(dve, t)
                if t % 4 == 1 and t > 4:
                    norm.scale(dve, t // 4 - 1)
            norm.scale(dve, NT // 4 - 1)


def decoder_kernel(nc, t, out, stages=range(6)):
    nc.disable_value_cache = True
    with ExitStack() as ctx:
        def sb(name, shape, dt, c=ctx):
            return c.enter_context(nc.sbuf_tensor(name, shape, dt))

        parts_q = nc.dram_tensor("parts_q", (3, D, S), BF16).ap()
        parts_k = nc.dram_tensor("parts_k", (3, D, S), BF16).ap()
        masks = nc.dram_tensor("key_masks", (3, S), BF16).ap()
        x_slots = nc.dram_tensor("x_slots", (EXPERT_TILES * P, D), F32).ap()
        y_slots = nc.dram_tensor("y_slots", (EXPERT_TILES * P, D), F32).ap()
        s_zero = nc.alloc_semaphore("slots_cleared")
        zeros = sb("zeros", [P, D], F32)
        x_tok = sb("x_tok", [P, NT, D], F32)
        x_fm = sb("x_fm", [P, DT, S], F32)
        cst = make_constants(nc, sb, None)
        shared = ctx.enter_context(ExitStack())
        q_st = sb("q_st", [P, 2, GH, S], BF16, shared)
        k_st = sb("k_st", [P, 2, GH, S], BF16, shared)
        v_grp = sb("v_grp", [P, NT, GH, 2 * SH], F32, shared)

        with ExitStack() as c:
            user = sb("user_mask", [1, CTX], U8, c)
            rows = sb("mask_rows", [1, 3, S], BF16, c)
            s_x, s_user, s_rows, s_store, s_query_ones, s_key_ones, s_v_ones, s_zeros = (
                c.enter_context(nc.semaphore(n)) for n in (
                    "load_x", "load_mask", "mask_rows", "store_masks", "query_ones", "key_ones", "v_ones", "zeros"))
            block = c.enter_context(nc.Block())

            @block.sync
            def _(sp):
                sp.dma_start(user[:, :], t["mask"]).then_inc(s_user, 16)
                sp.dma_start(x_fm[:, :, :], t["x_fm"].rearrange("(t p) n -> p t n", p=P)).then_inc(s_x, 16)
                sp.dma_start(x_tok[:, :, :], t["x"].rearrange("(t p) n -> p t n", p=P)).then_inc(s_x, 16)
                sp.wait_ge(s_rows, 5)
                sp.dma_start(masks.rearrange("(o r) n -> o r n", o=1), rows[:, :, :]).then_inc(s_store, 16)
                sp.wait_ge(s_store, 16)
                sp.wait_ge(s_x, 32)

            @block.scalar
            def _(act):
                act.wait_ge(s_zeros, 1)
                act.dma_start(x_slots.rearrange("(t p) n -> p t n", p=P),
                              zeros[:, :].rearrange("p (o n) -> p o n", o=1).to_broadcast((P, EXPERT_TILES, D)))\
                    .then_inc(s_zero, 16)

            @block.vector
            def _(dve):
                dve.memset(zeros[:, :], 0.0).then_inc(s_zeros, 1)
                dve.memset(rows[:, 0, :], 0.0).then_inc(s_rows, 1)
                dve.memset(rows[:, 1, 0:CTX], 0.0).then_inc(s_rows, 1)
                dve.memset(rows[:, 1, CTX:S], NEG).then_inc(s_rows, 1)
                dve.memset(rows[:, 2, CTX:S], NEG).then_inc(s_rows, 1)
                dve.wait_ge(s_user, 16)
                dve.tensor_scalar(rows[:, 2, 0:CTX], user[:, :], 1.0, -NEG, ALU.subtract,
                                  ALU.mult).then_inc(s_rows, 1)
                dve.memset(q_st[ROW_MASK:ROW_MAX + 1, :, :, :], 1.0).then_inc(s_query_ones, 1)

            @block.gpsimd
            def _(pool):
                pool.memset(k_st[ROW_MASK:ROW_MAX + 1, :, :, :], 1.0).then_inc(s_key_ones, 1)
                pool.wait_ge(s_key_ones, 1)
                pool.memset(v_grp[:, :, :, :], 1.0).then_inc(s_v_ones, 1)

        def attention(at, name, kv_source, mask, keep, dst, gamma=None, beta=None):
            with ExitStack() as c:
                s_load = nc.alloc_semaphore(f"{name}_load_stacks")
                cst["semaphores"].append(s_load)
                o_tok = sb(f"{name}_o_tok", [P, NT, D], F32, c)
                with ExitStack() as cc:
                    v_tok = sb(f"{name}_v", [P, at.tiles, D], F32, cc)
                    with ExitStack() as ccc:
                        kv = x_fm
                        if kv_source is not None:
                            kv = sb(f"{name}_ctx", [P, DT, at.keys], F32, ccc)
                            with ExitStack() as c4:
                                s_c = c4.enter_context(nc.semaphore(f"{name}_load_ctx"))
                                s_p = c4.enter_context(nc.semaphore(f"{name}_pad_ctx"))
                                block = c4.enter_context(nc.Block())

                                @block.sync
                                def _(sp):
                                    sp.dma_start(kv[:, :, 0:CTX], kv_source.rearrange("(t p) n -> p t n", p=P))\
                                        .then_inc(s_c, 16)
                                    sp.wait_ge(s_c, 16)

                                @block.vector
                                def _(dve):
                                    dve.memset(kv[:, :, CTX:CTXP], 0.0).then_inc(s_p, 1)

                        project(nc, at, f"{name}_proj", x_fm, kv, t[f"{name}_w"], t[f"{name}_bqk"],
                                t[f"{name}_bv"], v_tok, parts_q, parts_k, (q_st, k_st), s_load,
                                masks[mask:mask + 1, :], cst)
                    attend(nc, at, f"{name}_att", v_tok, parts_q, parts_k, o_tok, (q_st, k_st, v_grp), s_load, cst)
                close_attention(nc, f"{name}_close", x_tok, dst, x_fm, o_tok, t[f"{name}_wo"], t[f"{name}_bo"],
                                keep, gamma, beta, cst)

        if 0 in stages:
            clear_semaphores(nc, cst["semaphores"])
            with ExitStack() as c:
                z_tok = sb("z_tok", [P, NT, D], F32, c)
                attention(Attention("band", S, 32), "a0", None, 0, 1, z_tok, t["gamma"], t["beta"])
                gelu_ffn(nc, "f0", x_tok, z_tok, x_fm, t["f0_w1"], t["f0_b1"], t["f0_w2"], t["f0_b2"], cst)
        if 1 in stages:
            clear_semaphores(nc, cst["semaphores"])
            attention(Attention("causal", CTXP, 16), "x0", t["ctx_fm"], 1, 1, x_tok)
        if 2 in stages:
            clear_semaphores(nc, cst["semaphores"])
            with ExitStack() as c:
                gates = sb("l0_gates", [P, NT, 2, E], F32, c)
                top = sb("l0_top", [P, NT], F32, c)
                sums = sb("l0_sums", [P, NT], F32, c)
                spread = sb("l0_spread", [P, 2, S], F32, c)
                route(nc, "l0r", x_fm, t["l0_gate_w"], t["l0_gate_b"], E * R + E, gates, top, sums, spread, cst)
                lora_ffn(nc, "l0f", x_tok, x_fm, gates, top, sums, spread, t["l0_wi"], t["l0_bi"], t["l0_wo"],
                         t["l0_bo"], t["l0_lora_b"], cst)
        if 3 in stages:
            clear_semaphores(nc, cst["semaphores"])
            attention(Attention("full", S, 16), "a1", None, 0, 2, x_tok)
        if 4 in stages:
            clear_semaphores(nc, cst["semaphores"])
            attention(Attention("full", CTXP, 16), "x1", t["ctx_fm"], 2, 1, x_tok)
        shared.close()
        if 5 in stages:
            clear_semaphores(nc, cst["semaphores"])
            with ExitStack() as c:
                weights = (sb("l1_w1", [P, E, DT, DFF], F32, c), sb("l1_b1", [P, E, FT], F32, c),
                           sb("l1_w2", [P, E, FT, D], F32, c), sb("l1_b2", [P, E, D], F32, c))

                def load_weights(sp):
                    load_experts(sp, t["l1_w1"], t["l1_b1"], t["l1_w2"], t["l1_b2"], *weights, s_weights)

                gates = sb("l1_gates", [P, NT, 2, E], F32, c)
                top = sb("l1_top", [P, NT], F32, c)
                sums = sb("l1_sums", [P, NT], F32, c)
                slots = sb("l1_slots", [P, 2 * NT], U32, c)
                tile_expert = sb("l1_tile_expert", [1, EXPERT_TILES], I32, c)
                s_weights, s_scatter = (nc.alloc_semaphore(n) for n in ("l1_weights", "l1_scatter"))
                route(nc, "l1r", x_fm, t["l1_gate_w"], t["l1_gate_b"], E, gates, top, sums, None, cst,
                      load_weights)
                place_tokens(nc, "l1p", x_tok, gates, slots, tile_expert, x_slots, s_zero, s_scatter, cst)
                expert_ffn(nc, "l1f", x_tok, top, slots, tile_expert, x_slots, y_slots, weights, s_weights,
                           s_scatter, out, cst)
            return

        with ExitStack() as c:
            s_out = c.enter_context(nc.semaphore("store_out"))
            block = c.enter_context(nc.Block())

            @block.sync
            def _(sp):
                sp.dma_start(out.rearrange("(t p) n -> p t n", p=P), x_tok[:, :, :]).then_inc(s_out, 16)
                sp.wait_ge(s_out, 16)
                sp.wait_ge(s_zero, 16)


def _layout(inputs):
    import numpy as np
    a = {k: np.asarray(v) for k, v in inputs.items()}
    x, ctx = a["x"][0], a["ctx_1024"][0]
    o = {"x": x, "x_fm": x.T, "ctx_fm": ctx.T, "mask": a["mask_Bx1xS2_bf1"].reshape(1, CTX).view(np.uint8)}

    def columns(b):
        return b.reshape(-1, P).T

    def row(b):
        return b.reshape(1, -1)

    def block(name, q, k, v, out, bq, bk, bv, bo):
        o[f"{name}_w"] = np.stack([q, k, v])
        o[f"{name}_bqk"] = np.stack([columns(bq), columns(bk)])
        o[f"{name}_bv"], o[f"{name}_wo"], o[f"{name}_bo"] = row(bv), out, row(bo)

    p = "L0_attn_"
    block("a0", *(a[p + n] for n in ("Wq", "Wk", "Wv", "Wo", "bq", "bk", "bv", "bo")))
    o["gamma"], o["beta"] = row(a[p + "gamma"]), row(a[p + "beta"])
    o["f0_w1"], o["f0_b1"], o["f0_w2"], o["f0_b2"] = a[p + "W1"], columns(a[p + "b1"]), a[p + "W2"], row(a[p + "b2"])
    p = "L0_xattn_"
    block("x0", *(a[p + n].T for n in ("Wq", "Wk", "Wv", "Wo")), *(a[p + n] for n in ("bq", "bk", "bv", "bo")))
    p = "L0_ffn_"
    o["l0_wi"], o["l0_bi"], o["l0_wo"], o["l0_bo"] = a[p + "wi"].T, columns(a[p + "bi"]), a[p + "wo"].T, row(a[p + "bo"])
    o["l0_gate_w"] = np.concatenate([a[p + "lora_A"].reshape(E * R, D).T, a[p + "gate_w"].T], axis=1)
    o["l0_gate_b"] = row(a[p + "gate_b"])
    o["l0_lora_b"] = a[p + "lora_B"].transpose(0, 2, 1).reshape(E * R, DFF)
    p = "L1_attn_"
    w = a[p + "qkv_w"].reshape(NSH, 3, SH, D).transpose(1, 3, 0, 2).reshape(3, D, D)
    b = a[p + "qkv_b"].reshape(NSH, 3, SH).transpose(1, 0, 2).reshape(3, D)
    block("a1", w[0], w[1], w[2], a[p + "fc_w"].T, b[0], b[1], b[2], a[p + "fc_b"])
    p = "L1_xattn_"
    block("x1", *(a[p + n] for n in ("Wq", "Wk", "Wv", "Wo", "bq", "bk", "bv", "bo")))
    p = "L1_ffn_"
    o["l1_gate_w"], o["l1_gate_b"], o["l1_w1"], o["l1_w2"] = a[p + "gate_w"], row(a[p + "gate_b"]), a[p + "w1"], a[p + "w2"]
    o["l1_b1"], o["l1_b2"] = a[p + "b1"].reshape(E, FT, P).transpose(2, 0, 1), a[p + "b2"]
    return o


def kernel(**inputs):
    import numpy as np
    import concourse.bacc as bacc
    from concourse.bass_utils import run_bass_kernel_spmd

    nc = bacc.Bacc("TRN2", target_bir_lowering=False, num_devices=1)
    arrays, t = {}, {}
    for name, a in _layout(inputs).items():
        a = np.ascontiguousarray(a)
        arrays[f"in_{name}"] = a
        t[name] = nc.dram_tensor(f"in_{name}", a.shape, mybir.dt.from_np(a.dtype), kind="ExternalInput").ap()
    out = nc.dram_tensor("out", (S, D), F32, kind="ExternalOutput").ap()
    decoder_kernel(nc, t, out)
    r = run_bass_kernel_spmd(nc, [arrays], core_ids=[0])
    return r.results[0]["out"].reshape(1, S, D)
```

```python
import concourse.bass as bass
from concourse import mybir
from contextlib import ExitStack
from functools import partial

F32 = mybir.dt.float32
BF16 = mybir.dt.bfloat16
U8 = mybir.dt.uint8
U32 = mybir.dt.uint32
I32 = mybir.dt.int32
ALU = mybir.AluOpType
ACT = mybir.ActivationFunctionType
AX = mybir.AxisListType

P = 128
S = 2048
D = 256
DT = D // P
NT = S // P
CTX = 1601
CT = -(-CTX // P)
CTXP = CT * P
SH = 16
NSH = D // SH
GH = 4
NG = NSH // GH
QC = 512
NQ = S // QC
QT = QC // P
DFF = 1024
FT = DFF // P
E = 8
R = 16
EXPERT_TILES = 2 * NT + E - 1
NEG = -1.0e30
EPS = 1e-5
Q_PARTS = (0, 0, 1, 0, 2, 1)
K_PARTS = (0, 1, 0, 2, 0, 1)
ROWS_SPLIT = SH * len(Q_PARTS)
ROW_MASK, ROW_MAX = ROWS_SPLIT, ROWS_SPLIT + 1
BAND = 64


class Attention:

    def __init__(self, kind, keys, head_dim):
        self.kind, self.keys, self.head_dim = kind, keys, head_dim
        self.tiles = keys // P
        self.halves = head_dim // SH
        self.heads = GH // self.halves
        self.units = self.heads // 2
        self.pairs = [len(self.key_tiles(c)) for c in range(NQ)]
        self.pairs_group = sum(self.pairs)
        self.jobs = [self.heads * QT * len(self.max_chunks(QT * c)) for c in range(NQ)]
        self.jobs_group = sum(self.jobs)

    def key_tiles(self, c):
        if self.kind == "band":
            return [-1, 0, 1]
        if self.kind == "causal":
            return list(range(min(self.tiles, QT * (c + 1))))
        return list(range(self.tiles))

    def max_chunks(self, t):
        if self.kind == "band":
            lo, hi = max(t - 1, 0), min(t + 2, NT)
            return [(lo * P, (hi - lo) * P)]
        end = min(self.keys, (t + 1) * P) if self.kind == "causal" else self.keys
        return [(k, min(QC, end - k)) for k in range(0, end, QC)]


def clear_semaphores(nc, held):
    nc.clear_and_free_semaphores(held)
    held.clear()
    nc.all_engine_barrier()


def constants(sb):
    c = {"semaphores": []}
    c["ident"] = sb("ident", [P, P], F32)
    c["ident_bf"] = sb("ident_bf", [P, P], BF16)
    c["eps"] = sb("eps", [P, 1], F32)
    c["zeros"] = sb("zeros", [P, D], F32)
    c["causal_k"] = sb("causal_k", [P, 2 * QC], BF16)
    c["causal_q"] = sb("causal_q", [P, QC], BF16)
    c["band_k"] = sb("band_k", [P, 5, P], BF16)
    c["band_q"] = sb("band_q", [P, 3 * P], BF16)
    return c


def prepare(nc, t, c, x_tok, x_fm, masks, q_st, k_st, v_grp):
    with ExitStack() as ctx:
        user = ctx.enter_context(nc.sbuf_tensor("user_mask", [1, CTX], U8))
        rows = ctx.enter_context(nc.sbuf_tensor("mask_rows", [1, 3, S], BF16))
        ones = ctx.enter_context(nc.sbuf_tensor("ones_bf", [P, P], BF16))
        done, s_x, s_user, s_rows, s_store, s_ones, s_ones_set, s_zeros = (
            ctx.enter_context(nc.semaphore(n)) for n in ("const_done", "load_x", "load_mask", "mask_rows",
                                                         "store_masks", "ones", "ones_set", "zeros"))
        block = ctx.enter_context(nc.Block())

        @block.sync
        def _(sp):
            sp.dma_start(user[:, :], t["mask"]).then_inc(s_user, 16)
            sp.dma_start(x_fm[:, :, :], t["x_fm"].rearrange("(t p) n -> p t n", p=P)).then_inc(s_x, 16)
            sp.wait_ge(s_ones, 1)
            sp.dma_start(q_st[ROW_MASK:ROW_MASK + 1, :, :, :], ones[:, :]).then_inc(s_ones_set, 16)
            sp.dma_start(k_st[ROW_MAX:ROW_MAX + 1, :, :, :], ones[:, :]).then_inc(s_ones_set, 16)
            sp.dma_start(x_tok[:, :, :], t["x"].rearrange("(t p) n -> p t n", p=P)).then_inc(s_x, 16)
            sp.wait_ge(s_rows, 5)
            sp.dma_start(masks.rearrange("(o r) n -> o r n", o=1), rows[:, :, :]).then_inc(s_store, 16)
            sp.wait_ge(s_store, 16)
            sp.wait_ge(s_ones_set, 32)
            sp.wait_ge(s_x, 32)

        @block.vector
        def _(dve):
            dve.memset(ones[:, :], 1.0).then_inc(s_ones, 1)
            dve.memset(c["zeros"][:, :], 0.0).then_inc(s_zeros, 1)
            dve.memset(rows[:, 0, :], 0.0).then_inc(s_rows, 1)
            dve.memset(rows[:, 1, 0:CTX], 0.0).then_inc(s_rows, 1)
            dve.memset(rows[:, 1, CTX:S], NEG).then_inc(s_rows, 1)
            dve.memset(rows[:, 2, CTX:S], NEG).then_inc(s_rows, 1)
            dve.wait_ge(s_user, 16)
            dve.tensor_scalar(rows[:, 2, 0:CTX], user[:, :], 1.0, -NEG, ALU.subtract,
                              ALU.mult).then_inc(s_rows, 1)

        @block.gpsimd
        def _(pool):
            n = 0

            def fill(dst, value):
                nonlocal n
                pool.memset(dst, value).then_inc(done, 1)
                n += 1
                pool.wait_ge(done, n)

            def select(dst, op, fill_value, base, pattern, mult):
                nonlocal n
                pool.affine_select(out=dst, in_=dst, compare_op=op, fill=fill_value, base=base, pattern=pattern,
                                   channel_multiplier=mult).then_inc(done, 1)
                n += 1
                pool.wait_ge(done, n)

            fill(v_grp[:, :, :, :], 1.0)
            for eye in (c["ident"], c["ident_bf"]):
                fill(eye[:, :], 0.0)
                select(eye[:, :], ALU.not_equal, 1.0, 0, [[-1, P]], 1)
            fill(c["eps"][:, :], EPS)
            off = QC - P
            fill(c["causal_k"][:, :], 0.0)
            select(c["causal_k"][:, :], ALU.is_ge, NEG, -off, [[1, 2 * QC]], -1)
            fill(c["causal_q"][:, :], 0.0)
            select(c["causal_q"][:, :], ALU.is_ge, NEG, off, [[-1, QC]], 1)
            fill(c["band_k"][:, :, :], 0.0)
            fill(c["band_k"][:, 3, :], NEG)
            for i, r in enumerate((-1, 0, 1)):
                select(c["band_k"][:, i, :], ALU.is_ge, NEG, BAND - P * r, [[1, P]], -1)
                select(c["band_k"][:, i, :], ALU.is_ge, NEG, BAND + P * r, [[-1, P]], 1)
            fill(c["band_q"][:, :], 0.0)
            select(c["band_q"][:, :], ALU.is_ge, NEG, BAND - P, [[1, 3 * P]], -1)
            select(c["band_q"][:, :], ALU.is_ge, NEG, BAND + P, [[-1, 3 * P]], 1)


class RowNorm:

    def __init__(self, nc, name, sb, pb, sem, x_tok, x_fm, cst, gain=None):
        self.x_tok, self.x_fm, self.cst, self.gain = x_tok, x_fm, cst, gain
        self.stat = sb("rn_stat", [P, NT, 6], F32)
        self.mean_var = sb("rn_mean_var", [P, NT, 2], F32)
        self.std = sb("rn_std", [P, NT], F32)
        self.inv = sb("rn_inv", [P, NT], F32)
        self.ps = [pb(f"rn_ps{i}", [P, QC], F32) for i in range(2)] if x_fm is not None else None
        self.s_stat, self.s_mv, self.s_std, self.s_inv, self.s_x, self.s_turn, self.s_fm = map(
            sem, ("rn_stat", "rn_mv", "rn_std", "rn_inv", "rn_x", "rn_turn", "rn_fm"))
        self.per_tile = 3 if gain is not None else 1

    def statistics(self, dve, t):
        dve.bn_stats(self.stat[:, t, :], self.x_tok[:, t, :]).then_inc(self.s_stat, 1)
        dve.wait_ge(self.s_stat, t + 1)
        dve.bn_aggr(self.mean_var[:, t, :], self.stat[:, t, :]).then_inc(self.s_mv, 1)

    def root(self, act, quad):
        q = slice(quad * 4, quad * 4 + 4)
        act.wait_ge(self.s_mv, 4 * (quad + 1))
        act.activation(self.std[:, q], self.mean_var[:, q, 1], ACT.Sqrt,
                       bias=self.cst["eps"][:, 0:1]).then_inc(self.s_std, 1)

    def scale(self, dve, quad):
        q = slice(quad * 4, quad * 4 + 4)
        dve.wait_ge(self.s_std, quad + 1)
        dve.reciprocal(self.inv[:, q], self.std[:, q]).then_inc(self.s_inv, 1)
        dve.wait_ge(self.s_inv, quad + 1)
        for t in range(quad * 4, quad * 4 + 4):
            x = self.x_tok[:, t, :]
            dve.tensor_scalar(x, x, self.mean_var[:, t, 0:1], self.inv[:, t:t + 1], ALU.subtract,
                              ALU.mult).then_inc(self.s_x, 1)
            if self.gain is not None:
                dve.wait_ge(self.s_x, 3 * t + 1)
                dve.tensor_tensor(x, x, self.gain[:, 0, :], ALU.mult).then_inc(self.s_x, 1)
                dve.wait_ge(self.s_x, 3 * t + 2)
                dve.tensor_tensor(x, x, self.gain[:, 1, :], ALU.add).then_inc(self.s_x, 1)

    def turn(self, pe, t):
        pe.wait_ge(self.s_x, self.per_tile * (t + 1))
        if t >= 2:
            pe.wait_ge(self.s_fm, t - 1)
        for m in range(DT):
            mm = pe.transpose(self.ps[t % 2][:, m * P:(m + 1) * P], self.x_tok[:, t, m * P:(m + 1) * P],
                              self.cst["ident"][:, :])
        mm.then_inc(self.s_turn, 1)

    def copy_out(self, act, t):
        act.wait_ge(self.s_turn, t + 1)
        act.activation(self.x_fm[:, :, t * P:(t + 1) * P],
                       self.ps[t % 2][:, 0:DT * P].rearrange("p (a b) -> p a b", a=DT),
                       ACT.Copy).then_inc(self.s_fm, 1)


def load_stacks(sp, at, g, slot, q_st, k_st, parts_q, parts_k, s_load):
    for n, (qp, kp) in enumerate(zip(Q_PARTS, K_PARTS)):
        rows = slice(n * SH, (n + 1) * SH)
        for st, parts, part, length in ((q_st, parts_q, qp, S), (k_st, parts_k, kp, at.keys)):
            src = parts[part, bass.ds(g * GH * SH, GH * SH), 0:length]
            sp.dma_start(st[rows, bass.ds(slot, 1), :, 0:length],
                         src.rearrange("(o j d) n -> d o j n", d=SH, o=1)).then_inc(s_load, 16)


LOADS = 2 * len(Q_PARTS)


def project(nc, at, name, x_fm, kv_fm, kv_source, w, bias, v_bias, v_tok, parts_q, parts_k, stacks, maxima, s_load,
            mask, cst):
    q_st, k_st = stacks
    units = [(side, m, k, min(QC, n - k)) for m in range(DT) for side, n in ((0, S), (1, at.keys))
             for k in range(0, n, QC)]
    first = len(units) // DT
    NB, NS = 4, 6
    ahead = MaxStream.windows(at)[0]
    PER_UNIT = 4

    def entries_after(u):
        if u < first:
            return range(0)
        done = (u - first) * PER_UNIT
        return range(min(done, len(ahead.entries)), min(done + PER_UNIT, len(ahead.entries)))

    with ExitStack() as ctx:
        def sb(n, shape, dt):
            return ctx.enter_context(nc.sbuf_tensor(f"{name}_{n}", shape, dt))

        def sem(n):
            cst["semaphores"].append(nc.alloc_semaphore(f"{name}_{n}"))
            return cst["semaphores"][-1]

        w_sb = sb("w", [P, 3, DT, D], F32)
        bias_sb = sb("bias", [P, 2, DT], F32)
        vb_sb = sb("vb", [P, D], F32)
        exact = sb("exact", [P, 2, QC], F32)
        rest = sb("rest", [P, 2, QC], F32)
        parts = sb("parts", [P, NS, 3, QC], BF16)
        ps = [ctx.enter_context(nc.psum_tensor(f"{name}_ps{i}", [P, QC], F32)) for i in range(NB)]
        ps_m = [ctx.enter_context(nc.psum_tensor(f"{name}_psm{i}", [P, QC], F32)) for i in range(2)]
        ps_v = ps_m + [ctx.enter_context(nc.psum_tensor(f"{name}_psv{i}", [P, QC], F32)) for i in range(2)]
        s_product, s_read = sem("product"), sem("read")
        s_w, s_mm, s_exact, s_high, s_rest, s_mid, s_low = map(
            sem, ("w", "mm", "exact", "high", "rest", "mid", "low"))
        s_vmm, s_vout, s_mask = sem("vmm"), sem("vout"), sem("mask")
        s_store = [sem(f"store{i}") for i in range(NS)]
        s_wk, s_wv, s_kv, s_pad = sem("wk"), sem("wv"), sem("kv"), sem("pad")
        block = ctx.enter_context(nc.Block())

        @block.sync
        def _(sp):
            sp.dma_start(w_sb[:, 0, :, :], w[0].rearrange("(t p) n -> p t n", p=P)).then_inc(s_w, 16)
            sp.dma_start(bias_sb[:, :, :], bias.rearrange("s p t -> p s t")).then_inc(s_w, 16)
            sp.dma_start(w_sb[:, 1, :, :], w[1].rearrange("(t p) n -> p t n", p=P)).then_inc(s_wk, 16)
            if kv_source is not None:
                sp.dma_start(kv_fm[:, :, 0:CTX], kv_source.rearrange("(t p) n -> p t n", p=P)).then_inc(s_kv, 16)
            sp.dma_start(w_sb[:, 2, :, :], w[2].rearrange("(t p) n -> p t n", p=P)).then_inc(s_wv, 16)
            sp.dma_start(vb_sb[:, :], v_bias.to_broadcast((P, D))).then_inc(s_wv, 16)
            for slot in range(2):
                for j in range(GH):
                    sp.dma_start(k_st[ROW_MASK:ROW_MASK + 1, slot, j, 0:at.keys],
                                 mask[:, 0:at.keys]).then_inc(s_mask, 16)
            for u, (side, m, k, n) in enumerate(units):
                sp.wait_ge(s_low, u + 1)
                sp.wait_ge(s_mid, u + 1)
                sp.wait_ge(s_high, u + 1)
                dst = (parts_q, parts_k)[side]
                sp.dma_start(dst[:, m * P:(m + 1) * P, k:k + n].rearrange("s p n -> p s n"),
                             parts[:, u % NS, :, 0:n]).then_inc(s_store[u % NS], 16)
                if u == first - 1:
                    for i in range(NS):
                        sp.wait_ge(s_store[i], 16 * len(range(i, u + 1, NS)))
                    load_stacks(sp, at, 0, 0, q_st, k_st, parts_q, parts_k, s_load)
            for (_, c), x in ahead.turn_at.items():
                maxima.send(sp, 0, c, s_read, x + 1)
            for i in range(NS):
                sp.wait_ge(s_store[i], 16 * len(range(i, len(units), NS)))
            sp.wait_ge(s_mask, 16 * 2 * GH)

        @block.tensor
        def _(pe):
            def entries(some):
                for x in some:
                    if x == 0:
                        pe.wait_ge(s_load, 16 * LOADS)
                        pe.wait_ge(s_mask, 16 * 2 * GH)
                        pe.wait_ge(s_vout, at.tiles)
                    if x >= 2:
                        pe.wait_ge(s_read, x - 1)
                    maxima.product(pe, 0, ahead.entries[x], ps_m[x % 2], s_product)

            def v_tiles():
                for i in range(at.tiles):
                    if i >= 4:
                        pe.wait_ge(s_vout, i - 3)
                    for t in range(DT):
                        mm = pe.matmul(ps_v[i % 4][:, 0:D], kv_fm[:, t, i * P:(i + 1) * P], w_sb[:, 2, t, :],
                                       start=(t == 0), stop=(t == DT - 1))
                    mm.then_inc(s_vmm, 1)

            pe.wait_ge(s_w, 32)
            for u, (side, m, k, n) in enumerate(units):
                if u == S // QC:
                    pe.wait_ge(s_wk, 16)
                    if kv_source is not None:
                        pe.wait_ge(s_kv, 16)
                        pe.wait_ge(s_pad, 1)
                if u == first:
                    pe.wait_ge(s_wv, 32)
                    v_tiles()
                src = (x_fm, kv_fm)[side]
                if u >= NB:
                    pe.wait_ge(s_high, u - NB + 1)
                for t in range(DT):
                    mm = pe.matmul(ps[u % NB][:, 0:n], w_sb[:, side, t, m * P:(m + 1) * P], src[:, t, k:k + n],
                                   start=(t == 0), stop=(t == DT - 1))
                mm.then_inc(s_mm, 1)
                entries(entries_after(u))
            entries(range(entries_after(len(units) - 1).stop, len(ahead.entries)))

        @block.scalar
        def _(act):
            act.wait_ge(s_w, 32)
            for u, (side, m, k, n) in enumerate(units):
                act.wait_ge(s_mm, u + 1)
                if u >= 2:
                    act.wait_ge(s_rest, u - 1)
                act.activation(exact[:, u % 2, 0:n], ps[u % NB][:, 0:n], ACT.Identity,
                               bias=bias_sb[:, side, m:m + 1]).then_inc(s_exact, 1)
                if u >= NS:
                    act.wait_ge(s_store[u % NS], 16 * (u // NS))
                act.activation(parts[:, u % NS, 0, 0:n], ps[u % NB][:, 0:n], ACT.Identity,
                               bias=bias_sb[:, side, m:m + 1]).then_inc(s_high, 1)

        @block.gpsimd
        def _(pool):
            if kv_source is not None:
                pool.memset(kv_fm[:, :, CTX:CTXP], 0.0).then_inc(s_pad, 1)
                pool.wait_ge(s_pad, 1)
            for u, (side, m, k, n) in enumerate(units):
                pool.wait_ge(s_rest, u + 1)
                if u >= NS:
                    pool.wait_ge(s_store[u % NS], 16 * (u // NS))
                pool.tensor_copy(parts[:, u % NS, 1, 0:n], rest[:, u % 2, 0:n]).then_inc(s_mid, 1)

        @block.vector
        def _(dve):
            def low(u):
                n = units[u][3]
                dve.wait_ge(s_mid, u + 1)
                if u >= NS:
                    dve.wait_ge(s_store[u % NS], 16 * (u // NS))
                dve.tensor_tensor(parts[:, u % NS, 2, 0:n], rest[:, u % 2, 0:n], parts[:, u % NS, 1, 0:n],
                                  ALU.subtract).then_inc(s_low, 1)

            def entries(some):
                for x in some:
                    dve.wait_ge(s_product, x + 1)
                    maxima.reduce(dve, 0, ahead.entries[x], ps_m[x % 2], s_read, x + 1)

            def v_tiles():
                for i in range(at.tiles):
                    dve.wait_ge(s_vmm, i + 1)
                    dve.tensor_tensor(v_tok[:, i, :], ps_v[i % 4][:, 0:D], vb_sb[:, :],
                                      ALU.add).then_inc(s_vout, 1)

            for u, (side, m, k, n) in enumerate(units):
                if u == first:
                    low(u - 1)
                    dve.wait_ge(s_wv, 32)
                    v_tiles()
                entries(entries_after(u))
                dve.wait_ge(s_exact, u + 1)
                dve.wait_ge(s_high, u + 1)
                if u >= 2:
                    dve.wait_ge(s_low, u - 1)
                dve.tensor_tensor(rest[:, u % 2, 0:n], exact[:, u % 2, 0:n], parts[:, u % NS, 0, 0:n],
                                  ALU.subtract).then_inc(s_rest, 1)
                if u >= 1 and u != first:
                    low(u - 1)
            low(len(units) - 1)
            entries(range(entries_after(len(units) - 1).stop, len(ahead.entries)))


class MaxStream:
    AHEAD = {"full": 84, "causal": 64, "band": 16}

    @staticmethod
    def sequence(at, groups):
        out, waiting = [], []
        for dg in range(groups):
            for c in range(NQ):
                jobs = [(h, a, i, k, n) for h in range(at.heads) for a in range(QT)
                        for i, (k, n) in enumerate(at.max_chunks(QT * c + a))]
                for job in jobs:
                    out.append(("max", dg, c) + job + (job is jobs[-1],))
                    waiting = [(w, due - 1) for w, due in waiting]
                    if waiting and waiting[0][1] <= 0:
                        out.append(waiting.pop(0)[0])
                waiting.append((("turn", dg, c), 4))
        return out + [w for w, _ in waiting]

    @classmethod
    def windows(cls, at):
        one, two = cls.sequence(at, 1), cls.sequence(at, 2)
        ahead = cls.AHEAD[at.kind]
        return cls(one[:ahead]), cls(two[ahead:ahead + len(one)]), cls(one[ahead:])

    def __init__(self, entries):
        self.entries = entries
        self.turn_at = {e[1:3]: x for x, e in enumerate(entries) if e[0] == "turn"}

    def spread(self, at):
        starts = {(0, c): sum(at.pairs[:c]) for c in range(NQ)}
        starts[(1, 0)] = at.pairs_group
        due = [(max(starts[step] - 1.5, 1), x + 1) for step, x in self.turn_at.items() if step in starts]
        due.append((at.pairs_group, len(self.entries)))
        knots = [(0, 0)]
        while knots[-1][0] < at.pairs_group:
            k0, n0 = knots[-1]
            left = [(k, n) for k, n in due if k > k0]
            knots.append(max(left, key=lambda d: ((d[1] - n0) / (d[0] - k0), d[0])))

        def issued(k):
            for (k0, n0), (k1, n1) in zip(knots, knots[1:]):
                if k <= k1:
                    return min(len(self.entries), round(n0 + (n1 - n0) * (k - k0) / (k1 - k0)))

        self.places, done = [], 0
        for k in range(at.pairs_group):
            row = []
            for m in (0.25, 0.5, 0.75, 1.0):
                upto = max(done, issued(k + m))
                row.append(range(done, upto))
                done = upto
            self.places.append(row)


class Maxima:

    def __init__(self, nc, at, name, sb, stacks, cst):
        self.at, self.cst = at, cst
        self.q_st, self.k_st = stacks
        self.columns = at.heads * QT
        self.part = sb(f"{name}_part_max", [P, self.columns, 4], F32)
        self.neg = sb(f"{name}_neg_max", [P, self.columns], BF16)
        self.row = sb(f"{name}_neg_row", [self.columns, P], BF16)
        self.s_found = nc.alloc_semaphore(f"{name}_neg")
        self.s_sent = nc.alloc_semaphore(f"{name}_negd")
        cst["semaphores"] += [self.s_found, self.s_sent]

    def product(self, pe, g, entry, bank, s_product):
        at, q_st, k_st, cst = self.at, self.q_st, self.k_st, self.cst
        dg, c = entry[1:3]
        if entry[0] == "turn":
            pe.wait_ge(self.s_found, (g + dg) * NQ + c + 1)
            pe.transpose(bank[:, :].bitcast(BF16)[0:self.columns, 0:P], self.neg[:, :],
                         cst["ident_bf"][:, :]).then_inc(s_product, 1)
            return
        h, a, i, k, w, last = entry[3:]
        t, slot = QT * c + a, (g + dg) % 2
        out = bank[:, 0:w]
        masked = at.kind == "band" or (at.kind == "causal" and k + w == (t + 1) * P)
        for half in range(at.halves):
            rows = ROW_MASK + 1 if half == 0 else ROWS_SPLIT
            j = at.halves * h + half
            mm = pe.matmul(out, q_st[0:rows, slot, j, t * P:(t + 1) * P], k_st[0:rows, slot, j, k:k + w],
                           start=(half == 0), stop=(half == at.halves - 1 and not masked))
        if masked:
            if at.kind == "band":
                m = cst["band_q"][:, k - (t - 1) * P:k - (t - 1) * P + w]
            else:
                m = cst["causal_q"][:, QC - w:QC]
            mm = pe.matmul(out, cst["ident_bf"][:, :], m, start=False, stop=True)
        mm.then_inc(s_product, 1)

    def reduce(self, dve, g, entry, bank, s_read, count):
        dg, c = entry[1:3]
        n = (g + dg) * NQ + c
        if entry[0] == "turn":
            if not (type(n) is int and n == 0):
                dve.wait_ge(self.s_sent, 16 * self.at.heads * n)
            dve.tensor_copy(self.row[:, :], bank[:, :].bitcast(BF16)[0:self.columns, 0:P]).then_inc(s_read, 1)
            return
        h, a, i, k, w, last = entry[3:]
        dve.tensor_reduce(self.part[:, h * QT + a, i:i + 1], bank[:, 0:w], AX.X, ALU.max).then_inc(s_read, 1)
        if last:
            dve.wait_ge(s_read, count)
            dve.tensor_reduce(self.neg[:, :], self.part[:, :, 0:len(self.at.max_chunks(QT * c))], AX.X, ALU.max,
                              negate=True).then_inc(self.s_found, 1)
            dve.wait_ge(self.s_found, n + 1)

    def send(self, sp, slot, c, s_read, count):
        sp.wait_ge(s_read, count)
        for h in range(self.at.heads):
            sp.dma_start(self.q_st[ROW_MAX:ROW_MAX + 1, bass.ds(slot, 1), self.at.halves * h,
                                   c * QC:(c + 1) * QC],
                         self.row[h * QT:(h + 1) * QT, :]).then_inc(self.s_sent, 16)


def attend(nc, at, name, v_tok, parts_q, parts_k, o_tok, stacks, maxima, s_load, closing, cst, behind):
    scale = float(at.head_dim) ** -0.5
    HEADS, UNITS, HALVES = at.heads, at.units, at.halves
    q_st, k_st, v_grp = stacks
    _, body, end = MaxStream.windows(at)
    total = len(body.entries)
    V_FIRST = 6 if at.kind == "band" else 2
    body.spread(at)
    end.spread(at)
    with ExitStack() as ctx:
        def sb(n, shape, dt):
            return ctx.enter_context(nc.sbuf_tensor(f"{name}_{n}", shape, dt))

        def pb(n, shape, dt):
            return ctx.enter_context(nc.psum_tensor(f"{name}_{n}", shape, dt))

        def sem(n):
            cst["semaphores"].append(nc.alloc_semaphore(f"{name}_{n}"))
            return cst["semaphores"][-1]

        inv_den = sb("inv_den", [P, QT, GH, 1], F32)
        o_raw = sb("o_raw", [P, QC], F32)
        prob = sb("prob", [P, 2, HEADS, QC], F32)
        ps_s = [pb(f"ps_s{i}", [P, 2, QC], F32) for i in range(2)]
        ps_m = [pb(f"ps_m{i}", [P, QC], F32) for i in range(2)]
        ps_o = pb("ps_o", [P, QC], F32)
        ps_x = pb("ps_x", [P, QC], F32)
        s_scores = sem("scores")
        s_prob = sem("prob")
        s_pv = sem("pv")
        s_vgrp = sem("vgrp")
        s_msc = sem("msc")
        s_mred = sem("mred")
        s_ocopy = sem("ocopy")
        s_turn = sem("turn")
        s_inv = sem("inv")
        s_norm = sem("norm")
        block = ctx.enter_context(nc.Block())

        def pairs_before(g, c):
            return g * at.pairs_group + sum(at.pairs[:c])

        def entries_before(g):
            return g * total

        def slot(g):
            return g % 2

        @block.sync
        def _(sp):
            def group(g, stream, last):
                if not last:
                    sp.wait_ge(s_load, 16 * LOADS * (g + 1))
                    sp.wait_ge(s_pv, 2 + pairs_before(g, 0))
                    load_stacks(sp, at, g + 1, slot(g + 1), q_st, k_st, parts_q, parts_k, s_load)
                for (dg, c), x in stream.turn_at.items():
                    maxima.send(sp, slot(g + dg), c, s_mred, 2 + entries_before(g) + x + 1)

            load_closing(sp, *closing)
            with sp.Fori(0, NG - 1) as g:
                group(g, body, False)
            group(NG - 1, end, True)
            behind(sp)

        @block.gpsimd
        def _(pool):
            pool.sem_inc(s_prob, 2)
            pool.sem_inc(s_pv, 2)
            pool.sem_inc(s_mred, 2)
            pool.sem_inc(s_ocopy, 1)
            pool.sem_inc(s_norm, 1)
            pool.sem_inc(s_turn, 1)

            def group(g):
                pool.wait_ge(s_pv, 2 + pairs_before(g, 0))
                for some in (slice(0, V_FIRST), slice(V_FIRST, at.tiles)):
                    pool.tensor_copy(v_grp[:, some, :, 0:SH],
                                     v_tok[:, some, bass.ds(g * GH * SH, GH * SH)]
                                     .rearrange("p t (j d) -> p t j d", d=SH)).then_inc(s_vgrp, 1)

            with pool.Fori(0, NG - 1) as g:
                group(g)
            group(NG - 1)

        @block.tensor
        def _(pe):
            def scores(g, c, k, kt, u, un, between):
                bank = ps_s[k % 2 if UNITS == 1 else u]
                pe.wait_ge(s_prob, un + 1)
                for hh in range(2):
                    h = 2 * u + hh
                    if at.kind == "band":
                        for a in range(QT):
                            t = QT * c + a
                            inside = 0 <= t + kt < NT
                            key = (t + kt if inside else t) * P
                            qs = slice(c * QC + a * P, c * QC + (a + 1) * P)
                            out = bank[:, hh, a * P:(a + 1) * P]
                            for half in range(HALVES):
                                rows = ROW_MAX + 1 if half == 0 else ROWS_SPLIT
                                j = HALVES * h + half
                                pe.matmul(out, k_st[0:rows, bass.ds(slot(g), 1), j, key:key + P],
                                          q_st[0:rows, bass.ds(slot(g), 1), j, qs],
                                          start=(half == 0), stop=False)
                            mm = pe.matmul(out, cst["ident_bf"][:, :],
                                           cst["band_k"][:, kt + 1 if inside else 3, :],
                                           start=False, stop=True)
                    else:
                        diag = at.kind == "causal" and kt >= QT * c
                        mm = pe.matmul(bank[:, hh, :],
                                       k_st[0:ROW_MAX + 1, bass.ds(slot(g), 1), h, kt * P:(kt + 1) * P],
                                       q_st[0:ROW_MAX + 1, bass.ds(slot(g), 1), h, c * QC:(c + 1) * QC],
                                       start=True, stop=not diag)
                        if diag:
                            off = QC - P - P * (kt - QT * c)
                            mm = pe.matmul(bank[:, hh, :], cst["ident_bf"][:, :],
                                           cst["causal_k"][:, off:off + QC], start=False, stop=True)
                    if hh == 0:
                        between()
                mm.then_inc(s_scores, 1)

            def times_v(g, c, i, k, kt, between):
                if i == 0:
                    pe.wait_ge(s_ocopy, g * NQ + c + 1)
                    if c == 0:
                        pe.wait_ge(s_vgrp, 2 * g + 1)
                if c == (1 if at.kind == "band" else 0) and i == (0 if at.kind == "band" else V_FIRST):
                    pe.wait_ge(s_vgrp, 2 * g + 2)
                pe.wait_ge(s_prob, 2 + UNITS * (pairs_before(g, 0) + k + 1))
                n = at.pairs[c]
                if at.kind == "band":
                    for a in range(QT):
                        t = QT * c + a
                        key = t + kt if 0 <= t + kt < NT else t
                        for j in range(GH):
                            mm = pe.matmul(ps_o[32 * j:32 * j + 32, a * P:(a + 1) * P], v_grp[:, key, j, :],
                                           prob[:, k % 2, j // HALVES, a * P:(a + 1) * P],
                                           start=(i == 0 and a == 0), stop=(i == n - 1),
                                           skip_group_check=True)
                        if a == QT // 2 - 1:
                            between()
                else:
                    for half in range(2):
                        qs = slice(half * QC // 2, (half + 1) * QC // 2)
                        for j in range(GH):
                            mm = pe.matmul(ps_o[32 * j:32 * j + 32, qs], v_grp[:, kt, j, :],
                                           prob[:, k % 2, j, qs], start=(i == 0 and half == 0),
                                           stop=(i == n - 1), skip_group_check=True)
                        if half == 0:
                            between()
                mm.then_inc(s_pv, 1)

            def turn_out(n):
                pe.wait_ge(s_ocopy, n + 2)
                pe.wait_ge(s_norm, n + 1)
                for a in range(QT):
                    mm = pe.transpose(ps_x[:, a * P:(a + 1) * P], o_raw[:, a * P:(a + 1) * P],
                                      cst["ident"][:, :])
                mm.then_inc(s_turn, 1)

            def group(g, stream, before):
                k = 0
                for c in range(NQ):
                    n = g * NQ + c
                    pe.wait_ge(maxima.s_sent, 16 * HEADS * (n + 1))
                    for i, kt in enumerate(at.key_tiles(c)):
                        places = [partial(entries, g, stream, place) for place in stream.places[k]]
                        for u in range(UNITS):
                            scores(g, c, k, kt, u, UNITS * (pairs_before(g, 0) + k) + u, places[u])
                        if UNITS == 1:
                            places[1]()
                        if before is not None:
                            times_v(*before, places[2])
                        else:
                            places[2]()
                        places[3]()
                        if i == 2 and n > 0:
                            turn_out(n - 1)
                        before = (g, c, i, k, kt)
                        k += 1
                return before

            def entries(g, stream, place):
                for x in place:
                    stream_entry(g, stream, x)

            def stream_entry(g, stream, x):
                ahead = [i for i, e in enumerate(stream.entries) if e[1] == 1]
                if ahead and x == ahead[0]:
                    pe.wait_ge(s_load, 16 * LOADS * (g + 2))
                pe.wait_ge(s_mred, entries_before(g) + x + 1)
                maxima.product(pe, g, stream.entries[x], ps_m[x % 2], s_msc)

            before = None
            for g in range(NG):
                before = group(g, body if g < NG - 1 else end, before)
            times_v(*before, lambda: None)
            turn_out(NG * NQ - 1)

        @block.scalar
        def _(act):
            def copy_o(g, c):
                n = g * NQ + c
                act.wait_ge(s_pv, 2 + pairs_before(g, c + 1))
                act.wait_ge(s_turn, n + 1)
                act.activation(o_raw[:, :], ps_o[:, :], ACT.Copy).then_inc(s_ocopy, 1)

            def group(g, first=False):
                k = 0
                for c in range(NQ):
                    for i in range(at.pairs[c]):
                        pair = pairs_before(g, 0) + k
                        act.wait_ge(s_pv, pair + (2 if k == 0 and at.pairs_group % 2 else 1))
                        for u in range(UNITS):
                            un = UNITS * pair + u
                            act.wait_ge(s_scores, un + 1)
                            bank = ps_s[k % 2 if UNITS == 1 else u]
                            act.activation(prob[:, k % 2, 2 * u:2 * u + 2, :], bank[:, :, :], ACT.Exp,
                                           scale=scale).then_inc(s_prob, 1)
                        if i == 0 and not (first and c == 0):
                            copy_o(g, c - 1)
                        k += 1

            act.wait_ge(s_prob, 2)
            act.wait_ge(s_ocopy, 1)
            act.wait_ge(s_turn, 1)
            group(0, first=True)
            with act.Fori(1, NG) as g:
                group(g)
            copy_o(NG, -1)

        @block.vector
        def _(dve):
            def normalise(g, c):
                gg, cc = (g - 1, NQ - 1) if c < 0 else (g, c)
                n = g * NQ + c
                heads = ps_x[:, :].rearrange("p (a j d) -> p a j d", a=QT, j=GH)
                dve.wait_ge(s_turn, n + 2)
                dve.reciprocal(inv_den[:, :, :, :], heads[:, :, :, SH:SH + 1]).then_inc(s_inv, 1)
                dve.wait_ge(s_inv, n + 1)
                dve.tensor_tensor(o_tok[:, cc * QT:(cc + 1) * QT, bass.ds(gg * GH * SH, GH * SH)]
                                  .rearrange("p a (j d) -> p a j d", d=SH), heads[:, :, :, 0:SH],
                                  inv_den[:, :, :, :].to_broadcast((P, QT, GH, SH)), ALU.mult).then_inc(s_norm, 1)

            def group(g, stream, first=False):
                k = 0
                for c in range(NQ):
                    for i in range(at.pairs[c]):
                        for place in stream.places[k]:
                            for x in place:
                                count = entries_before(g) + x + 1
                                dve.wait_ge(s_msc, count)
                                maxima.reduce(dve, g, stream.entries[x], ps_m[x % 2], s_mred, 2 + count)
                        if i == 2 and not (first and c == 0):
                            normalise(g, c - 1)
                        k += 1

            dve.wait_ge(s_mred, 2)
            dve.wait_ge(s_norm, 1)
            group(0, body, first=True)
            with dve.Fori(1, NG - 1) as g:
                group(g, body)
            group(NG - 1, end)
            normalise(NG, -1)


def load_closing(sp, wo_sb, bo_sb, gain, s_w, wo, bo, gamma, beta):
    sp.dma_start(wo_sb[:, :, :], wo.rearrange("(t p) n -> p t n", p=P)).then_inc(s_w, 16)
    sp.dma_start(bo_sb[:, :], bo.to_broadcast((P, D))).then_inc(s_w, 16)
    if gamma is not None:
        sp.dma_start(gain[:, 0, :], gamma.to_broadcast((P, D))).then_inc(s_w, 16)
        sp.dma_start(gain[:, 1, :], beta.to_broadcast((P, D))).then_inc(s_w, 16)


def close_attention(nc, name, x_tok, dst, x_fm, o_tok, closing, keep, cst):
    with ExitStack() as ctx:
        def sb(n, shape, dt):
            return ctx.enter_context(nc.sbuf_tensor(f"{name}_{n}", shape, dt))

        def pb(n, shape, dt):
            return ctx.enter_context(nc.psum_tensor(f"{name}_{n}", shape, dt))

        def sem(n):
            cst["semaphores"].append(nc.alloc_semaphore(f"{name}_{n}"))
            return cst["semaphores"][-1]

        wo_sb, bo_sb, gain, s_w = closing[:4]
        o_fm = sb("o_fm", [P, 2, DT, P], F32)
        ps_o = [pb(f"pso{i}", [P, QC], F32) for i in range(2)]
        ps_y = [pb(f"psy{i}", [P, QC], F32) for i in range(2)]
        s_turn, s_fm, s_mm, s_base, s_y = map(sem, ("turn", "fm", "mm", "base", "y"))
        norm = RowNorm(nc, name, sb, pb, sem, dst, x_fm, cst, gain)
        LAG = 7
        block = ctx.enter_context(nc.Block())
        loads = 16 * (2 if gain is None else 4)

        @block.gpsimd
        def _(pool):
            pool.wait_ge(s_w, loads)
            for t in range(NT):
                src = x_tok
                if keep == 2:
                    pool.tensor_tensor(dst[:, t, :], x_tok[:, t, :], x_tok[:, t, :], ALU.add).then_inc(s_base, 1)
                    pool.wait_ge(s_base, 2 * t + 1)
                    src = dst
                pool.tensor_tensor(dst[:, t, :], src[:, t, :], bo_sb[:, :], ALU.add).then_inc(s_base, 1)

        @block.tensor
        def _(pe):
            def turn(t):
                if t >= 2:
                    pe.wait_ge(s_fm, t - 1)
                for m in range(DT):
                    mm = pe.transpose(ps_o[t % 2][:, m * P:(m + 1) * P], o_tok[:, t, m * P:(m + 1) * P],
                                      cst["ident"][:, :])
                mm.then_inc(s_turn, 1)

            def product(t):
                pe.wait_ge(s_fm, t + 1)
                if t >= 2:
                    pe.wait_ge(s_y, t - 1)
                for m in range(DT):
                    mm = pe.matmul(ps_y[t % 2][:, 0:D], o_fm[:, t % 2, m, :], wo_sb[:, m, :],
                                   start=(m == 0), stop=(m == DT - 1))
                mm.then_inc(s_mm, 1)

            pe.wait_ge(s_w, loads)
            turn(0)
            for t in range(NT):
                if t + 1 < NT:
                    turn(t + 1)
                product(t)
                if t >= LAG:
                    norm.turn(pe, t - LAG)
            for t in range(NT - LAG, NT):
                norm.turn(pe, t)

        @block.scalar
        def _(act):
            def copy(t):
                act.wait_ge(s_turn, t + 1)
                if t >= 2:
                    act.wait_ge(s_mm, t - 1)
                act.activation(o_fm[:, t % 2, :, :], ps_o[t % 2][:, 0:D].rearrange("p (a b) -> p a b", a=DT),
                               ACT.Copy).then_inc(s_fm, 1)

            copy(0)
            for t in range(NT):
                if t + 1 < NT:
                    copy(t + 1)
                if t % 4 == 1 and t > 4:
                    norm.root(act, t // 4 - 1)
                if t >= LAG:
                    norm.copy_out(act, t - LAG)
            norm.root(act, NT // 4 - 1)
            for t in range(NT - LAG, NT):
                norm.copy_out(act, t)

        @block.vector
        def _(dve):
            for t in range(NT):
                dve.wait_ge(s_mm, t + 1)
                dve.wait_ge(s_base, (t + 1) * (2 if keep == 2 else 1))
                dve.tensor_tensor(dst[:, t, :], dst[:, t, :], ps_y[t % 2][:, 0:D], ALU.add).then_inc(s_y, 1)
                dve.wait_ge(s_y, t + 1)
                norm.statistics(dve, t)
                if t % 4 == 1 and t > 4:
                    norm.scale(dve, t // 4 - 1)
            norm.scale(dve, NT // 4 - 1)


def gelu_ffn(nc, name, x_tok, z_tok, x_fm, w1, b1, w2, b2, cst):
    with ExitStack() as ctx:
        def sb(n, shape, dt):
            return ctx.enter_context(nc.sbuf_tensor(f"{name}_{n}", shape, dt))

        def pb(n, shape, dt):
            return ctx.enter_context(nc.psum_tensor(f"{name}_{n}", shape, dt))

        def sem(n):
            cst["semaphores"].append(nc.alloc_semaphore(f"{name}_{n}"))
            return cst["semaphores"][-1]

        w1_sb = sb("w1", [P, DT, DFF], F32)
        w2_sb = sb("w2", [P, FT, D], F32)
        b1_sb = sb("b1", [P, FT], F32)
        b2_sb = sb("b2", [P, D], F32)
        h_fm = sb("h", [P, 2, FT, QC], F32)
        ps_h = [pb(f"psh{i}", [P, QC], F32) for i in range(4)]
        ps_y = [pb(f"psy{i}", [P, QC], F32) for i in range(2)]
        s_w, s_w2, s_up, s_h, s_dn, s_y, s_base = map(sem, ("w", "w2", "up", "h", "dn", "y", "base"))
        norm = RowNorm(nc, name, sb, pb, sem, x_tok, x_fm, cst)
        block = ctx.enter_context(nc.Block())

        @block.sync
        def _(sp):
            sp.dma_start(w1_sb[:, :, :], w1.rearrange("(t p) n -> p t n", p=P)).then_inc(s_w, 16)
            sp.dma_start(b1_sb[:, :], b1).then_inc(s_w, 16)
            sp.dma_start(b2_sb[:, :], b2.to_broadcast((P, D))).then_inc(s_w, 16)
            sp.dma_start(w2_sb[:, :, :], w2.rearrange("(t p) n -> p t n", p=P)).then_inc(s_w2, 16)

        @block.gpsimd
        def _(pool):
            pool.wait_ge(s_w, 48)
            for n in range(NT):
                pool.tensor_tensor(x_tok[:, n, :], x_tok[:, n, :], z_tok[:, n, :], ALU.add).then_inc(s_base, 1)
                pool.wait_ge(s_base, 2 * n + 1)
                pool.tensor_tensor(x_tok[:, n, :], x_tok[:, n, :], b2_sb[:, :], ALU.add).then_inc(s_base, 1)

        @block.tensor
        def _(pe):
            def up(c):
                for f in range(FT):
                    u = c * FT + f
                    if u >= 4:
                        pe.wait_ge(s_h, u - 3)
                    for t in range(DT):
                        mm = pe.matmul(ps_h[u % 4][:, :], w1_sb[:, t, f * P:(f + 1) * P],
                                       x_fm[:, t, c * QC:(c + 1) * QC], start=(t == 0), stop=(t == DT - 1))
                    mm.then_inc(s_up, 1)

            def down(c):
                pe.wait_ge(s_h, (c + 1) * FT)
                for a in range(QT):
                    n = c * QT + a
                    if n >= 2:
                        pe.wait_ge(s_y, n - 1)
                    for f in range(FT):
                        mm = pe.matmul(ps_y[n % 2][:, 0:D], h_fm[:, c % 2, f, a * P:(a + 1) * P],
                                       w2_sb[:, f, :], start=(f == 0), stop=(f == FT - 1))
                    mm.then_inc(s_dn, 1)

            pe.wait_ge(s_w, 48)
            up(0)
            pe.wait_ge(s_w2, 16)
            for c in range(NQ):
                if c + 1 < NQ:
                    up(c + 1)
                if c >= 2:
                    for t in range((c - 2) * QT, (c - 1) * QT):
                        norm.turn(pe, t)
                down(c)
            for t in range((NQ - 2) * QT, NT):
                norm.turn(pe, t)

        @block.scalar
        def _(act):
            act.wait_ge(s_w, 48)
            for c in range(NQ):
                if c >= 2:
                    act.wait_ge(s_dn, (c - 1) * QT)
                for f in range(FT):
                    u = c * FT + f
                    act.wait_ge(s_up, u + 1)
                    act.activation(h_fm[:, c % 2, f, :], ps_h[u % 4][:, :], ACT.Gelu,
                                   bias=b1_sb[:, f:f + 1]).then_inc(s_h, 1)
                if c >= 2:
                    norm.root(act, c - 2)
            for c in range(NQ):
                if c >= NQ - 2:
                    norm.root(act, c)
                for t in range(c * QT, (c + 1) * QT):
                    norm.copy_out(act, t)

        @block.vector
        def _(dve):
            for n in range(NT):
                dve.wait_ge(s_base, 2 * n + 2)
                dve.wait_ge(s_dn, n + 1)
                dve.tensor_tensor(x_tok[:, n, :], x_tok[:, n, :], ps_y[n % 2][:, 0:D], ALU.add).then_inc(s_y, 1)
                dve.wait_ge(s_y, n + 1)
                norm.statistics(dve, n)
                if n % 4 == 3 and n > 4:
                    norm.scale(dve, n // 4 - 1)
            norm.scale(dve, NT // 4 - 1)


def route(nc, name, x_fm, gate_w, gate_b, cols, gates, top, sums, spread, cst, load_more=lambda sp: None):
    lora = cols > E
    with ExitStack() as ctx:
        def sb(n, shape, dt):
            return ctx.enter_context(nc.sbuf_tensor(f"{name}_{n}", shape, dt))

        def sem(n):
            cst["semaphores"].append(nc.alloc_semaphore(f"{name}_{n}"))
            return cst["semaphores"][-1]

        w_sb = sb("w", [P, DT, cols], F32)
        b_sb = sb("b", [P, E], F32)
        logit = sb("logit", [P, NT, E], F32)
        best = sb("best", [P, NT, 8], F32)
        index = sb("index", [P, NT, 8], U32)
        index_f = sb("index_f", [P, NT, 2], F32)
        order = sb("order", [P, E], F32)
        delta = sb("delta", [P, NT, E + 1], F32)
        a_tok = sb("a", [P, NT, E * R], F32) if lora else None
        picked = sb("picked", [P, 2, NT, E * R], F32) if lora else None
        swap = sb("swap", [P, NT, E], F32)
        ps = [ctx.enter_context(nc.psum_tensor(f"{name}_ps{i}", [P, QC], F32)) for i in range(2)]
        ps_t = [ctx.enter_context(nc.psum_tensor(f"{name}_pst{i}", [P, QC], F32)) for i in range(2)]
        s_w, s_mm, s_logit, s_a, s_exp, s_turn, s_out = map(sem, ("w", "mm", "logit", "a", "exp", "turn", "out"))
        s_best, s_index, s_chain, s_delta, s_picked = map(sem, ("best", "index", "chain", "delta", "picked"))
        block = ctx.enter_context(nc.Block())

        @block.sync
        def _(sp):
            sp.dma_start(w_sb[:, :, :], gate_w.rearrange("(t p) n -> p t n", p=P)).then_inc(s_w, 16)
            sp.dma_start(b_sb[:, :], gate_b.to_broadcast((P, E))).then_inc(s_w, 16)
            load_more(sp)

        @block.tensor
        def _(pe):
            pe.wait_ge(s_w, 32)
            for t in range(NT):
                if t >= 2:
                    pe.wait_ge(s_logit, t - 1)
                for k in range(DT):
                    mm = pe.matmul(ps[t % 2][:, 0:cols], x_fm[:, k, t * P:(t + 1) * P], w_sb[:, k, :],
                                   start=(k == 0), stop=(k == DT - 1))
                mm.then_inc(s_mm, 1)
            if lora:
                for n in range(2 * NQ):
                    which, c = divmod(n, NQ)
                    pe.wait_ge(s_picked, which + 1)
                    if n >= 2:
                        pe.wait_ge(s_out, n - 1)
                    for a in range(QT):
                        mm = pe.transpose(ps_t[n % 2][:, a * P:(a + 1) * P], picked[:, which, c * QT + a, :],
                                          cst["ident"][:, :])
                    mm.then_inc(s_turn, 1)

        @block.vector
        def _(dve):
            links = 0

            def link(instruction):
                nonlocal links
                instruction.then_inc(s_chain, 1)
                links += 1
                dve.wait_ge(s_chain, links)

            for e in range(E):
                link(dve.memset(order[:, e:e + 1], float(e)))
            dve.wait_ge(s_w, 32)
            for t in range(NT):
                dve.wait_ge(s_mm, t + 1)
                if lora:
                    link(dve.tensor_copy(a_tok[:, t, :], ps[t % 2][:, 0:E * R]))
                dve.tensor_tensor(logit[:, t, :], ps[t % 2][:, cols - E:cols], b_sb[:, :],
                                  ALU.add).then_inc(s_logit, 1)
                dve.wait_ge(s_logit, t + 1)
                dve.max(best[:, t, :], logit[:, t, :]).then_inc(s_best, 1)
                dve.wait_ge(s_best, t + 1)
                dve.max_index(index[:, t, :], best[:, t, :], logit[:, t, :]).then_inc(s_index, 1)
            dve.tensor_tensor(delta[:, :, 0:E], logit[:, :, :], best[:, :, 0:1].to_broadcast((P, NT, E)),
                              ALU.subtract).then_inc(s_delta, 1)
            dve.tensor_tensor(delta[:, :, E:E + 1], best[:, :, 1:2], best[:, :, 0:1],
                              ALU.subtract).then_inc(s_delta, 1)
            dve.wait_ge(s_index, NT)
            link(dve.tensor_copy(index_f[:, :, :], index[:, :, 0:2]))
            for s in range(2):
                for t in range(NT):
                    ins = dve.tensor_scalar(gates[:, t, s, :], order[:, :], index_f[:, t, s:s + 1], None,
                                            ALU.is_equal)
                    if t == NT - 1:
                        link(ins)
            dve.wait_ge(s_exp, 1)
            link(dve.tensor_reduce(sums[:, :], delta[:, :, 0:E], AX.X, ALU.add))
            link(dve.tensor_copy(top[:, :], delta[:, :, E]))
            if lora:
                def wide(g):
                    return g.rearrange("p t (e o) -> p t e o", o=1).to_broadcast((P, NT, E, R))

                a4 = a_tok[:, :, :].rearrange("p t (e r) -> p t e r", r=R)
                link(dve.tensor_tensor(swap[:, :, :], gates[:, :, 1, :], gates[:, :, 0, :], ALU.subtract))
                for s, g in ((0, gates[:, :, 0, :]), (1, swap[:, :, :])):
                    dve.tensor_tensor(picked[:, s, :, :].rearrange("p t (e r) -> p t e r", r=R), a4, wide(g),
                                      ALU.mult).then_inc(s_picked, 1)

        @block.scalar
        def _(act):
            act.wait_ge(s_delta, 2)
            act.activation(delta[:, :, :], delta[:, :, :], ACT.Exp).then_inc(s_exp, 1)
            if lora:
                for n in range(2 * NQ):
                    which, c = divmod(n, NQ)
                    act.wait_ge(s_turn, n + 1)
                    act.activation(spread[:, which, c * QC:(c + 1) * QC], ps_t[n % 2][:, :],
                                   ACT.Copy).then_inc(s_out, 1)


def lora_ffn(nc, name, x_tok, x_fm, gates, top, sums, spread, wi, bi, wo, bo, lora_b, cst):
    with ExitStack() as ctx:
        def sb(n, shape, dt):
            return ctx.enter_context(nc.sbuf_tensor(f"{name}_{n}", shape, dt))

        def sem(n):
            cst["semaphores"].append(nc.alloc_semaphore(f"{name}_{n}"))
            return cst["semaphores"][-1]

        w1_sb = sb("w1", [P, DT, DFF], F32)
        lb_sb = sb("lb", [P, DFF], F32)
        w2_sb = sb("w2", [P, FT, D], F32)
        b1_sb = sb("b1", [P, FT], F32)
        b2_sb = sb("b2", [P, 2, D], F32)
        val = sb("val", [P, 2, NT], F32)
        h_fm = sb("h", [P, 2, FT, QC], F32)
        h_two = sb("h_two", [P, 2, 2, QC], F32)
        y_sb = sb("y", [P, 2, D], F32)
        ps_h = [ctx.enter_context(nc.psum_tensor(f"{name}_psh{i}", [P, QC], F32)) for i in range(4)]
        ps_y = [ctx.enter_context(nc.psum_tensor(f"{name}_psy{i}", [P, QC], F32)) for i in range(2)]
        s_w, s_w2, s_one, s_two, s_h1, s_h2, s_h, s_dn, s_a, s_b, s_v = map(
            sem, ("w", "w2", "one", "two", "h1", "h2", "h", "dn", "a", "b", "v"))
        norm = RowNorm(nc, name, sb, lambda n, shape, dt: ctx.enter_context(nc.psum_tensor(f"{name}_{n}", shape, dt)),
                       sem, x_tok, x_fm, cst)
        block = ctx.enter_context(nc.Block())
        UNITS = NQ * FT

        @block.sync
        def _(sp):
            sp.dma_start(w1_sb[:, :, :], wi.rearrange("(t p) n -> p t n", p=P)).then_inc(s_w, 16)
            sp.dma_start(lb_sb[:, :], lora_b).then_inc(s_w, 16)
            sp.dma_start(b1_sb[:, :], bi).then_inc(s_w, 16)
            sp.dma_start(w2_sb[:, :, :], wo.rearrange("(t p) n -> p t n", p=P)).then_inc(s_w2, 16)
            sp.dma_start(b2_sb[:, 0, :], bo.to_broadcast((P, D))).then_inc(s_w2, 16)

        @block.tensor
        def _(pe):
            def first(u):
                c, f = divmod(u, FT)
                if u >= 4:
                    pe.wait_ge(s_h2, u - 3)
                for t in range(DT):
                    pe.matmul(ps_h[u % 4][:, :], w1_sb[:, t, f * P:(f + 1) * P], x_fm[:, t, c * QC:(c + 1) * QC],
                              start=(t == 0), stop=False)
                pe.matmul(ps_h[u % 4][:, :], lb_sb[:, f * P:(f + 1) * P], spread[:, 0, c * QC:(c + 1) * QC],
                          start=False, stop=True).then_inc(s_one, 1)

            def second(u):
                c, f = divmod(u, FT)
                pe.wait_ge(s_h1, u + 1)
                pe.matmul(ps_h[u % 4][:, :], lb_sb[:, f * P:(f + 1) * P], spread[:, 1, c * QC:(c + 1) * QC],
                          start=False, stop=True, skip_group_check=True).then_inc(s_two, 1)

            def down(n):
                c, a = divmod(n, QT)
                pe.wait_ge(s_h, (c + 1) * FT)
                if n >= 2:
                    pe.wait_ge(s_a, n - 1)
                for f in range(FT):
                    mm = pe.matmul(ps_y[n % 2][:, 0:D], h_fm[:, c % 2, f, a * P:(a + 1) * P],
                                   w2_sb[:, f, :], start=(f == 0), stop=(f == FT - 1))
                mm.then_inc(s_dn, 1)

            pe.wait_ge(s_w, 48)
            for u in range(UNITS):
                first(u)
                if u >= 1:
                    second(u - 1)
                if u == 4:
                    pe.wait_ge(s_w2, 32)
                c, f = divmod(u, FT)
                if c >= 1 and f >= FT - QT:
                    down((c - 1) * QT + f - (FT - QT))
                if c >= 2 and f >= FT - QT:
                    norm.turn(pe, (c - 2) * QT + f - (FT - QT))
            second(UNITS - 1)
            for a in range(QT):
                norm.turn(pe, (NQ - 2) * QT + a)
                down((NQ - 1) * QT + a)
            for a in range(QT):
                norm.turn(pe, (NQ - 1) * QT + a)

        @block.scalar
        def _(act):
            act.wait_ge(s_w, 48)
            for u in range(UNITS):
                c, f = divmod(u, FT)
                if u >= 2:
                    act.wait_ge(s_h, u - 1)
                act.wait_ge(s_one, u + 1)
                act.activation(h_two[:, u % 2, 0, :], ps_h[u % 4][:, :], ACT.Relu,
                               bias=b1_sb[:, f:f + 1]).then_inc(s_h1, 1)
                act.wait_ge(s_two, u + 1)
                act.activation(h_two[:, u % 2, 1, :], ps_h[u % 4][:, :], ACT.Relu,
                               bias=b1_sb[:, f:f + 1]).then_inc(s_h2, 1)
                if c >= 2 and f == 1:
                    norm.root(act, c - 2)
                if c >= 2 and f >= FT - QT:
                    norm.copy_out(act, (c - 2) * QT + f - (FT - QT))
            for c in (NQ - 2, NQ - 1):
                norm.root(act, c)
                for a in range(QT):
                    norm.copy_out(act, c * QT + a)

        @block.vector
        def _(dve):
            dve.reciprocal(val[:, 0, :], sums[:, :]).then_inc(s_v, 1)
            dve.wait_ge(s_v, 1)
            dve.scalar_tensor_tensor(out=val[:, 1, :], in0=top[:, :], scalar=1.0, in1=val[:, 0, :], op0=ALU.add,
                                     op1=ALU.mult).then_inc(s_v, 1)
            dve.wait_ge(s_w2, 32)
            dve.tensor_scalar(b2_sb[:, 1, :], b2_sb[:, 0, :], 2.0, None, ALU.mult).then_inc(s_v, 1)
            dve.wait_ge(s_v, 3)

            def out(n):
                dve.wait_ge(s_dn, n + 1)
                if n >= 2:
                    dve.wait_ge(s_b, n - 1)
                dve.tensor_tensor(y_sb[:, n % 2, :], ps_y[n % 2][:, 0:D], b2_sb[:, 1, :], ALU.add).then_inc(s_a, 1)
                dve.wait_ge(s_a, n + 1)
                dve.scalar_tensor_tensor(out=x_tok[:, n, :], in0=y_sb[:, n % 2, :], scalar=val[:, 1, n:n + 1],
                                         in1=x_tok[:, n, :], op0=ALU.mult, op1=ALU.add).then_inc(s_b, 1)
                dve.wait_ge(s_b, n + 1)
                norm.statistics(dve, n)

            for u in range(UNITS):
                c, f = divmod(u, FT)
                dve.wait_ge(s_h2, u + 1)
                if f == 0 and c >= 2:
                    dve.wait_ge(s_dn, (c - 1) * QT)
                dve.tensor_tensor(h_fm[:, c % 2, f, :], h_two[:, u % 2, 0, :], h_two[:, u % 2, 1, :],
                                  ALU.add).then_inc(s_h, 1)
                if c >= 1 and f >= FT - QT:
                    out((c - 1) * QT + f - (FT - QT))
                if c >= 2 and f == 2:
                    norm.scale(dve, c - 2)
            norm.scale(dve, NQ - 2)
            for a in range(QT):
                out((NQ - 1) * QT + a)
            norm.scale(dve, NQ - 1)


def place_tokens(nc, name, x_tok, gates, slots, tile_expert, x_slots, s_zero, s_scatter, cst):
    C = 2 * NT
    with ExitStack() as ctx:
        def sb(n, shape, dt):
            return ctx.enter_context(nc.sbuf_tensor(f"{name}_{n}", shape, dt))

        def sem(n):
            cst["semaphores"].append(nc.alloc_semaphore(f"{name}_{n}"))
            return cst["semaphores"][-1]

        before = sb("before", [P, P], F32)
        ones = sb("ones", [P, P], F32)
        ladder = sb("ladder", [P, 64], F32)
        total = sb("total", [P, C, E], F32)
        upto = sb("upto", [P, 2, C, E], F32)
        rank = sb("rank", [P, C, E], F32)
        over = sb("over", [P, E, NT], F32)
        tiles = sb("tiles", [P, E], F32)
        end = sb("end", [P, E], F32)
        base = sb("base", [P, E], F32)
        slot_f = sb("slot_f", [P, C], F32)
        past = sb("past", [1, EXPERT_TILES, E], F32)
        expert_f = sb("expert_f", [1, EXPERT_TILES], F32)
        ps_before = ctx.enter_context(nc.psum_tensor(f"{name}_ps_before", [P, QC], F32))
        ps_total = ctx.enter_context(nc.psum_tensor(f"{name}_ps_total", [P, QC], F32))
        s_const, s_count, s_chain, s_slots = map(sem, ("const", "count", "chain", "slots"))
        choice = gates[:, :, :, :].rearrange("p t s e -> p (t s) e")
        block = ctx.enter_context(nc.Block())

        @block.tensor
        def _(pe):
            pe.wait_ge(s_const, 3)
            flat = gates[:, :, :, :].rearrange("p t s e -> p (t s e)")
            pe.matmul(ps_total[:, 0:C * E], ones[:, :], flat, start=True, stop=True).then_inc(s_count, 1)
            pe.matmul(ps_before[:, 0:C * E], before[:, :], flat, start=True, stop=True).then_inc(s_count, 1)

        @block.vector
        def _(dve):
            links = 0

            def link(instruction):
                nonlocal links
                instruction.then_inc(s_chain, 1)
                links += 1
                dve.wait_ge(s_chain, links)

            link(dve.memset(ladder[:, 0:1], 0.0))
            for n in (1, 2, 4, 8, 16, 32):
                link(dve.tensor_scalar(ladder[:, n:2 * n], ladder[:, 0:n], float(n), None, ALU.add))
            dve.wait_ge(s_count, 1)
            link(dve.tensor_copy(total[:, :, :], ps_total[:, 0:C * E].rearrange("p (c e) -> p c e", e=E)))
            src, side, n = total[:, :, :], 0, 1
            while n < C:
                dst = upto[:, side, :, :]
                link(dve.tensor_copy(dst[:, 0:n, :], src[:, 0:n, :]))
                link(dve.tensor_tensor(dst[:, n:C, :], src[:, n:C, :], src[:, 0:C - n, :], ALU.add))
                src, side, n = dst, 1 - side, 2 * n
            count = src[:, C - 1, :].rearrange("p (e o) -> p e o", o=1)
            link(dve.tensor_scalar(base[:, :].rearrange("p (e o) -> p e o", o=1), count, 1.0 / P, None, ALU.mult))
            link(dve.tensor_tensor(over[:, :, :],
                                   base[:, :].rearrange("p (e o) -> p e o", o=1).to_broadcast((P, E, NT)),
                                   ladder[:, 0:NT].rearrange("p (o n) -> p o n", o=1).to_broadcast((P, E, NT)),
                                   ALU.is_gt))
            link(dve.tensor_reduce(tiles[:, :], over[:, :, :], AX.X, ALU.add))
            link(dve.tensor_copy(end[:, 0:1], tiles[:, 0:1]))
            for e in range(1, E):
                link(dve.tensor_tensor(end[:, e:e + 1], end[:, e - 1:e], tiles[:, e:e + 1], ALU.add))
            link(dve.tensor_tensor(base[:, :], end[:, :], tiles[:, :], ALU.subtract))
            link(dve.tensor_scalar(base[:, :], base[:, :], float(P), None, ALU.mult))
            link(dve.tensor_tensor(rank[:, :, :], src, total[:, :, :], ALU.subtract))
            link(dve.tensor_tensor(rank[:, :, :], rank[:, :, :],
                                   base[:, :].rearrange("p (o e) -> p o e", o=1).to_broadcast((P, C, E)), ALU.add))
            dve.wait_ge(s_count, 2)
            link(dve.tensor_tensor(rank[:, :, :], rank[:, :, :],
                                   ps_before[:, 0:C * E].rearrange("p (c e) -> p c e", e=E), ALU.add))
            link(dve.tensor_tensor(rank[:, :, :], rank[:, :, :], choice, ALU.mult))
            link(dve.tensor_reduce(slot_f[:, :], rank[:, :, :], AX.X, ALU.add))
            dve.tensor_copy(slots[:, :], slot_f[:, :]).then_inc(s_slots, 1)
            link(dve.tensor_tensor(
                past[:, :, :],
                ladder[0:1, 0:EXPERT_TILES].rearrange("p (n o) -> p n o", o=1).to_broadcast((1, EXPERT_TILES, E)),
                end[0:1, :].rearrange("p (o e) -> p o e", o=1).to_broadcast((1, EXPERT_TILES, E)), ALU.is_ge))
            link(dve.tensor_reduce(expert_f[:, :], past[:, :, :], AX.X, ALU.add))
            link(dve.tensor_scalar(expert_f[:, :], expert_f[:, :], float(E - 1), None, ALU.min))
            link(dve.tensor_copy(tile_expert[:, :], expert_f[:, :]))

        @block.gpsimd
        def _(pool):
            pool.memset(ones[:, :], 1.0).then_inc(s_const, 1)
            pool.wait_ge(s_const, 1)
            pool.memset(before[:, :], 1.0).then_inc(s_const, 1)
            pool.wait_ge(s_const, 2)
            pool.affine_select(out=before[:, :], in_=before[:, :], compare_op=ALU.is_ge, fill=0.0, base=-1,
                               pattern=[[1, P]], channel_multiplier=-1).then_inc(s_const, 1)
            pool.wait_ge(s_const, 3)
            pool.wait_ge(s_slots, 1)
            pool.wait_ge(s_zero, 16)
            for c in range(C):
                pool.indirect_dma_start(x_slots, bass.IndirectOffsetOnAxis(slots[:, c:c + 1], 0),
                                        x_tok[:, c // 2, :], None).then_inc(s_scatter, 16)


def load_experts(sp, w1, b1, w2, b2, w1_sb, b1_sb, w2_sb, b2_sb, s_weights):
    for e in range(E):
        sp.dma_start(w1_sb[:, e, :, :], w1[e].rearrange("(t p) n -> p t n", p=P)).then_inc(s_weights, 16)
        sp.dma_start(w2_sb[:, e, :, :], w2[e].rearrange("(t p) n -> p t n", p=P)).then_inc(s_weights, 16)
    sp.dma_start(b1_sb[:, :, :], b1).then_inc(s_weights, 16)
    sp.dma_start(b2_sb[:, :, :], b2.rearrange("(o e) n -> o e n", o=1).to_broadcast((P, E, D)))\
        .then_inc(s_weights, 16)


EXPERT_LOADS = 2 * E + 2


def expert_ffn(nc, name, x_tok, top, slots, tile_expert, x_slots, y_slots, weights, s_weights, s_scatter, out, cst):
    w1_sb, b1_sb, w2_sb, b2_sb = weights
    HALF = DFF // QC
    FH = FT // HALF
    DEPTH = 4
    with ExitStack() as ctx:
        def sb(n, shape, dt):
            return ctx.enter_context(nc.sbuf_tensor(f"{name}_{n}", shape, dt))

        def sem(n):
            cst["semaphores"].append(nc.alloc_semaphore(f"{name}_{n}"))
            return cst["semaphores"][-1]

        x_rows = sb("x_rows", [P, D], F32)
        x_cols = sb("x_cols", [P, DT, P], F32)
        h_rows = sb("h_rows", [P, HALF, QC], F32)
        h_cols = sb("h_cols", [P, FT, P], F32)
        y_rows = sb("y_rows", [P, D], F32)
        part = sb("part", [P, 2, NT], F32)
        y_two = sb("y_two", [P, DEPTH, 2, D], F32)
        ps_x = ctx.enter_context(nc.psum_tensor(f"{name}_ps_x", [P, QC], F32))
        ps_h = [ctx.enter_context(nc.psum_tensor(f"{name}_ps_h{i}", [P, QC], F32)) for i in range(HALF)]
        ps_t = [ctx.enter_context(nc.psum_tensor(f"{name}_ps_t{i}", [P, QC], F32)) for i in range(HALF)]
        ps_y = ctx.enter_context(nc.psum_tensor(f"{name}_ps_y", [P, QC], F32))
        s_row = sem("row")
        s_xturn = sem("xturn")
        s_xcol = sem("xcol")
        s_up = sem("up")
        s_hrow = sem("hrow")
        s_hturn = sem("hturn")
        s_hcol = sem("hcol")
        s_down = sem("down")
        s_y = sem("y")
        s_stored = sem("stored")
        s_part, s_first, s_sum, s_out = map(sem, ("part", "first", "sum", "out"))
        s_two = [sem(f"two{i}") for i in range(DEPTH)]
        norm = RowNorm(nc, name, sb, None, sem, x_tok, None, cst)
        block = ctx.enter_context(nc.Block())
        N = EXPERT_TILES

        def rows(dram, i):
            return dram[bass.ds(i * P, P), :]

        def expert_of(engine, i):
            return engine.value_load(tile_expert[0:1, bass.ds(i, 1)], min_val=0, max_val=E - 1)

        @block.sync
        def _(sp):
            def load(i):
                sp.dma_start(x_rows[:, :], rows(x_slots, i)).then_inc(s_row, 16)

            def store(i):
                sp.wait_ge(s_y, i + 2)
                sp.dma_start(rows(y_slots, i), y_rows[:, :]).then_inc(s_stored, 16)

            sp.wait_ge(s_scatter, 16 * 2 * NT)
            load(0)
            sp.wait_ge(s_xturn, 1)
            load(1)
            with sp.Fori(0, N - 2) as i:
                sp.wait_ge(s_xturn, i + 2)
                load(i + 2)
                store(i)
            store(N - 2)
            store(N - 1)
            for t in range(NT):
                sp.wait_ge(norm.s_x, t + 1)
                sp.dma_start(out[t * P:(t + 1) * P, :], x_tok[:, t, :]).then_inc(s_out, 16)
            sp.wait_ge(s_out, 16 * NT)

        @block.tensor
        def _(pe):
            def turn_x(i, first=False):
                pe.wait_ge(s_row, 16 * (i + 1))
                if not first:
                    pe.wait_ge(s_xcol, i)
                for m in range(DT):
                    mm = pe.transpose(ps_x[:, m * P:(m + 1) * P], x_rows[:, m * P:(m + 1) * P], cst["ident"][:, :])
                mm.then_inc(s_xturn, 1)

            def up(i, first=False):
                e = expert_of(pe, i)
                pe.wait_ge(s_xcol, i + 1)
                if not first:
                    pe.wait_ge(s_hrow, HALF * i)
                for hh in range(HALF):
                    for m in range(DT):
                        mm = pe.matmul(ps_h[hh][:, :], x_cols[:, m, :],
                                       w1_sb[:, bass.ds(e, 1), m, hh * QC:(hh + 1) * QC],
                                       start=(m == 0), stop=(m == DT - 1))
                    mm.then_inc(s_up, 1)

            def turn_h(i, first=False):
                for hh in range(HALF):
                    pe.wait_ge(s_hrow, HALF * i + hh + 1)
                    if not first:
                        pe.wait_ge(s_hcol, FT * i + FH * hh - FH)
                    for f in range(FH):
                        mm = pe.transpose(ps_t[hh][:, f * P:(f + 1) * P], h_rows[:, hh, f * P:(f + 1) * P],
                                          cst["ident"][:, :])
                    mm.then_inc(s_hturn, 1)

            def down(i, e):
                pe.wait_ge(s_y, i + 1)
                pe.wait_ge(s_hcol, FT * (i + 1))
                for f in range(FT):
                    mm = pe.matmul(ps_y[:, 0:D], h_cols[:, f, :], w2_sb[:, bass.ds(e, 1), f, :],
                                   start=(f == 0), stop=(f == FT - 1))
                mm.then_inc(s_down, 1)

            turn_x(0, first=True)
            pe.wait_ge(s_weights, 16 * EXPERT_LOADS)
            up(0, first=True)
            turn_x(1)
            turn_h(0, first=True)
            with pe.Fori(0, N - 2) as i:
                up(i + 1)
                e = expert_of(pe, i)
                turn_x(i + 2)
                down(i, e)
                turn_h(i + 1)
            up(N - 1)
            down(N - 2, expert_of(pe, N - 2))
            turn_h(N - 1)
            down(N - 1, expert_of(pe, N - 1))

        @block.scalar
        def _(act):
            def copy_x(i, first=False):
                act.wait_ge(s_xturn, i + 1)
                if not first:
                    act.wait_ge(s_up, HALF * i)
                act.activation(x_cols[:, :, :], ps_x[:, 0:D].rearrange("p (a b) -> p a b", a=DT),
                               ACT.Copy).then_inc(s_xcol, 1)

            def relu(i, first=False):
                e = expert_of(act, i)
                if not first:
                    act.wait_ge(s_down, i)
                for f in range(FT):
                    act.wait_ge(s_hturn, HALF * i + f // FH + 1)
                    act.activation(h_cols[:, f, :], ps_t[f // FH][:, f % FH * P:(f % FH + 1) * P], ACT.Relu,
                                   bias=b1_sb[:, bass.ds(e, 1), f]).then_inc(s_hcol, 1)

            copy_x(0, first=True)
            act.wait_ge(s_weights, 16 * EXPERT_LOADS)
            copy_x(1)
            relu(0, first=True)
            with act.Fori(0, N - 2) as i:
                copy_x(i + 2)
                relu(i + 1)
            relu(N - 1)
            for quad in range(NT // 4):
                norm.root(act, quad)

        @block.gpsimd
        def _(pool):
            pool.sem_inc(s_y, 1)
            pool.sem_inc(s_stored, 16)
            pool.wait_ge(s_stored, 16 * (N + 1))
            for t in range(NT):
                if t >= DEPTH:
                    pool.wait_ge(s_sum, t - DEPTH + 1)
                for s in range(2):
                    pool.indirect_dma_start(y_two[:, t % DEPTH, s, :], None, y_slots,
                                            bass.IndirectOffsetOnAxis(slots[:, 2 * t + s:2 * t + s + 1], 0))\
                        .then_inc(s_two[t % DEPTH], 16)

        @block.vector
        def _(dve):
            dve.tensor_scalar(part[:, 1, :], top[:, :], 1.0, None, ALU.add).then_inc(s_part, 1)
            dve.wait_ge(s_part, 1)
            dve.reciprocal(part[:, 0, :], part[:, 1, :]).then_inc(s_part, 1)
            dve.wait_ge(s_part, 2)
            dve.tensor_tensor(part[:, 1, :], part[:, 0, :], top[:, :], ALU.mult).then_inc(s_part, 1)
            dve.wait_ge(s_weights, 16 * EXPERT_LOADS)

            def copy_h(i, first=False):
                for hh in range(HALF):
                    dve.wait_ge(s_up, HALF * i + hh + 1)
                    if not first:
                        dve.wait_ge(s_hturn, HALF * i + hh - 1)
                    dve.tensor_copy(h_rows[:, hh, :], ps_h[hh][:, :]).then_inc(s_hrow, 1)

            def add_bias(i):
                e = expert_of(dve, i)
                dve.wait_ge(s_down, i + 1)
                dve.wait_ge(s_stored, 16 * (i + 1))
                dve.tensor_tensor(y_rows[:, :], ps_y[:, 0:D], b2_sb[:, bass.ds(e, 1), :]
                                  .rearrange("p o n -> p (o n)"), ALU.add).then_inc(s_y, 1)

            copy_h(0, first=True)
            with dve.Fori(0, N - 1) as i:
                copy_h(i + 1)
                add_bias(i)
            add_bias(N - 1)
            dve.wait_ge(s_part, 3)
            for t in range(NT):
                dve.wait_ge(s_two[t % DEPTH], 32 * (t // DEPTH + 1))
                dve.scalar_tensor_tensor(out=x_tok[:, t, :], in0=y_two[:, t % DEPTH, 0, :],
                                         scalar=part[:, 0, t:t + 1], in1=x_tok[:, t, :], op0=ALU.mult,
                                         op1=ALU.add).then_inc(s_first, 1)
                dve.wait_ge(s_first, t + 1)
                dve.scalar_tensor_tensor(out=x_tok[:, t, :], in0=y_two[:, t % DEPTH, 1, :],
                                         scalar=part[:, 1, t:t + 1], in1=x_tok[:, t, :], op0=ALU.mult,
                                         op1=ALU.add).then_inc(s_sum, 1)
                dve.wait_ge(s_sum, t + 1)
                norm.statistics(dve, t)
                if t % 4 == 1 and t > 4:
                    norm.scale(dve, t // 4 - 1)
            norm.scale(dve, NT // 4 - 1)


def decoder_kernel(nc, t, out):
    nc.disable_value_cache = True
    with ExitStack() as ctx:
        def sb(name, shape, dt, c=ctx):
            return c.enter_context(nc.sbuf_tensor(name, shape, dt))

        parts_q = nc.dram_tensor("parts_q", (3, D, S), BF16).ap()
        parts_k = nc.dram_tensor("parts_k", (3, D, S), BF16).ap()
        masks = nc.dram_tensor("key_masks", (3, S), BF16).ap()
        x_slots = nc.dram_tensor("x_slots", (EXPERT_TILES * P, D), F32).ap()
        y_slots = nc.dram_tensor("y_slots", (EXPERT_TILES * P, D), F32).ap()
        s_zero = nc.alloc_semaphore("slots_cleared")
        x_tok = sb("x_tok", [P, NT, D], F32)
        x_fm = sb("x_fm", [P, DT, S], F32)
        cst = constants(sb)
        shared = ctx.enter_context(ExitStack())
        q_st = sb("q_st", [P, 2, GH, S], BF16, shared)
        k_st = sb("k_st", [P, 2, GH, S], BF16, shared)
        v_grp = sb("v_grp", [P, NT, GH, 2 * SH], F32, shared)
        prepare(nc, t, cst, x_tok, x_fm, masks, q_st, k_st, v_grp)

        def attention(at, name, kv_source, mask, keep, dst, gamma=None, beta=None, behind=lambda sp: None):
            with ExitStack() as c:
                s_load, s_closing = (nc.alloc_semaphore(f"{name}_{n}") for n in ("load_stacks", "load_closing"))
                cst["semaphores"] += [s_load, s_closing]
                o_tok = sb(f"{name}_o_tok", [P, NT, D], F32, c)
                v_tok = sb(f"{name}_v", [P, at.tiles, D], F32, c)
                maxima = Maxima(nc, at, name, lambda n, shape, dt: sb(n, shape, dt, c), (q_st, k_st), cst)
                with ExitStack() as cc:
                    kv = x_fm if kv_source is None else sb(f"{name}_ctx", [P, DT, at.keys], F32, cc)
                    project(nc, at, f"{name}_proj", x_fm, kv, kv_source, t[f"{name}_w"], t[f"{name}_bqk"],
                            t[f"{name}_bv"], v_tok, parts_q, parts_k, (q_st, k_st), maxima, s_load,
                            masks[mask:mask + 1, :], cst)
                wo_sb = sb(f"{name}_wo_sb", [P, DT, D], F32, c)
                bo_sb = sb(f"{name}_bo_sb", [P, D], F32, c)
                gain = sb(f"{name}_gain", [P, 2, D], F32, c) if gamma is not None else None
                closing = (wo_sb, bo_sb, gain, s_closing, t[f"{name}_wo"], t[f"{name}_bo"], gamma, beta)
                attend(nc, at, f"{name}_att", v_tok, parts_q, parts_k, o_tok, (q_st, k_st, v_grp), maxima,
                       s_load, closing, cst, behind)
                close_attention(nc, f"{name}_close", x_tok, dst, x_fm, o_tok, closing, keep, cst)

        def clear_slots(sp):
            sp.dma_start(x_slots.rearrange("(t p) n -> p t n", p=P),
                         cst["zeros"][:, :].rearrange("p (o n) -> p o n", o=1).to_broadcast((P, EXPERT_TILES, D)))\
                .then_inc(s_zero, 16)

        clear_semaphores(nc, cst["semaphores"])
        with ExitStack() as c:
            z_tok = sb("z_tok", [P, NT, D], F32, c)
            attention(Attention("band", S, 32), "a0", None, 0, 1, z_tok, t["gamma"], t["beta"],
                      clear_slots)
            gelu_ffn(nc, "f0", x_tok, z_tok, x_fm, t["f0_w1"], t["f0_b1"], t["f0_w2"], t["f0_b2"], cst)
        clear_semaphores(nc, cst["semaphores"])
        attention(Attention("causal", CTXP, 16), "x0", t["ctx_fm"], 1, 1, x_tok)
        clear_semaphores(nc, cst["semaphores"])
        with ExitStack() as c:
            gates = sb("l0_gates", [P, NT, 2, E], F32, c)
            top = sb("l0_top", [P, NT], F32, c)
            sums = sb("l0_sums", [P, NT], F32, c)
            spread = sb("l0_spread", [P, 2, S], F32, c)
            route(nc, "l0r", x_fm, t["l0_gate_w"], t["l0_gate_b"], E * R + E, gates, top, sums, spread, cst)
            lora_ffn(nc, "l0f", x_tok, x_fm, gates, top, sums, spread, t["l0_wi"], t["l0_bi"], t["l0_wo"],
                     t["l0_bo"], t["l0_lora_b"], cst)
        clear_semaphores(nc, cst["semaphores"])
        attention(Attention("full", S, 16), "a1", None, 0, 2, x_tok)
        clear_semaphores(nc, cst["semaphores"])
        attention(Attention("full", CTXP, 16), "x1", t["ctx_fm"], 2, 1, x_tok)
        shared.close()
        clear_semaphores(nc, cst["semaphores"])
        with ExitStack() as c:
            weights = (sb("l1_w1", [P, E, DT, DFF], F32, c), sb("l1_b1", [P, E, FT], F32, c),
                       sb("l1_w2", [P, E, FT, D], F32, c), sb("l1_b2", [P, E, D], F32, c))

            def load_weights(sp):
                load_experts(sp, t["l1_w1"], t["l1_b1"], t["l1_w2"], t["l1_b2"], *weights, s_weights)

            gates = sb("l1_gates", [P, NT, 2, E], F32, c)
            top = sb("l1_top", [P, NT], F32, c)
            sums = sb("l1_sums", [P, NT], F32, c)
            slots = sb("l1_slots", [P, 2 * NT], U32, c)
            tile_expert = sb("l1_tile_expert", [1, EXPERT_TILES], I32, c)
            s_weights, s_scatter = (nc.alloc_semaphore(n) for n in ("l1_weights", "l1_scatter"))
            route(nc, "l1r", x_fm, t["l1_gate_w"], t["l1_gate_b"], E, gates, top, sums, None, cst,
                  load_weights)
            place_tokens(nc, "l1p", x_tok, gates, slots, tile_expert, x_slots, s_zero, s_scatter, cst)
            expert_ffn(nc, "l1f", x_tok, top, slots, tile_expert, x_slots, y_slots, weights, s_weights,
                       s_scatter, out, cst)


def _layout(inputs):
    import numpy as np
    a = {k: np.asarray(v) for k, v in inputs.items()}
    x, ctx = a["x"][0], a["ctx_1024"][0]
    o = {"x": x, "x_fm": x.T, "ctx_fm": ctx.T, "mask": a["mask_Bx1xS2_bf1"].reshape(1, CTX).view(np.uint8)}

    def columns(b):
        return b.reshape(-1, P).T

    def row(b):
        return b.reshape(1, -1)

    def block(name, q, k, v, out, bq, bk, bv, bo):
        o[f"{name}_w"] = np.stack([q, k, v])
        o[f"{name}_bqk"] = np.stack([columns(bq), columns(bk)])
        o[f"{name}_bv"], o[f"{name}_wo"], o[f"{name}_bo"] = row(bv), out, row(bo)

    p = "L0_attn_"
    block("a0", *(a[p + n] for n in ("Wq", "Wk", "Wv", "Wo", "bq", "bk", "bv", "bo")))
    o["gamma"], o["beta"] = row(a[p + "gamma"]), row(a[p + "beta"])
    o["f0_w1"], o["f0_b1"], o["f0_w2"], o["f0_b2"] = a[p + "W1"], columns(a[p + "b1"]), a[p + "W2"], row(a[p + "b2"])
    p = "L0_xattn_"
    block("x0", *(a[p + n].T for n in ("Wq", "Wk", "Wv", "Wo")), *(a[p + n] for n in ("bq", "bk", "bv", "bo")))
    p = "L0_ffn_"
    o["l0_wi"], o["l0_bi"], o["l0_wo"], o["l0_bo"] = a[p + "wi"].T, columns(a[p + "bi"]), a[p + "wo"].T, row(a[p + "bo"])
    o["l0_gate_w"] = np.concatenate([a[p + "lora_A"].reshape(E * R, D).T, a[p + "gate_w"].T], axis=1)
    o["l0_gate_b"] = row(a[p + "gate_b"])
    o["l0_lora_b"] = a[p + "lora_B"].transpose(0, 2, 1).reshape(E * R, DFF)
    p = "L1_attn_"
    w = a[p + "qkv_w"].reshape(NSH, 3, SH, D).transpose(1, 3, 0, 2).reshape(3, D, D)
    b = a[p + "qkv_b"].reshape(NSH, 3, SH).transpose(1, 0, 2).reshape(3, D)
    block("a1", w[0], w[1], w[2], a[p + "fc_w"].T, b[0], b[1], b[2], a[p + "fc_b"])
    p = "L1_xattn_"
    block("x1", *(a[p + n] for n in ("Wq", "Wk", "Wv", "Wo", "bq", "bk", "bv", "bo")))
    p = "L1_ffn_"
    o["l1_gate_w"], o["l1_gate_b"], o["l1_w1"], o["l1_w2"] = a[p + "gate_w"], row(a[p + "gate_b"]), a[p + "w1"], a[p + "w2"]
    o["l1_b1"], o["l1_b2"] = a[p + "b1"].reshape(E, FT, P).transpose(2, 0, 1), a[p + "b2"]
    return o


def kernel(**inputs):
    import numpy as np
    import concourse.bacc as bacc
    from concourse.bass_utils import run_bass_kernel_spmd

    nc = bacc.Bacc("TRN2", target_bir_lowering=False, num_devices=1)
    arrays, t = {}, {}
    for name, a in _layout(inputs).items():
        a = np.ascontiguousarray(a)
        arrays[f"in_{name}"] = a
        t[name] = nc.dram_tensor(f"in_{name}", a.shape, mybir.dt.from_np(a.dtype), kind="ExternalInput").ap()
    out = nc.dram_tensor("out", (S, D), F32, kind="ExternalOutput").ap()
    decoder_kernel(nc, t, out)
    r = run_bass_kernel_spmd(nc, [arrays], core_ids=[0])
    return r.results[0]["out"].reshape(1, S, D)
```
